# Optimizing a Trainium2 kernel written in Bass

```python
import numpy as np
import jax
import jax.numpy as jnp

def _softmax(x, axis=-1):
    return jax.nn.softmax(x, axis=axis)

def _gelu(x):
    return jax.nn.gelu(x, approximate=True)

def _silu(x):
    return jax.nn.silu(x)

def _sigmoid(x):
    return jax.nn.sigmoid(x)

def _layernorm(x, axis=-1, eps=1e-05):
    m = jnp.mean(x, axis=axis, keepdims=True)
    v = jnp.var(x, axis=axis, keepdims=True)
    return (x - m) / jnp.sqrt(v + eps)

def _scatter_add(tgt, idx, src, axis=0):
    return tgt.at[idx].add(src)

def _segment_sum(src, seg, n):
    return jax.ops.segment_sum(src, seg, n)
kernel_name = 'mk_flamingo_gated_d1_seqx_r4_d6f9ee'

def setup_inputs(seed: int=0):
    np.random.seed(seed)
    _w = jnp.asarray

    def _rec_inputs():
        import jax
        import jax.numpy as jnp
        _rk = jax.random.key(seed)
        x = 7.22e-05 + 1 * jax.random.normal(jax.random.fold_in(_rk, 1), (16, 100, 512), jnp.float32)
        _lenS = 100 - jax.random.randint(jax.random.fold_in(_rk, 7), (16,), 0, max(1, 100 // 4) + 1, jnp.int32)
        _lenS2 = 361 - jax.random.randint(jax.random.fold_in(_rk, 8), (16,), 0, max(1, 361 // 4) + 1, jnp.int32)
        _ctx_512P = jax.random.normal(jax.random.fold_in(_rk, 11), (16, 16, 128), jnp.float32)
        _ctx_512c = jax.random.dirichlet(jax.random.fold_in(_rk, 511), 0.3 * jnp.ones((16,), jnp.float32), (16, 361))
        _ctx_512t = jnp.einsum('bsk,bkd->bsd', _ctx_512c, _ctx_512P)
        _ctx_512t = _ctx_512t * jax.lax.rsqrt(jnp.mean(jnp.square(_ctx_512t)) + 1e-12) * 0.953939
        ctx_512 = -0.000514642 + 1.00011 * (_ctx_512t + 0.3 * jax.random.normal(jax.random.fold_in(_rk, 611), (16, 361, 128), jnp.float32))
        _g = jax.random.normal(jax.random.fold_in(_rk, 9001), (2, 1), jnp.float32)
        _g = jnp.sign(_g) * jnp.maximum(jnp.abs(_g), 1.0) + (_g == 0) * 1.0
        g_xattn = _g[0]
        g_ffn = _g[1]
        return (x, ctx_512, g_xattn, g_ffn)
    x, ctx_512, g_xattn, g_ffn = _rec_inputs()

    def _L0_xattn_setup():
        import jax, jax.numpy as jnp
        import numpy as np
        B, S, H, NH, L = (2, 512, 512, 16, 128)
        HD = H // NH
        key = jax.random.key(seed)
        k1, k2, k3, k4, k5 = jax.random.split(key, 5)
        scale = 0.02
        return {'q': jax.random.normal(k1, (B, S, H), dtype=jnp.float32), 'latent_kv': jax.random.normal(k2, (B, S, L), dtype=jnp.float32), 'Wq': jax.random.normal(k3, (H, H), dtype=jnp.float32) * scale, 'Wkv_expand': jax.random.normal(k4, (2 * H, L), dtype=jnp.float32) * scale, 'Wout': jax.random.normal(k5, (H, H), dtype=jnp.float32) * scale}
    _L0_xattn_all = _L0_xattn_setup()
    _L0_xattn_in = {k: v for k, v in _L0_xattn_all.items() if k in ('Wq', 'Wkv_expand', 'Wout')}
    del _L0_xattn_all

    def _L0_ffn_setup():
        import jax, jax.numpy as jnp
        import numpy as np
        H, I, E = (512, 1024, 8)
        B, S = (2, 512)
        key = jax.random.key(seed)
        ks = jax.random.split(key, 5)
        scale = 0.02
        return {'hidden_states': jax.random.normal(ks[0], (B, S, H), dtype=jnp.float32), 'router_w': jax.random.normal(ks[1], (H, E), dtype=jnp.float32) * scale, 'gate_w': jax.random.normal(ks[2], (E, H, I), dtype=jnp.float32) * scale, 'up_w': jax.random.normal(ks[3], (E, H, I), dtype=jnp.float32) * scale, 'down_w': jax.random.normal(ks[4], (E, I, H), dtype=jnp.float32) * scale}
    _L0_ffn_all = _L0_ffn_setup()
    _L0_ffn_in = {k: v for k, v in _L0_ffn_all.items() if k in ('router_w', 'gate_w', 'up_w', 'down_w')}
    del _L0_ffn_all
    return {'x': x, 'ctx_512': ctx_512, 'g_xattn': g_xattn, 'g_ffn': g_ffn, 'L0_xattn_Wq': _L0_xattn_in['Wq'], 'L0_xattn_Wkv_expand': _L0_xattn_in['Wkv_expand'], 'L0_xattn_Wout': _L0_xattn_in['Wout'], 'L0_ffn_router_w': _L0_ffn_in['router_w'], 'L0_ffn_gate_w': _L0_ffn_in['gate_w'], 'L0_ffn_up_w': _L0_ffn_in['up_w'], 'L0_ffn_down_w': _L0_ffn_in['down_w']}

def reference(x, ctx_512, g_xattn, g_ffn, L0_xattn_Wq, L0_xattn_Wkv_expand, L0_xattn_Wout, L0_ffn_router_w, L0_ffn_gate_w, L0_ffn_up_w, L0_ffn_down_w):
    import jax
    import jax.numpy as jnp

    def _L0_xattn_ref(q, latent_kv, Wq, Wkv_expand, Wout):
        import jax, jax.numpy as jnp
        import numpy as np
        B, S, H, NH, L = (2, 512, 512, 16, 128)
        HD = H // NH
        b, sq, _ = q.shape
        sk = latent_kv.shape[1]
        qp = q @ Wq.T
        kv = latent_kv @ Wkv_expand.T
        k, v = jnp.split(kv, 2, axis=-1)
        qh = qp.reshape(b, sq, NH, HD).transpose(0, 2, 1, 3)
        kh = k.reshape(b, sk, NH, HD).transpose(0, 2, 1, 3)
        vh = v.reshape(b, sk, NH, HD).transpose(0, 2, 1, 3)
        inv_sqrt_d = 1.0 / jnp.sqrt(jnp.float32(HD))
        scores = jnp.einsum('bhqd,bhkd->bhqk', qh, kh) * inv_sqrt_d
        causal = jnp.tril(jnp.ones((sq, sk), dtype=bool))
        scores = jnp.where(causal, scores, jnp.finfo(scores.dtype).min)
        attn = jax.nn.softmax(scores, axis=-1)
        out = jnp.einsum('bhqk,bhkd->bhqd', attn, vh)
        out = out.transpose(0, 2, 1, 3).reshape(b, sq, H)
        return out @ Wout.T

    def _L0_ffn_ref(hidden_states, router_w, gate_w, up_w, down_w):
        import jax, jax.numpy as jnp
        import numpy as np
        H, I, E = (512, 1024, 8)
        B, S = (2, 512)
        hidden_shape = hidden_states.shape
        x = hidden_states.reshape(-1, hidden_shape[-1])
        route = jax.nn.sigmoid(x @ router_w)
        max_ind = jnp.argmax(route, axis=1)
        max_prob = jnp.take_along_axis(route, max_ind[:, None], axis=1)
        out = jnp.zeros_like(x)
        num_experts = gate_w.shape[0]
        for e in range(num_experts):
            mask = (max_ind == e)[:, None]
            h = jax.nn.silu(x @ gate_w[e]) * (x @ up_w[e])
            out = out + jnp.where(mask, h @ down_w[e], 0.0)
        out = out * max_prob
        return out.reshape(hidden_shape)
    x = x + jnp.tanh(g_xattn[0]) * _L0_xattn_ref(_layernorm(x, axis=-1), ctx_512, L0_xattn_Wq, L0_xattn_Wkv_expand, L0_xattn_Wout)
    x = x + jnp.tanh(g_ffn[0]) * _L0_ffn_ref(_layernorm(x, axis=-1), L0_ffn_router_w, L0_ffn_gate_w, L0_ffn_up_w, L0_ffn_down_w)
    return x

_drawn_inputs = setup_inputs


def setup_inputs(seed=0):
    import zlib

    import numpy as np

    out = dict(_drawn_inputs(seed))
    spreads = {}
    factors = {'L0_xattn_Wq': 27.611}
    for name, (base, spread) in spreads.items():
        noise = np.random.default_rng([zlib.crc32(name.encode()), seed]).standard_normal(out[name].shape)
        drawn = base * np.exp(spread * noise) if base else spread * noise
        out[name] = jnp.asarray(drawn.astype(out[name].dtype))
    for name, factor in factors.items():
        out[name] = (out[name] * factor).astype(out[name].dtype)
    return out
```

```python
from contextlib import ExitStack

import concourse.bass as bass
from concourse import mybir

F32 = mybir.dt.float32
F32R = mybir.dt.float32r
BF16 = mybir.dt.bfloat16
I32 = mybir.dt.int32
ALU = mybir.AluOpType
ACT = mybir.ActivationFunctionType
AX = mybir.AxisListType

P = 128
BANK = 512
EPS = 1e-5
MASKED = -3.0e38
OUT_OF_BOUNDS = 1 << 20
CREDIT = 2


class Signal:

    def __init__(self, sem, per, credit=0):
        self.sem, self.per, self.credit = sem, per, credit

    def after(self, turn, count):
        return turn * self.per + (self.credit + count)


class Chain:

    def __init__(self, eng, sem, per):
        self.eng, self.sem, self.per = eng, sem, per
        self.turn, self.base, self.count = 0, 0, 0

    def begin(self, turn, base):
        self.turn, self.base, self.count = turn, base, 0

    def link(self, ins):
        ins.then_inc(self.sem, 1)
        self.count += 1
        self.eng.wait_ge(self.sem, self.turn * self.per + (self.base + self.count))


def flamingo_block(nc, x, ctx, g_xattn, g_ffn, Wq, Wkv, Wout, router_w, gate_w, up_w, down_w, out):
    B, S, H = x.shape
    L = ctx.shape[2]
    E, _, I = gate_w.shape
    HD = 32
    NH = H // HD
    T = B * S
    KC = H // P
    CB = 4
    NCH = B // CB
    CT = CB * S
    HP = P // HD
    NT = CB * HP
    V1 = HD + 1
    SCALE = HD ** -0.5
    CAP = 256
    TT = CAP // P
    BLOCKS = -(-T // CAP)
    SLOTS = BLOCKS * CAP
    MORE = E * (BLOCKS - 1)
    UNITS_MAX = E + (T - E) // CAP
    NJ = 4
    JW = I // NJ
    JC = JW // P
    DEEP = 3
    XW = H + 8
    assert L == P and H == KC * P and CB * S <= BANK and JW * KC == JC * H == 1024

    xf = x.rearrange("b s d -> (b s) d")
    x_chunk = x.rearrange("(c i) s d -> c s i d", i=CB)
    ctx_chunk = ctx[:, 0:S, :].rearrange("(c i) s d -> c s i d", i=CB)
    of = out.rearrange("b s d -> (b s) d")

    x1_rows = nc.dram_tensor("x1_rows", [T, XW], F32, kind="Internal").ap()
    x2_rows = nc.dram_tensor("x2_rows", [T, H], F32, kind="Internal").ap()
    token_table = nc.dram_tensor("token_table", [E * SLOTS, 1], I32, kind="Internal").ap()
    unit_table = nc.dram_tensor("unit_table", [UNITS_MAX, 2], I32, kind="Internal").ap()

    st = ExitStack()
    with st:
        def sb(name, shape, dt):
            return st.enter_context(nc.sbuf_tensor(name, shape, dt))

        def sem(name):
            return st.enter_context(nc.semaphore(name))

        ident = sb("ident", [P, P], F32)
        mask = sb("mask", [P, S], F32)
        before = sb("before", [P, S], BF16)
        ones = sb("ones", [P, S], BF16)
        rev_e = sb("rev_e", [P, E], F32)
        tanh_x = sb("tanh_x", [P, 1], F32)
        tanh_f = sb("tanh_f", [P, 1], F32)
        gates = sb("gates", [P, 2], F32)
        thr = sb("thr", [P, MORE], F32)
        earlier = sb("earlier", [P, MORE], F32)
        unit_row = sb("unit_row", [P, 2], I32)
        first_rows = sb("first_rows", [E, 2], I32)
        empty = sb("empty", [P, E * SLOTS // P], I32)

        wq_hi = sb("wq_hi", [P, KC, H], F32R)
        wq_lo = sb("wq_lo", [P, KC, H], F32R)
        wo_hi = sb("wo_hi", [P, KC, H], F32R)
        wo_lo = sb("wo_lo", [P, KC, H], F32R)
        wkv_hi = sb("wkv_hi", [P, 2 * H], F32R)
        wkv_lo = sb("wkv_lo", [P, 2 * H], F32R)
        router = sb("router", [P, KC, E], F32)

        xt = sb("xt", [P, CB, H], F32)
        xn = sb("xn", [P, CB, H], F32)
        x_hi = sb("x_hi", [P, KC, CT], F32R)
        x_lo = sb("x_lo", [P, KC, CT], F32R)
        ctx_t = sb("ctx_t", [P, CB, L], F32)
        c_hi = sb("c_hi", [P, CT], F32R)
        c_lo = sb("c_lo", [P, CT], F32R)
        qT = sb("qT", [P, KC, CT], F32)
        kT = sb("kT", [P, KC, CT], F32)
        v = sb("v", [P, CB, NH, HD], F32)
        sm = sb("sm", [P, DEEP, HP, S], F32)
        pr = sb("pr", [P, 2, HP, S], F32)
        pn = sb("pn", [P, DEEP, HP, S], F32)
        pT = sb("pT", [P, DEEP, HP, S], F32)
        nmx = sb("nmx", [P, DEEP, HP], F32)
        tot = sb("tot", [P, DEEP, HP], F32)
        inv = sb("inv", [P, DEEP, HP], F32)
        ao_hi = sb("ao_hi", [P, KC, S], F32R)
        ao_lo = sb("ao_lo", [P, KC, S], F32R)
        xr = sb("xr", [P, 2, H], F32)
        x1 = sb("x1", [P, CB, XW], F32)
        x2 = sb("x2", [P, CB, H], F32)

        class NormBuffers:

            def __init__(self, name):
                self.bn = sb(f"{name}_bn", [P, CB, 6], F32)
                self.half = sb(f"{name}_half", [P, CB], I32)
                self.mean, self.var, self.nhv, self.tmp, self.rstd, self.shift = (
                    sb(f"{name}_{k}", [P, CB], F32) for k in ("mean", "var", "nhv", "tmp", "rstd", "shift"))

        norm1, norm2 = NormBuffers("norm1"), NormBuffers("norm2")

        ex = sb("ex", [P, CB, E], F32)
        sig = sb("sig", [P, CB, E], F32)
        cand = sb("cand", [P, CB, E], F32)
        prob = sb("prob", [P, CB], F32)
        best = sb("best", [P, CB], F32)
        hot = sb("hot", [P, CB, E], BF16)
        pos = sb("pos", [P, CB, E], F32)
        slot_f = sb("slot_f", [P, CB], F32)
        slot_i = sb("slot_i", [P, CB], I32)
        next_slot = sb("next_slot", [P, E], F32)
        tok_f = sb("tok_f", [P, CB], F32)
        tok_i = sb("tok_i", [P, CB], I32)
        valid = sb("valid", [P, E, BLOCKS - 1], F32)
        picked = sb("picked", [P, MORE], F32)
        u_rank = sb("u_rank", [P, 1], F32)
        u_valid = sb("u_valid", [P, 1], F32)
        u_slot = sb("u_slot", [P, 1], I32)
        u_count = sb("u_count", [P, 1], F32)
        more_units = sb("more_units", [P, 1], I32)
        units = sb("units", [1, 2 * UNITS_MAX], I32)

        raw = sb("raw", [P, 2, 3, 1024], F32)
        gu_hi = sb("gu_hi", [P, 2, 2, KC, JW], F32R)
        gu_lo = sb("gu_lo", [P, 2, 2, KC, JW], F32R)
        idx_next = sb("idx_next", [P, TT], I32)
        idx_now = sb("idx_now", [P, TT], I32)
        dn_hi, dn_lo = (w[:].rearrange("p (s k) n -> p s k n", s=2) for w in (wq_hi, wq_lo))
        h_hi, h_lo = (w[:].rearrange("p (s k n) -> p s k n", s=2, k=JC) for w in (wkv_hi, wkv_lo))
        x2T = xn[:].rearrange("p i d -> p (i d)")[:, 0:KC * CT].rearrange("p (k t) -> p k t", k=KC)
        xg = x2
        x1g = x1
        rows = xn
        silu_g = kT[:, 0:2, 0:JC * CAP // 2]
        h_f = qT[:, 0:2, 0:JC * CAP // 2]
        wq_raw = raw[:, 0, 0:2, :].rearrange("p a b -> p (a b)").rearrange("p (o i) -> p o i", o=KC)
        wo_raw = raw[:, 1, 0:2, :].rearrange("p a b -> p (a b)").rearrange("p (o i) -> p o i", o=KC)
        wkv_raw = raw[:, 0, 2, :].rearrange("p (r l) -> p r l", l=L)

        banks = [st.enter_context(nc.psum_tensor(f"bank{i}", [P, BANK], F32)) for i in range(8)]
        score_b, turn_b, out_b, misc_b = banks[0:3], banks[3:5], banks[5:7], banks[7]
        gate_b, up_b, y_b, xT_b = banks[0:2], banks[2:4], banks[4:6], banks[6:8]

        wq_loaded, wo_loaded, wkv_loaded = sem("wq_loaded"), sem("wo_loaded"), sem("wkv_loaded")
        small_loaded = sem("small_loaded")
        consts = sem("consts")
        tanh_done = sem("tanh_done")
        w_turned, w_hi_done, w_lo_done = sem("w_turned"), sem("w_hi_done"), sem("w_lo_done")

        xt_loaded = Signal(sem("xt_loaded"), 16)
        ctx_loaded = Signal(sem("ctx_loaded"), 16)
        xr_loaded = [Signal(sem(f"xr_loaded{i}"), 16 * CB // 2) for i in range(2)]
        ln1_ready = Signal(sem("ln1_ready"), 1)
        xn_done = Signal(sem("xn_done"), CB, CB)
        xT_ready = Signal(sem("xT_ready"), CB)
        x_hi_done = Signal(sem("x_hi_done"), CB)
        x_lo_done = Signal(sem("x_lo_done"), CB)
        cT_ready = Signal(sem("cT_ready"), 1, 1)
        c_hi_done = Signal(sem("c_hi_done"), 1)
        c_lo_done = Signal(sem("c_lo_done"), 1)
        q_ready = Signal(sem("q_ready"), KC)
        q_done = Signal(sem("q_done"), KC)
        k_ready = Signal(sem("k_ready"), KC)
        k_done = Signal(sem("k_done"), KC)
        v_ready = Signal(sem("v_ready"), CB)
        v_done = Signal(sem("v_done"), CB)
        s_ready = Signal(sem("s_ready"), NT)
        masked = Signal(sem("masked"), NT, NT)
        max_done = Signal(sem("max_done"), NT)
        exp_done = Signal(sem("exp_done"), NT, DEEP)
        inv_done = Signal(sem("inv_done"), NT)
        probs = Signal(sem("probs"), NT, DEEP)
        pT_ready = Signal(sem("pT_ready"), NT, DEEP)
        pT_copied = Signal(sem("pT_copied"), NT, NT)
        o_ready = Signal(sem("o_ready"), NT, DEEP)
        ao_hi_done = Signal(sem("ao_hi_done"), CB)
        ao_lo_done = Signal(sem("ao_lo_done"), CB)
        y_ready = Signal(sem("y_ready"), CB, 1)
        x1_done = Signal(sem("x1_done"), CB, 2)
        ln2_ready = Signal(sem("ln2_ready"), 1)
        x2_done = Signal(sem("x2_done"), CB)
        x2T_ready = Signal(sem("x2T_ready"), CB)
        x2T_copied = Signal(sem("x2T_copied"), CB)
        logits_ready = Signal(sem("logits_ready"), 1)
        ex_done = Signal(sem("ex_done"), 1)
        hot_done = Signal(sem("hot_done"), 1)
        rank_ready = Signal(sem("rank_ready"), 1)
        rank_used = Signal(sem("rank_used"), 1, 1)
        slots_done = Signal(sem("slots_done"), 1)
        rows_stored = Signal(sem("rows_stored"), 32, 16)
        tok_scattered = Signal(sem("tok_scattered"), 16 * CB, 16 * 3)
        dve_chain = sem("dve_chain")

        rows_known = sem("rows_known")
        wait_passed = sem("wait_passed")
        units_scattered = sem("units_scattered")
        units_loaded = sem("units_loaded")
        raw_loaded = [[Signal(sem(f"raw_loaded{w}_{s}"), 16 * NJ // 2) for s in range(2)] for w in range(3)]
        w_hi = [Signal(sem(f"w_hi{w}"), NJ) for w in range(3)]
        w_lo = [Signal(sem(f"w_lo{w}"), NJ, 2) for w in range(3)]
        gu_ready = Signal(sem("gu_ready"), NJ, 2)
        dn_done = Signal(sem("dn_done"), NJ, 2)
        silu_done = Signal(sem("silu_done"), NJ, 2)
        h_done = Signal(sem("h_done"), NJ, 2)
        h_hi_done = Signal(sem("h_hi_done"), NJ, 1)
        h_lo_done = Signal(sem("h_lo_done"), NJ, 1)
        idx_next_loaded = Signal(sem("idx_next_loaded"), 16)
        idx_now_loaded = Signal(sem("idx_now_loaded"), 16)
        xg_loaded = Signal(sem("xg_loaded"), 16 * TT)
        x1g_loaded = Signal(sem("x1g_loaded"), 16 * TT)
        gT_ready = Signal(sem("gT_ready"), TT)
        g_hi_done = Signal(sem("g_hi_done"), TT)
        g_lo_done = Signal(sem("g_lo_done"), TT, TT)
        rows_done = Signal(sem("rows_done"), TT, TT)
        rows_sent = Signal(sem("rows_sent"), 16 * TT)
        unit_sent = Signal(sem("unit_sent"), 1, 1)

        CONSTS = 18

        block = st.enter_context(nc.Block())

        @block.sync
        def _(sp):
            sp.sem_inc(rows_stored.sem, rows_stored.credit)
            sp.dma_start(xt[0:S], x_chunk[0]).then_inc(xt_loaded.sem, 16)
            sp.dma_start(ctx_t[0:S], ctx_chunk[0]).then_inc(ctx_loaded.sem, 16)
            sp.dma_start(wq_raw, Wq.rearrange("(o p) i -> p o i", p=P)).then_inc(wq_loaded, 16)
            sp.dma_start(gates[:, 0:1], g_xattn.rearrange("(a b) -> a b", a=1).to_broadcast([P, 1])).then_inc(small_loaded, 16)
            sp.dma_start(gates[:, 1:2], g_ffn.rearrange("(a b) -> a b", a=1).to_broadcast([P, 1])).then_inc(small_loaded, 16)
            sp.dma_start(router[:], router_w.rearrange("(k p) e -> p k e", p=P)).then_inc(small_loaded, 16)
            sp.dma_start(wkv_raw, Wkv.rearrange("(r p) l -> p r l", p=P)).then_inc(wkv_loaded, 16)
            sp.dma_start(wo_raw, Wout.rearrange("(o p) i -> p o i", p=P)).then_inc(wo_loaded, 16)

            def load_chunk(c):
                sp.wait_ge(xn_done.sem, xn_done.after(c, 0))
                sp.dma_start(xt[0:S], x_chunk[bass.ds(c, 1)].rearrange("c s i d -> (c s) i d")).then_inc(xt_loaded.sem, 16)
                sp.wait_ge(cT_ready.sem, cT_ready.after(c, 0))
                sp.dma_start(ctx_t[0:S], ctx_chunk[bass.ds(c, 1)].rearrange("c s i d -> (c s) i d")).then_inc(ctx_loaded.sem, 16)

            def residuals_and_stores(c):
                for i in range(CB):
                    sp.wait_ge(x1_done.sem, x1_done.after(c, i - 1))
                    sp.dma_start(xr[0:S, i % 2, :], xf[bass.ds(c * CT + i * S, S), :]).then_inc(xr_loaded[i % 2].sem, 16)
                sp.wait_ge(slots_done.sem, slots_done.after(c, 1))
                sp.dma_start(x2_rows[bass.ds(c * CT, CT), :].rearrange("(i s) d -> s i d", s=S), x2[0:S]).then_inc(rows_stored.sem, 16)
                sp.dma_start(x1_rows[bass.ds(c * CT, CT), :].rearrange("(i s) d -> s i d", s=S), x1[0:S]).then_inc(rows_stored.sem, 16)

            with sp.Fori(0, NCH - 1) as c:
                load_chunk(c + 1)
                residuals_and_stores(c)
            residuals_and_stores(NCH - 1)

            def load_step(e, u, j):
                s = j % 2
                src = [gate_w[bass.ds(e, 1), :, j * JW:(j + 1) * JW].rearrange("e (k p) n -> p (e k) n", p=P),
                       up_w[bass.ds(e, 1), :, j * JW:(j + 1) * JW].rearrange("e (k p) n -> p (e k) n", p=P),
                       down_w[bass.ds(e, 1), j * JW:(j + 1) * JW, :].rearrange("e (k p) n -> p (e k) n", p=P)]
                for w in range(3):
                    sp.wait_ge(w_lo[w].sem, w_lo[w].after(u, j - 1))
                    k = KC if w < 2 else JC
                    sp.dma_start(raw[:, s, w, :].rearrange("p (k n) -> p k n", k=k), src[w]).then_inc(raw_loaded[w][s].sem, 16)

            sp.wait_ge(w_turned, 10)
            for j in range(2):
                load_step(0, 0, j)
            sp.wait_ge(units_scattered, 16)
            sp.dma_start(units[:], unit_table.rearrange("(a u) w -> a (u w)", a=1)).then_inc(units_loaded, 16)
            for j in range(2, NJ):
                load_step(0, 0, j)
            sp.wait_ge(units_loaded, 16)
            sp.wait_ge(rows_known, 1)
            more = sp.value_load(more_units[0:1, 0:1], min_val=0, max_val=UNITS_MAX - E)
            with sp.Fori(1, more + E) as u:
                e = sp.value_load(units[0:1, bass.ds(u * 2, 1)], min_val=0, max_val=E - 1)
                for j in range(NJ):
                    load_step(e, u, j)

        @block.gpsimd
        def _(pool):
            nc.gpsimd.memset(ident[:], 0.0).then_inc(consts, 1)
            nc.gpsimd.memset(mask[:], 0.0).then_inc(consts, 1)
            nc.gpsimd.memset(before[:], 1.0).then_inc(consts, 1)
            nc.gpsimd.memset(ones[:], 1.0).then_inc(consts, 1)
            nc.gpsimd.memset(earlier[:], 1.0).then_inc(consts, 1)
            nc.gpsimd.memset(empty[:], OUT_OF_BOUNDS).then_inc(consts, 1)
            pool.wait_ge(consts, 6)
            nc.gpsimd.affine_select(out=ident[:], in_=ident[:], compare_op=ALU.not_equal, fill=1.0, base=0,
                                    pattern=[[-1, P]], channel_multiplier=1).then_inc(consts, 1)
            nc.gpsimd.affine_select(out=mask[:], in_=mask[:], compare_op=ALU.is_ge, fill=MASKED, base=0,
                                    pattern=[[-1, S]], channel_multiplier=1).then_inc(consts, 1)
            nc.gpsimd.affine_select(out=before[:], in_=before[:], compare_op=ALU.is_ge, fill=0.0, base=-1,
                                    pattern=[[1, S]], channel_multiplier=-1).then_inc(consts, 1)
            nc.gpsimd.affine_select(out=earlier[:], in_=earlier[:], compare_op=ALU.is_ge, fill=0.0, base=-1,
                                    pattern=[[-1, MORE]], channel_multiplier=1).then_inc(consts, 1)
            nc.gpsimd.iota(rev_e[:], [[-1, E]], base=E, channel_multiplier=0,
                           allow_small_or_imprecise_dtypes=True).then_inc(consts, 1)
            nc.gpsimd.iota(next_slot[:], [[SLOTS, E]], base=0, channel_multiplier=0,
                           allow_small_or_imprecise_dtypes=True).then_inc(consts, 1)
            nc.gpsimd.iota(thr[:], [[SLOTS, E], [CAP, BLOCKS - 1]], base=CAP, channel_multiplier=0,
                           allow_small_or_imprecise_dtypes=True).then_inc(consts, 1)
            nc.gpsimd.iota(tok_f[:], [[S, CB]], base=0, channel_multiplier=1,
                           allow_small_or_imprecise_dtypes=True).then_inc(consts, 1)
            nc.gpsimd.memset(x1[:], 0.0).then_inc(consts, 1)
            nc.gpsimd.memset(x2[:], 0.0).then_inc(consts, 1)
            nc.gpsimd.iota(first_rows[:, 0:1], [[0, 1]], base=0, channel_multiplier=1).then_inc(consts, 1)
            nc.gpsimd.iota(first_rows[:, 1:2], [[0, 1]], base=0, channel_multiplier=SLOTS).then_inc(consts, 1)
            pool.wait_ge(consts, CONSTS)
            nc.gpsimd.dma_start(token_table.rearrange("(p n) o -> p (n o)", p=P), empty[:]).then_inc(tok_scattered.sem, 16)
            nc.gpsimd.dma_start(unit_table[0:E, :], first_rows[:]).then_inc(tok_scattered.sem, 16)
            nc.gpsimd.dma_start(unit_table[E:UNITS_MAX, :], first_rows[0:UNITS_MAX - E, :]).then_inc(tok_scattered.sem, 16)
            for s in (xn_done, probs, unit_sent):
                pool.sem_inc(s.sem, s.credit)
            pool.wait_ge(tok_scattered.sem, tok_scattered.after(0, 0))

            def normalise(dst, src, ln, i):
                return nc.gpsimd.tensor_scalar(dst[0:S, i, :], src[0:S, i, 0:H], ln.rstd[0:S, i:i + 1],
                                               ln.shift[0:S, i:i + 1], ALU.mult, ALU.add)

            def normalise_chunk(c):
                pool.wait_ge(ln1_ready.sem, ln1_ready.after(c, 1))
                pool.sem_inc(wait_passed, 1)
                for i in range(CB):
                    normalise(xn, xt, norm1, i).then_inc(xn_done.sem, 1)

            def attend(c, last):
                for n in range(NT):
                    pool.wait_ge(inv_done.sem, inv_done.after(c, n + 1))
                    pool.wait_ge(pT_ready.sem, pT_ready.after(c, n + 1 - DEEP))
                    nc.gpsimd.tensor_tensor(pn[0:S, n % DEEP], pr[0:S, n % 2],
                                            inv[0:S, n % DEEP].unsqueeze(2).to_broadcast([S, HP, S]),
                                            ALU.mult).then_inc(probs.sem, 1)
                    if n == 9 and not last:
                        normalise_chunk(c + 1)

            def finish_chunk(c):
                pool.wait_ge(ln2_ready.sem, ln2_ready.after(c, 1))
                pool.wait_ge(rows_stored.sem, rows_stored.after(c, 0))
                pool.sem_inc(wait_passed, 1)
                for i in range(CB):
                    normalise(x2, x1, norm2, i).then_inc(x2_done.sem, 1)
                pool.wait_ge(slots_done.sem, slots_done.after(c, 1))
                pool.sem_inc(wait_passed, 1)
                for i in range(CB):
                    nc.gpsimd.indirect_dma_start(token_table, bass.IndirectOffsetOnAxis(ap=slot_i[0:S, i:i + 1], axis=0),
                                                 tok_i[0:S, i:i + 1], None).then_inc(tok_scattered.sem, 16)

            normalise_chunk(0)
            with pool.Fori(0, NCH - 1) as c:
                attend(c, False)
                finish_chunk(c)
            attend(NCH - 1, True)
            finish_chunk(NCH - 1)

            pool.wait_ge(rows_known, 1)
            nc.gpsimd.indirect_dma_start(unit_table, bass.IndirectOffsetOnAxis(ap=u_slot[0:MORE, :], axis=0),
                                         unit_row[0:MORE, :], None, bounds_check=UNITS_MAX - 1,
                                         oob_is_err=False).then_inc(units_scattered, 16)
            pool.wait_ge(rows_stored.sem, rows_stored.after(NCH, 0))
            pool.wait_ge(tok_scattered.sem, tok_scattered.after(NCH, 0))

            def gather_next(base, u):
                pool.wait_ge(g_lo_done.sem, g_lo_done.after(u, 0))
                nc.gpsimd.dma_start(idx_next[:], token_table[bass.ds(base, CAP), :].rearrange("(p t) o -> p (t o)", p=P)
                                    ).then_inc(idx_next_loaded.sem, 16)
                pool.wait_ge(idx_next_loaded.sem, idx_next_loaded.after(u, 16))
                pool.sem_inc(wait_passed, 1)
                for t in range(TT):
                    nc.gpsimd.indirect_dma_start(xg[:, t, :], None, x2_rows,
                                                 bass.IndirectOffsetOnAxis(ap=idx_next[:, t:t + 1], axis=0),
                                                 bounds_check=T - 1, oob_is_err=False).then_inc(xg_loaded.sem, 16)

            def gather_now(base, u):
                nc.gpsimd.dma_start(idx_now[:], token_table[bass.ds(base, CAP), :].rearrange("(p t) o -> p (t o)", p=P)
                                    ).then_inc(idx_now_loaded.sem, 16)
                pool.wait_ge(idx_now_loaded.sem, idx_now_loaded.after(u, 16))
                pool.sem_inc(wait_passed, 1)
                for t in range(TT):
                    nc.gpsimd.indirect_dma_start(x1g[:, t, :], None, x1_rows,
                                                 bass.IndirectOffsetOnAxis(ap=idx_now[:, t:t + 1], axis=0),
                                                 bounds_check=T - 1, oob_is_err=False).then_inc(x1g_loaded.sem, 16)

            def send_rows(u):
                for t in range(TT):
                    pool.wait_ge(rows_done.sem, rows_done.after(u, t + 1))
                    pool.sem_inc(wait_passed, 1)
                    nc.gpsimd.indirect_dma_start(of, bass.IndirectOffsetOnAxis(ap=idx_now[:, t:t + 1], axis=0),
                                                 rows[:, t, :], None, bounds_check=T - 1,
                                                 oob_is_err=False).then_inc(rows_sent.sem, 16)
                pool.wait_ge(rows_sent.sem, rows_sent.after(u, 16 * TT))
                pool.sem_inc(unit_sent.sem, 1)

            slot_max = E * SLOTS - CAP
            gather_next(0, 0)
            pool.wait_ge(units_loaded, 16)
            more = pool.value_load(more_units[0:1, 0:1], min_val=0, max_val=UNITS_MAX - E)
            with pool.Fori(0, more + (E - 1)) as u:
                base = pool.value_load(units[0:1, bass.ds(u * 2 + 3, 1)], min_val=0, max_val=slot_max)
                gather_next(base, u + 1)
                base = pool.value_load(units[0:1, bass.ds(u * 2 + 1, 1)], min_val=0, max_val=slot_max)
                gather_now(base, u)
                send_rows(u)
            base = pool.value_load(units[0:1, bass.ds(more * 2 + (2 * E - 1), 1)], min_val=0, max_val=slot_max)
            last = more + (E - 1)
            gather_now(base, last)
            send_rows(last)

        @block.scalar
        def _(act):
            def copy(dst, src):
                return nc.scalar.activation(dst, src, ACT.Copy)

            act.wait_ge(small_loaded, 48)
            nc.scalar.activation(tanh_x[:], gates[:, 0:1], ACT.Tanh).then_inc(tanh_done, 1)
            nc.scalar.activation(tanh_f[:], gates[:, 1:2], ACT.Tanh).then_inc(tanh_done, 1)
            for s in (exp_done, pT_copied, silu_done, h_hi_done):
                act.sem_inc(s.sem, s.credit)
            for n in range(10):
                act.wait_ge(w_turned, n + 1)
                dst = wq_hi[:, n, :] if n < KC else wkv_hi[:, (n - 4) * 512:(n - 3) * 512] if n < 6 else wo_hi[:, n - 6, :]
                copy(dst, banks[n % 8][:]).then_inc(w_hi_done, 1)

            def split_token(c, i):
                act.wait_ge(xT_ready.sem, xT_ready.after(c, i + 1))
                copy(x_hi[:, :, i * S:(i + 1) * S],
                     misc_b[:, 0:KC * S].rearrange("p (k s) -> p k s", k=KC)).then_inc(x_hi_done.sem, 1)

            def split_context(c):
                act.wait_ge(cT_ready.sem, cT_ready.after(c, 1))
                copy(c_hi[:], misc_b[:, 0:CT]).then_inc(c_hi_done.sem, 1)

            def keep_query(c, m):
                act.wait_ge(q_ready.sem, q_ready.after(c, m + 1))
                nc.scalar.activation(qT[:, m, :], score_b[m % DEEP][:, 0:CT], ACT.Copy, scale=SCALE).then_inc(q_done.sem, 1)

            def keep_keys(c, m):
                act.wait_ge(k_ready.sem, k_ready.after(c, m + 1))
                copy(kT[:, m, :], score_b[(KC + m) % DEEP][:, 0:CT]).then_inc(k_done.sem, 1)

            def keep_values(c, i):
                act.wait_ge(v_ready.sem, v_ready.after(c, i + 1))
                copy(v[0:S, i].rearrange("p h d -> p (h d)"), turn_b[i % 2][0:S, :]).then_inc(v_done.sem, 1)

            def attend(c, last):
                for n in range(NT + 4):
                    if n < NT:
                        act.wait_ge(max_done.sem, max_done.after(c, n + 1))
                        act.wait_ge(probs.sem, probs.after(c, n - 2 + 1))
                        for h in range(HP):
                            ins = nc.scalar.activation(pr[0:S, n % 2, h, :], sm[0:S, n % DEEP, h, :], ACT.Exp,
                                                       bias=nmx[0:S, n % DEEP, h:h + 1],
                                                       accum_out=tot[0:S, n % DEEP, h:h + 1])
                        ins.then_inc(exp_done.sem, 1)
                    if 2 <= n < NT + 2:
                        m = n - 2
                        act.wait_ge(pT_ready.sem, pT_ready.after(c, m + 1))
                        act.wait_ge(o_ready.sem, o_ready.after(c, m + 1 - DEEP))
                        copy(pT[0:S, m % DEEP], turn_b[m % 2][0:S, 0:HP * S].rearrange("p (h s) -> p h s", h=HP)
                             ).then_inc(pT_copied.sem, 1)
                    if n >= 7 and n % HP == 3:
                        i = n // HP - 1
                        act.wait_ge(o_ready.sem, o_ready.after(c, HP * (i + 1)))
                        act.wait_ge(y_ready.sem, y_ready.after(c, i))
                        copy(ao_hi[:], out_b[i % 2][:, 0:KC * S].rearrange("p (k s) -> p k s", k=KC)).then_inc(ao_hi_done.sem, 1)
                    if 12 <= n < 12 + CB and not last:
                        split_token(c + 1, n - 12)
                    if n == 12 + CB and not last:
                        split_context(c + 1)

            def finish_chunk(c, last):
                if not last:
                    for m in range(KC):
                        keep_query(c + 1, m)
                for i in range(CB):
                    act.wait_ge(x2T_ready.sem, x2T_ready.after(c, i + 1))
                    copy(x2T[:, :, i * S:(i + 1) * S],
                         misc_b[:, 0:KC * S].rearrange("p (k s) -> p k s", k=KC)).then_inc(x2T_copied.sem, 1)
                if not last:
                    for m in range(KC):
                        keep_keys(c + 1, m)
                act.wait_ge(logits_ready.sem, logits_ready.after(c, 1))
                nc.scalar.activation(ex[0:S], misc_b[0:S, 0:CB * E].rearrange("p (i e) -> p i e", e=E), ACT.Exp,
                                     scale=-1.0).then_inc(ex_done.sem, 1)
                if not last:
                    for i in range(CB):
                        keep_values(c + 1, i)

            for i in range(CB):
                split_token(0, i)
            split_context(0)
            for m in range(KC):
                keep_query(0, m)
            for m in range(KC):
                keep_keys(0, m)
            for i in range(CB):
                keep_values(0, i)
            with act.Fori(0, NCH - 1) as c:
                attend(c, False)
                finish_chunk(c, False)
            attend(NCH - 1, True)
            finish_chunk(NCH - 1, True)

            def split(u, j, w):
                s = j % 2
                act.wait_ge(raw_loaded[w][s].sem, raw_loaded[w][s].after(u, 16 * (j // 2 + 1)))
                if w < 2:
                    act.wait_ge(gu_ready.sem, gu_ready.after(u, j - 1))
                    dst = gu_hi[:, s, w]
                else:
                    act.wait_ge(dn_done.sem, dn_done.after(u, j - 1))
                    dst = dn_hi[:, s]
                copy(dst, raw[:, s, w, :].rearrange("p (k n) -> p k n", k=KC if w < 2 else JC)).then_inc(w_hi[w].sem, 1)

            def split_tokens(u):
                for t in range(TT):
                    act.wait_ge(gT_ready.sem, gT_ready.after(u, t + 1))
                    copy(x_hi[:, :, t * P:(t + 1) * P], xT_b[t][:].rearrange("p (k s) -> p k s", k=KC)
                         ).then_inc(g_hi_done.sem, 1)

            def step(u, j):
                act.wait_ge(gu_ready.sem, gu_ready.after(u, j + 1))
                act.wait_ge(h_done.sem, h_done.after(u, j))
                nc.scalar.activation(silu_g, gate_b[j % 2][:].rearrange("p (a n) -> p a n", a=2), ACT.Silu
                                     ).then_inc(silu_done.sem, 1)
                act.wait_ge(h_done.sem, h_done.after(u, j + 1))
                act.wait_ge(dn_done.sem, dn_done.after(u, j - 1))
                copy(h_hi[:, j % 2], h_f).then_inc(h_hi_done.sem, 1)
                split(u, j, 2)

            act.wait_ge(units_loaded, 16)
            more = act.value_load(more_units[0:1, 0:1], min_val=0, max_val=UNITS_MAX - E)
            for w in range(2):
                split(0, 0, w)
            split_tokens(0)
            for w in range(2):
                split(0, 1, w)
            step(0, 0)
            with act.Fori(0, more + (E - 1)) as u:
                for j in range(1, NJ):
                    for w in range(2):
                        split(*((u, j + 1) if j + 1 < NJ else (u + 1, 0)), w)
                    if j == NJ - 1:
                        act.wait_ge(gu_ready.sem, gu_ready.after(u, NJ))
                        split_tokens(u + 1)
                    step(u, j)
                for w in range(2):
                    split(u + 1, 1, w)
                step(u + 1, 0)
            last = more + (E - 1)
            for j in range(1, NJ):
                if j + 1 < NJ:
                    for w in range(2):
                        split(last, j + 1, w)
                step(last, j)

        @block.vector
        def _(dve):
            PER_CHUNK = 54
            chain = Chain(dve, dve_chain, PER_CHUNK)
            link = chain.link

            def lo_part(dst, src, hi):
                return nc.vector.tensor_tensor(dst, src, hi.bitcast(F32), ALU.subtract)

            def norm_step(ln, part):
                mean, var, nhv, tmp, rstd, shift = (t[0:S] for t in (ln.mean, ln.var, ln.nhv, ln.tmp, ln.rstd, ln.shift))
                even_mean, even_m2, odd_mean, odd_m2 = (ln.bn[0:S, :, k] for k in (1, 2, 4, 5))
                if part == 0:
                    nc.vector.tensor_tensor(mean, even_mean, odd_mean, ALU.add)
                    nc.vector.tensor_tensor(var, even_m2, odd_m2, ALU.add)
                    link(nc.vector.tensor_tensor(tmp, even_mean, odd_mean, ALU.subtract))
                elif part == 1:
                    link(nc.vector.scalar_tensor_tensor(out=tmp, in0=tmp, scalar=0.25, in1=tmp, op0=ALU.mult, op1=ALU.mult))
                elif part == 2:
                    link(nc.vector.scalar_tensor_tensor(out=var, in0=var, scalar=1.0 / H, in1=tmp, op0=ALU.mult, op1=ALU.add))
                elif part == 3:
                    link(nc.vector.tensor_scalar(var, var, EPS, None, ALU.add))
                elif part == 4:
                    nc.vector.tensor_scalar(nhv, var, -0.5, None, ALU.mult)
                    link(nc.vector.tensor_scalar(ln.half[0:S], var.bitcast(I32), 1, None, ALU.logical_shift_right))
                elif part == 5:
                    link(nc.vector.tensor_scalar(rstd.bitcast(I32), ln.half[0:S], -1.0, float(0x5F3759DF), ALU.mult, ALU.add))
                elif part < 15:
                    if part % 3 == 0:
                        link(nc.vector.tensor_tensor(tmp, rstd, rstd, ALU.mult))
                    elif part % 3 == 1:
                        link(nc.vector.tensor_tensor(tmp, tmp, nhv, ALU.mult))
                    else:
                        link(nc.vector.scalar_tensor_tensor(out=rstd, in0=tmp, scalar=1.5, in1=rstd, op0=ALU.add, op1=ALU.mult))
                else:
                    link(nc.vector.scalar_tensor_tensor(out=shift, in0=mean, scalar=-0.5, in1=rstd, op0=ALU.mult, op1=ALU.mult))

            NORM_STEPS = 16

            for s in (masked, x1_done, rank_used, h_done, h_lo_done, g_lo_done, rows_done, *w_lo):
                dve.sem_inc(s.sem, s.credit)
            for n in range(10):
                dve.wait_ge(w_hi_done, n + 1)
                hi, lo = ((wq_hi[:, n, :], wq_lo[:, n, :]) if n < KC else
                          (wkv_hi[:, (n - 4) * 512:(n - 3) * 512], wkv_lo[:, (n - 4) * 512:(n - 3) * 512]) if n < 6 else
                          (wo_hi[:, n - 6, :], wo_lo[:, n - 6, :]))
                lo_part(lo, banks[n % 8][:], hi).then_inc(w_lo_done, 1)
            dve.wait_ge(consts, CONSTS)
            dve.wait_ge(tanh_done, 2)
            chain.begin(0, 0)
            link(nc.vector.tensor_tensor(picked[0:MORE], thr[0:MORE], ident[0:MORE, 0:MORE], ALU.mult))
            link(nc.vector.tensor_reduce(u_rank[0:MORE], picked[0:MORE], AX.X, ALU.add))
            link(nc.vector.tensor_copy(unit_row[0:MORE, 1:2], u_rank[0:MORE]))
            link(nc.vector.tensor_tensor(valid[0:MORE], ident[0:MORE, 0:MORE].rearrange("p (e k) -> p e k", e=E),
                                         rev_e[0:MORE].unsqueeze(2).to_broadcast([MORE, E, BLOCKS - 1]), ALU.mult))
            link(nc.vector.tensor_reduce(u_valid[0:MORE], valid[0:MORE].rearrange("p e k -> p (e k)"), AX.X, ALU.add))
            link(nc.vector.tensor_scalar(unit_row[0:MORE, 0:1], u_valid[0:MORE], -1.0, float(E), ALU.mult, ALU.add))

            def stats(c, i):
                if i == 0:
                    dve.wait_ge(xt_loaded.sem, xt_loaded.after(c, 16))
                    dve.wait_ge(xn_done.sem, xn_done.after(c, 0))
                link(nc.vector.bn_stats(norm1.bn[0:S, i, :], xt[0:S, i, :]))

            def split_token(c, i):
                dve.wait_ge(x_hi_done.sem, x_hi_done.after(c, i + 1))
                lo_part(x_lo[:, :, i * S:(i + 1) * S], misc_b[:, 0:KC * S].rearrange("p (k s) -> p k s", k=KC),
                        x_hi[:, :, i * S:(i + 1) * S]).then_inc(x_lo_done.sem, 1)

            def split_context(c):
                dve.wait_ge(c_hi_done.sem, c_hi_done.after(c, 1))
                lo_part(c_lo[:], misc_b[:, 0:CT], c_hi[:]).then_inc(c_lo_done.sem, 1)

            def residual(c, i):
                dve.wait_ge(y_ready.sem, y_ready.after(c, i + 1))
                dve.wait_ge(xr_loaded[i % 2].sem, xr_loaded[i % 2].after(c, 16 * (i // 2 + 1)))
                dve.wait_ge(rows_stored.sem, rows_stored.after(c, 0))
                nc.vector.scalar_tensor_tensor(out=x1[0:S, i, 0:H], in0=out_b[i % 2][0:S, :], scalar=tanh_x[0:S, 0:1],
                                               in1=xr[0:S, i % 2, :], op0=ALU.mult, op1=ALU.add).then_inc(x1_done.sem, 1)
                dve.wait_ge(x1_done.sem, x1_done.after(c, i + 1))
                if i == 0:
                    dve.wait_ge(rank_used.sem, rank_used.after(c, 0))
                link(nc.vector.bn_stats(norm2.bn[0:S, i, :], x1[0:S, i, 0:H]))

            def attend(c, last):
                for n in range(NT + 6):
                    if n < NT:
                        b = n % DEEP
                        dve.wait_ge(s_ready.sem, s_ready.after(c, n + 1))
                        dve.wait_ge(exp_done.sem, exp_done.after(c, n + 1 - DEEP))
                        nc.vector.tensor_tensor(sm[0:S, b], score_b[b][0:S, 0:HP * S].rearrange("p (h s) -> p h s", h=HP),
                                                mask[0:S].unsqueeze(1).to_broadcast([S, HP, S]), ALU.add
                                                ).then_inc(masked.sem, 1)
                        dve.wait_ge(masked.sem, masked.after(c, n + 1))
                        nc.vector.tensor_reduce(nmx[0:S, b], sm[0:S, b], AX.X, ALU.max, negate=True).then_inc(max_done.sem, 1)
                    if 1 <= n <= NT:
                        b = (n - 1) % DEEP
                        dve.wait_ge(exp_done.sem, exp_done.after(c, n))
                        dve.wait_ge(probs.sem, probs.after(c, n - DEEP))
                        nc.vector.reciprocal(inv[0:S, b], tot[0:S, b]).then_inc(inv_done.sem, 1)
                    if n >= 8 and n % HP == 0:
                        i = n // HP - 2
                        dve.wait_ge(ao_hi_done.sem, ao_hi_done.after(c, i + 1))
                        lo_part(ao_lo[:], out_b[i % 2][:, 0:KC * S].rearrange("p (k s) -> p k s", k=KC), ao_hi[:]).then_inc(ao_lo_done.sem, 1)
                    if n >= 9 and n % HP == 1:
                        residual(c, n // HP - 2)
                    if n < CB and not last:
                        stats(c + 1, n)
                    elif n < CB + 4 and not last:
                        for part in range((n - CB) * 4, (n - CB) * 4 + 4):
                            norm_step(norm1, part)
                        if n == CB + 3:
                            dve.sem_inc(ln1_ready.sem, 1)
                    if 13 <= n < 13 + CB and not last:
                        split_token(c + 1, n - 13)
                    if n == 13 + CB and not last:
                        split_context(c + 1)

            def finish_chunk(c):
                for part in range(NORM_STEPS):
                    norm_step(norm2, part)
                dve.sem_inc(ln2_ready.sem, 1)
                dve.wait_ge(ex_done.sem, ex_done.after(c, 1))
                link(nc.vector.tensor_scalar(ex[0:S], ex[0:S], 1.0, None, ALU.add))
                link(nc.vector.reciprocal(sig[0:S], ex[0:S]))
                link(nc.vector.tensor_reduce(prob[0:S], sig[0:S], AX.X, ALU.max))
                link(nc.vector.tensor_tensor(cand[0:S], sig[0:S], prob[0:S].unsqueeze(2).to_broadcast([S, CB, E]), ALU.is_equal))
                link(nc.vector.tensor_tensor(cand[0:S], cand[0:S], rev_e[0:S].unsqueeze(1).to_broadcast([S, CB, E]), ALU.mult))
                link(nc.vector.tensor_reduce(best[0:S], cand[0:S], AX.X, ALU.max))
                nc.vector.tensor_tensor(hot[0:S], cand[0:S], best[0:S].unsqueeze(2).to_broadcast([S, CB, E]), ALU.is_equal
                                        ).then_inc(hot_done.sem, 1)
                link(nc.vector.tensor_scalar(x1[0:S, :, H], prob[0:S], tanh_f[0:S, 0:1], None, ALU.mult))
                dve.wait_ge(rank_ready.sem, rank_ready.after(c, 1))
                dve.wait_ge(tok_scattered.sem, tok_scattered.after(c, 0))
                link(nc.vector.tensor_tensor(pos[0:S], misc_b[0:S, 0:CB * E].rearrange("p (i e) -> p i e", e=E),
                                             next_slot[0:S].unsqueeze(1).to_broadcast([S, CB, E]), ALU.add))
                link(nc.vector.tensor_tensor(pos[0:S], pos[0:S], hot[0:S], ALU.mult))
                link(nc.vector.tensor_reduce(slot_f[0:S], pos[0:S], AX.X, ALU.add))
                link(nc.vector.tensor_copy(slot_i[0:S], slot_f[0:S]))
                link(nc.vector.tensor_copy(tok_i[0:S], tok_f[0:S]))
                link(nc.vector.tensor_scalar(tok_f[0:S], tok_f[0:S], float(CT), None, ALU.add))
                link(nc.vector.tensor_tensor(next_slot[0:S], next_slot[0:S], misc_b[0:S, CB * E:CB * E + E], ALU.add))
                dve.sem_inc(slots_done.sem, 1)
                dve.sem_inc(rank_used.sem, 1)

            for i in range(CB):
                stats(0, i)
            for part in range(NORM_STEPS):
                norm_step(norm1, part)
            dve.sem_inc(ln1_ready.sem, 1)
            for i in range(CB):
                split_token(0, i)
            split_context(0)
            FIRST = chain.count
            with dve.Fori(0, NCH - 1) as c:
                chain.begin(c, FIRST)
                attend(c, False)
                finish_chunk(c)
                assert chain.count == PER_CHUNK, chain.count
            chain.begin(NCH - 1, FIRST)
            attend(NCH - 1, True)
            finish_chunk(NCH - 1)

            link(nc.vector.tensor_tensor(valid[0:MORE], next_slot[0:MORE].unsqueeze(2).to_broadcast([MORE, E, BLOCKS - 1]),
                                         thr[0:MORE].rearrange("p (e k) -> p e k", e=E), ALU.is_gt))
            vflat = valid[0:MORE].rearrange("p e k -> p (e k)")
            link(nc.vector.tensor_reduce(u_count[0:MORE], vflat, AX.X, ALU.add))
            link(nc.vector.tensor_copy(more_units[0:MORE], u_count[0:MORE]))
            link(nc.vector.tensor_tensor(picked[0:MORE], vflat, earlier[0:MORE], ALU.mult))
            link(nc.vector.tensor_reduce(u_rank[0:MORE], picked[0:MORE], AX.X, ALU.add))
            link(nc.vector.tensor_tensor(picked[0:MORE], vflat, ident[0:MORE, 0:MORE], ALU.mult))
            link(nc.vector.tensor_reduce(u_valid[0:MORE], picked[0:MORE], AX.X, ALU.add))
            link(nc.vector.tensor_scalar(u_valid[0:MORE], u_valid[0:MORE], -float(OUT_OF_BOUNDS), float(E + OUT_OF_BOUNDS),
                                         ALU.mult, ALU.add))
            link(nc.vector.tensor_tensor(u_rank[0:MORE], u_rank[0:MORE], u_valid[0:MORE], ALU.add))
            nc.vector.tensor_copy(u_slot[0:MORE], u_rank[0:MORE]).then_inc(rows_known, 1)

            def split(u, j, w):
                s = j % 2
                dve.wait_ge(w_hi[w].sem, w_hi[w].after(u, j + 1))
                hi, lo = (gu_hi[:, s, w], gu_lo[:, s, w]) if w < 2 else (dn_hi[:, s], dn_lo[:, s])
                lo_part(lo, raw[:, s, w, :].rearrange("p (k n) -> p k n", k=KC if w < 2 else JC), hi).then_inc(w_lo[w].sem, 1)

            def split_tokens(u):
                for t in range(TT):
                    dve.wait_ge(g_hi_done.sem, g_hi_done.after(u, t + 1))
                    lo_part(x_lo[:, :, t * P:(t + 1) * P], xT_b[t][:].rearrange("p (k s) -> p k s", k=KC),
                            x_hi[:, :, t * P:(t + 1) * P]).then_inc(g_lo_done.sem, 1)

            def step(u, j):
                dve.wait_ge(silu_done.sem, silu_done.after(u, j + 1))
                dve.wait_ge(h_hi_done.sem, h_hi_done.after(u, j))
                dve.wait_ge(h_lo_done.sem, h_lo_done.after(u, j))
                nc.vector.tensor_tensor(h_f, silu_g, up_b[j % 2][:].rearrange("p (a n) -> p a n", a=2), ALU.mult
                                        ).then_inc(h_done.sem, 1)
                dve.wait_ge(h_hi_done.sem, h_hi_done.after(u, j + 1))
                lo_part(h_lo[:, j % 2], h_f, h_hi[:, j % 2]).then_inc(h_lo_done.sem, 1)
                split(u, j, 2)

            def finish(u):
                dve.wait_ge(dn_done.sem, dn_done.after(u, NJ))
                dve.wait_ge(x1g_loaded.sem, x1g_loaded.after(u, 16 * TT))
                dve.wait_ge(unit_sent.sem, unit_sent.after(u, 0))
                for t in range(TT):
                    nc.vector.scalar_tensor_tensor(out=rows[:, t, :], in0=y_b[t][:], scalar=x1g[:, t, H:H + 1],
                                                   in1=x1g[:, t, 0:H], op0=ALU.mult, op1=ALU.add).then_inc(rows_done.sem, 1)

            dve.wait_ge(units_loaded, 16)
            more = dve.value_load(more_units[0:1, 0:1], min_val=0, max_val=UNITS_MAX - E)
            for w in range(2):
                split(0, 0, w)
            split_tokens(0)
            for w in range(2):
                split(0, 1, w)
            step(0, 0)
            with dve.Fori(0, more + (E - 1)) as u:
                for j in range(1, NJ):
                    for w in range(2):
                        split(*((u, j + 1) if j + 1 < NJ else (u + 1, 0)), w)
                    if j == NJ - 1:
                        split_tokens(u + 1)
                    step(u, j)
                for w in range(2):
                    split(u + 1, 1, w)
                step(u + 1, 0)
                finish(u)
            last = more + (E - 1)
            for j in range(1, NJ):
                if j + 1 < NJ:
                    for w in range(2):
                        split(last, j + 1, w)
                step(last, j)
            finish(last)

        @block.tensor
        def _(pe):
            def three(dst, a, b, first, last):
                nc.tensor.matmul(dst, a[0], b[0], start=first, stop=False)
                nc.tensor.matmul(dst, a[0], b[1], start=False, stop=False)
                return nc.tensor.matmul(dst, a[1], b[0], start=False, stop=last)

            for s in (cT_ready, pT_ready, o_ready, y_ready, gu_ready, dn_done):
                pe.sem_inc(s.sem, s.credit)
            pe.wait_ge(consts, CONSTS)
            for n in range(10):
                pe.wait_ge(wq_loaded if n < 4 else wkv_loaded if n < 6 else wo_loaded, 16)
                if n >= 8:
                    pe.wait_ge(w_lo_done, n - 7)
                for o in range(4):
                    src = (wq_raw[:, o, n * P:(n + 1) * P] if n < 4 else wkv_raw[:, (n - 4) * 4 + o, :] if n < 6 else
                           wo_raw[:, o, (n - 6) * P:(n - 5) * P])
                    ins = nc.tensor.transpose(banks[n % 8][:, o * P:(o + 1) * P], src, ident[:])
                ins.then_inc(w_turned, 1)
            pe.wait_ge(w_lo_done, 10)
            pe.wait_ge(small_loaded, 48)

            def turn_chunk(c, i, first):
                pe.wait_ge(xn_done.sem, xn_done.after(c, i + 1))
                if i == 0 and not first:
                    pe.wait_ge(rank_used.sem, rank_used.after(c - 1, 0))
                if i:
                    pe.wait_ge(x_lo_done.sem, x_lo_done.after(c, i))
                for k in range(KC):
                    ins = nc.tensor.transpose(misc_b[:, k * S:(k + 1) * S], xn[0:S, i, k * P:(k + 1) * P], ident[0:S, 0:S])
                ins.then_inc(xT_ready.sem, 1)

            def turn_context(c):
                pe.wait_ge(ctx_loaded.sem, ctx_loaded.after(c, 16))
                pe.wait_ge(x_lo_done.sem, x_lo_done.after(c, CB))
                for i in range(CB):
                    ins = nc.tensor.transpose(misc_b[:, i * S:(i + 1) * S], ctx_t[0:S, i, :], ident[0:S, 0:S])
                ins.then_inc(cT_ready.sem, 1)

            def queries(c, m):
                if m == 0:
                    pe.wait_ge(x_lo_done.sem, x_lo_done.after(c, CB))
                    pe.wait_ge(masked.sem, masked.after(c, 0))
                if m >= DEEP:
                    pe.wait_ge(q_done.sem, q_done.after(c, m - DEEP + 1))
                for k in range(KC):
                    ins = three(score_b[m % DEEP][:, 0:CT], (wq_hi[:, k, m * P:(m + 1) * P], wq_lo[:, k, m * P:(m + 1) * P]),
                                (x_hi[:, k, :], x_lo[:, k, :]), k == 0, k == KC - 1)
                ins.then_inc(q_ready.sem, 1)

            def keys(c, m):
                if m == 0:
                    pe.wait_ge(c_lo_done.sem, c_lo_done.after(c, 1))
                if m < DEEP:
                    pe.wait_ge(q_done.sem, q_done.after(c, KC + m - DEEP + 1))
                else:
                    pe.wait_ge(k_done.sem, k_done.after(c, m - DEEP + 1))
                three(score_b[(KC + m) % DEEP][:, 0:CT], (wkv_hi[:, m * P:(m + 1) * P], wkv_lo[:, m * P:(m + 1) * P]),
                      (c_hi[:], c_lo[:]), True, True).then_inc(k_ready.sem, 1)

            def values(c, i):
                if i < 2:
                    pe.wait_ge(pT_copied.sem, pT_copied.after(c, 0))
                else:
                    pe.wait_ge(v_done.sem, v_done.after(c, i - 1))
                r = slice(i * S, (i + 1) * S)
                three(turn_b[i % 2][0:S, :], (c_hi[:, r], c_lo[:, r]), (wkv_hi[:, H:2 * H], wkv_lo[:, H:2 * H]),
                      True, True).then_inc(v_ready.sem, 1)

            def scores(c, n):
                i, j, b = n // HP, n % HP, n % DEEP
                if n == 0:
                    pe.wait_ge(k_done.sem, k_done.after(c, KC))
                if n >= DEEP:
                    pe.wait_ge(masked.sem, masked.after(c, n - DEEP + 1))
                for m in range(KC):
                    ins = nc.tensor.matmul(score_b[b][0:S, m * S:(m + 1) * S],
                                           qT[j * HD:(j + 1) * HD, m, i * S:(i + 1) * S],
                                           kT[j * HD:(j + 1) * HD, m, i * S:(i + 1) * S], start=True, stop=True,
                                           tile_position=(j * HD, 0))
                ins.then_inc(s_ready.sem, 1)

            def turn_probs(c, n):
                pe.wait_ge(probs.sem, probs.after(c, n + 1))
                if n < 2:
                    pe.wait_ge(v_done.sem, v_done.after(c, CB))
                else:
                    pe.wait_ge(pT_copied.sem, pT_copied.after(c, n - 1))
                for h in range(HP):
                    ins = nc.tensor.transpose(turn_b[n % 2][0:S, h * S:(h + 1) * S], pn[0:S, n % DEEP, h, :], ident[0:S, 0:S])
                ins.then_inc(pT_ready.sem, 1)

            def weigh(c, n):
                i, j = n // HP, n % HP
                pe.wait_ge(pT_copied.sem, pT_copied.after(c, n + 1))
                if j == 0:
                    pe.wait_ge(x1_done.sem, x1_done.after(c, i - 1))
                for m in range(KC):
                    ins = nc.tensor.matmul(out_b[i % 2][j * HD:(j + 1) * HD, m * S:(m + 1) * S], v[0:S, i, m * HP + j, :],
                                           pT[0:S, n % DEEP, m, :], start=True, stop=True, tile_position=(0, j * HD))
                ins.then_inc(o_ready.sem, 1)

            def project(c, i):
                pe.wait_ge(ao_lo_done.sem, ao_lo_done.after(c, i + 1))
                for k in range(KC):
                    ins = three(out_b[i % 2][0:S, :], (ao_hi[:, k, :], ao_lo[:, k, :]), (wo_hi[:, k, :], wo_lo[:, k, :]),
                                k == 0, k == KC - 1)
                ins.then_inc(y_ready.sem, 1)

            def turn_normed(c, i, last):
                pe.wait_ge(x2_done.sem, x2_done.after(c, i + 1))
                if i:
                    pe.wait_ge(x2T_copied.sem, x2T_copied.after(c, i))
                elif last:
                    pe.wait_ge(rank_used.sem, rank_used.after(c, 0))
                else:
                    pe.wait_ge(c_lo_done.sem, c_lo_done.after(c + 1, 1))
                for k in range(KC):
                    ins = nc.tensor.transpose(misc_b[:, k * S:(k + 1) * S], x2[0:S, i, k * P:(k + 1) * P], ident[0:S, 0:S])
                ins.then_inc(x2T_ready.sem, 1)

            def route(c):
                pe.wait_ge(x2T_copied.sem, x2T_copied.after(c, CB))
                for i in range(CB):
                    for k in range(KC):
                        ins = nc.tensor.matmul(misc_b[0:S, i * E:(i + 1) * E], x2T[:, k, i * S:(i + 1) * S], router[:, k, :],
                                               start=k == 0, stop=k == KC - 1)
                ins.then_inc(logits_ready.sem, 1)

            def rank(c):
                pe.wait_ge(hot_done.sem, hot_done.after(c, 1))
                nc.tensor.matmul(misc_b[0:S, 0:CB * E], before[0:S, :], hot[0:S].rearrange("p i e -> p (i e)"),
                                 start=True, stop=False, skip_group_check=True)
                for i in range(CB - 1):
                    later = CB - 1 - i
                    nc.tensor.matmul(misc_b[0:S, (i + 1) * E:CB * E], ones[0:S, :],
                                     hot[0:S, i:i + 1, :].to_broadcast([S, later, E]), start=False, stop=False,
                                     skip_group_check=True)
                for i in range(CB):
                    ins = nc.tensor.matmul(misc_b[0:S, CB * E:CB * E + E], ones[0:S, :], hot[0:S, i, :], start=False,
                                           stop=i == CB - 1, skip_group_check=True)
                ins.then_inc(rank_ready.sem, 1)

            def attend(c, last):
                for n in range(DEEP):
                    scores(c, n)
                for n in range(NT + 4):
                    if n < NT:
                        turn_probs(c, n)
                        if n + DEEP < NT:
                            scores(c, n + DEEP)
                    if 2 <= n < NT + 2:
                        weigh(c, n - 2)
                    if n >= 7 and n % HP == 3:
                        project(c, n // HP - 1)
                    if 11 <= n < 11 + CB and not last:
                        turn_chunk(c + 1, n - 11, False)
                    if n == 11 + CB and not last:
                        turn_context(c + 1)

            for i in range(CB):
                turn_chunk(0, i, True)
            turn_context(0)
            for m in range(KC):
                queries(0, m)
            for m in range(KC):
                keys(0, m)
            for i in range(CB):
                values(0, i)
            with pe.Fori(0, NCH - 1) as c:
                attend(c, False)
                for m in range(KC):
                    queries(c + 1, m)
                for i in range(CB):
                    turn_normed(c, i, False)
                for m in range(KC):
                    keys(c + 1, m)
                route(c)
                for i in range(CB):
                    values(c + 1, i)
                rank(c)
            attend(NCH - 1, True)
            for i in range(CB):
                turn_normed(NCH - 1, i, True)
            route(NCH - 1)
            rank(NCH - 1)

            def turn_tokens(u):
                pe.wait_ge(xg_loaded.sem, xg_loaded.after(u, 16 * TT))
                pe.wait_ge(g_lo_done.sem, g_lo_done.after(u, 0))
                for t in range(TT):
                    for k in range(KC):
                        ins = nc.tensor.transpose(xT_b[t][:, k * P:(k + 1) * P], xg[:, t, k * P:(k + 1) * P], ident[:])
                    ins.then_inc(gT_ready.sem, 1)

            def gate_up(u, j):
                s = j % 2
                if j == 0:
                    pe.wait_ge(g_lo_done.sem, g_lo_done.after(u, TT))
                for w, bank in ((0, gate_b[s]), (1, up_b[s])):
                    pe.wait_ge(w_lo[w].sem, w_lo[w].after(u, j + 1))
                    if w == 0:
                        pe.wait_ge(silu_done.sem, silu_done.after(u, j - 1))
                    else:
                        pe.wait_ge(h_done.sem, h_done.after(u, j - 1))
                    for m in range(JC):
                        for k in range(KC):
                            r = slice(m * P, (m + 1) * P)
                            ins = three(bank[:, m * CAP:(m + 1) * CAP], (gu_hi[:, s, w, k, r], gu_lo[:, s, w, k, r]),
                                        (x_hi[:, k, 0:CAP], x_lo[:, k, 0:CAP]), k == 0, k == KC - 1)
                ins.then_inc(gu_ready.sem, 1)

            def down(u, j):
                s = j % 2
                pe.wait_ge(w_lo[2].sem, w_lo[2].after(u, j + 1))
                pe.wait_ge(h_lo_done.sem, h_lo_done.after(u, j + 1))
                if j == 0:
                    pe.wait_ge(rows_done.sem, rows_done.after(u, 0))
                for t in range(TT):
                    for k in range(JC):
                        r = slice(t * P, (t + 1) * P)
                        ins = three(y_b[t][:], (h_hi[:, s, k, r], h_lo[:, s, k, r]), (dn_hi[:, s, k, :], dn_lo[:, s, k, :]),
                                    j == 0 and k == 0, j == NJ - 1 and k == JC - 1)
                ins.then_inc(dn_done.sem, 1)

            pe.wait_ge(units_loaded, 16)
            more = pe.value_load(more_units[0:1, 0:1], min_val=0, max_val=UNITS_MAX - E)
            turn_tokens(0)
            gate_up(0, 0)
            with pe.Fori(0, more + (E - 1)) as u:
                gate_up(u, 1)
                down(u, 0)
                gate_up(u, 2)
                down(u, 1)
                turn_tokens(u + 1)
                gate_up(u, 3)
                down(u, 2)
                gate_up(u + 1, 0)
                down(u, 3)
            last = more + (E - 1)
            gate_up(last, 1)
            down(last, 0)
            gate_up(last, 2)
            down(last, 1)
            gate_up(last, 3)
            down(last, 2)
            down(last, 3)


_INS = ["x", "ctx_512", "g_xattn", "g_ffn", "L0_xattn_Wq", "L0_xattn_Wkv_expand", "L0_xattn_Wout", "L0_ffn_router_w",
        "L0_ffn_gate_w", "L0_ffn_up_w", "L0_ffn_down_w"]


def kernel(**inputs):
    import numpy as np
    import concourse.bacc as bacc
    from concourse.bass_utils import run_bass_kernel_spmd

    nc = bacc.Bacc("TRN2", target_bir_lowering=False, num_devices=1)
    arrays, args = {}, []
    for name in _INS:
        a = np.ascontiguousarray(inputs[name])
        arrays[f"in_{name}"] = a
        args.append(nc.dram_tensor(f"in_{name}", a.shape, mybir.dt.from_np(a.dtype), kind="ExternalInput").ap())
    out = nc.dram_tensor("out_x", inputs["x"].shape, F32, kind="ExternalOutput").ap()
    flamingo_block(nc, *args, out)
    r = run_bass_kernel_spmd(nc, [arrays], core_ids=[0])
    return r.results[0]["out_x"]
```

```python
from contextlib import ExitStack

import concourse.bass as bass
from concourse import mybir

F32 = mybir.dt.float32
F32R = mybir.dt.float32r
BF16 = mybir.dt.bfloat16
I32 = mybir.dt.int32
ALU = mybir.AluOpType
ACT = mybir.ActivationFunctionType
AX = mybir.AxisListType

P = 128
BANK = 512
EPS = 1e-5
MASKED = -3.0e38
OUT_OF_BOUNDS = 1 << 20


class Signal:

    def __init__(self, sem, per, credit=0):
        self.sem, self.per, self.credit = sem, per, credit

    def after(self, turn, count):
        return turn * self.per + (self.credit + count)


class Chain:

    def __init__(self, eng, sem, per):
        self.eng, self.sem, self.per = eng, sem, per
        self.turn, self.base, self.count = 0, 0, 0

    def begin(self, turn, base):
        self.turn, self.base, self.count = turn, base, 0

    def link(self, ins):
        ins.then_inc(self.sem, 1)
        self.count += 1
        self.eng.wait_ge(self.sem, self.turn * self.per + (self.base + self.count))


def flamingo_block(nc, x, ctx, g_xattn, g_ffn, Wq, Wkv, Wout, router_w, gate_w, up_w, down_w, out):
    B, S, H = x.shape
    L = ctx.shape[2]
    E, _, I = gate_w.shape
    HD = 32
    NH = H // HD
    T = B * S
    KC = H // P
    CB = 4
    NCH = B // CB
    CT = CB * S
    HP = P // HD
    NT = CB * KC
    SCALE = HD ** -0.5
    CAP = 256
    TT = CAP // P
    BLOCKS = -(-T // CAP)
    SLOTS = BLOCKS * CAP
    MORE = E * (BLOCKS - 1)
    UNITS_MAX = E + (T - E) // CAP
    NJ = 4
    JW = I // NJ
    JC = JW // P
    DEEP = 3
    KEEP = HP + 2
    XW = H + 8
    assert L == P and H == KC * P and CB * S <= BANK and JW * KC == JC * H == 1024

    xf = x.rearrange("b s d -> (b s) d")
    x_chunk = x.rearrange("(c i) s d -> c s i d", i=CB)
    ctx_chunk = ctx[:, 0:S, :].rearrange("(c i) s d -> c s i d", i=CB)
    of = out.rearrange("b s d -> (b s) d")

    x1_rows = nc.dram_tensor("x1_rows", [T, XW], F32, kind="Internal").ap()
    x2_rows = nc.dram_tensor("x2_rows", [T, H], F32, kind="Internal").ap()
    token_table = nc.dram_tensor("token_table", [E * SLOTS, 1], I32, kind="Internal").ap()
    unit_table = nc.dram_tensor("unit_table", [UNITS_MAX, 2], I32, kind="Internal").ap()

    st = ExitStack()
    with st:
        def sb(name, shape, dt):
            return st.enter_context(nc.sbuf_tensor(name, shape, dt))

        def sem(name):
            return st.enter_context(nc.semaphore(name))

        ident = sb("ident", [P, P], F32)
        eye = sb("eye", [P, P], BF16)
        mask = sb("mask", [P, S], BF16)
        before = sb("before", [P, S], BF16)
        ones = sb("ones", [P, S], BF16)
        rev_e = sb("rev_e", [P, E], F32)
        tanh_x = sb("tanh_x", [P, 1], F32)
        tanh_f = sb("tanh_f", [P, 1], F32)
        gates = sb("gates", [P, 2], F32)
        thr = sb("thr", [P, MORE], F32)
        earlier = sb("earlier", [P, MORE], F32)
        unit_row = sb("unit_row", [P, 2], I32)
        first_rows = sb("first_rows", [E, 2], I32)
        empty = sb("empty", [P, E * SLOTS // P], I32)

        wq_hi = sb("wq_hi", [P, KC, H], F32R)
        wq_lo = sb("wq_lo", [P, KC, H], F32R)
        wo_hi = sb("wo_hi", [P, KC, H], F32R)
        wo_lo = sb("wo_lo", [P, KC, H], F32R)
        wkv_hi = sb("wkv_hi", [P, 2 * H], F32R)
        wkv_lo = sb("wkv_lo", [P, 2 * H], F32R)
        router = sb("router", [P, KC, E], F32)

        xt = sb("xt", [P, CB, H], F32)
        xn = sb("xn", [P, CB, H], F32)
        x_hi = sb("x_hi", [P, KC, CT], F32R)
        x_lo = sb("x_lo", [P, KC, CT], F32R)
        ctx_t = sb("ctx_t", [P, CB, L], F32)
        c_hi = sb("c_hi", [P, CT], F32R)
        c_lo = sb("c_lo", [P, CT], F32R)
        qT = sb("qT", [P, KC, CT], F32)
        v = sb("v", [P, CB, NH, HD], F32)
        pr = sb("pr", [P, 2, HP, S], F32)
        pn = sb("pn", [P, DEEP, HP, S], F32)
        pT = sb("pT", [P, KEEP, HP, S], F32)
        nmx = sb("nmx", [P, DEEP, HP], F32)
        tot = sb("tot", [P, DEEP, HP], F32)
        inv = sb("inv", [P, DEEP, HP], F32)
        ao_hi = sb("ao_hi", [P, KC, S], F32R)
        ao_lo = sb("ao_lo", [P, KC, S], F32R)
        xr = sb("xr", [P, 2, H], F32)
        x1 = sb("x1", [P, CB, XW], F32)
        x2 = sb("x2", [P, CB, H], F32)
        x2T = sb("x2T", [P, KC, CT], F32)

        class NormBuffers:

            def __init__(self, name):
                self.bn = sb(f"{name}_bn", [P, CB, 6], F32)
                self.half = sb(f"{name}_half", [P, CB], I32)
                self.mean, self.var, self.nhv, self.tmp, self.rstd, self.shift = (
                    sb(f"{name}_{k}", [P, CB], F32) for k in ("mean", "var", "nhv", "tmp", "rstd", "shift"))

        norm1, norm2 = NormBuffers("norm1"), NormBuffers("norm2")

        ex_t = sb("ex_t", [E, CT], F32)
        ex = sb("ex", [P, CB, E], F32)
        sig = sb("sig", [P, CB, E], F32)
        cand = sb("cand", [P, CB, E], F32)
        prob = sb("prob", [P, CB], F32)
        scale = sb("scale", [P, CB, XW - H], F32)
        best = sb("best", [P, CB], F32)
        hot = sb("hot", [P, CB, E], BF16)
        pos = sb("pos", [P, CB, E], F32)
        slot_f = sb("slot_f", [P, CB], F32)
        slot_i = sb("slot_i", [P, CB], I32)
        next_slot = sb("next_slot", [P, E], F32)
        tok_f = sb("tok_f", [P, CB], F32)
        tok_i = sb("tok_i", [P, CB], I32)
        valid = sb("valid", [P, E, BLOCKS - 1], F32)
        picked = sb("picked", [P, MORE], F32)
        u_rank = sb("u_rank", [P, 1], F32)
        u_valid = sb("u_valid", [P, 1], F32)
        u_slot = sb("u_slot", [P, 1], I32)
        u_count = sb("u_count", [P, 1], F32)
        more_units = sb("more_units", [P, 1], I32)
        units = sb("units", [1, 2 * UNITS_MAX], I32)

        staging = sb("staging", [P, max(2 * 3 * 1024, KC * CB * HP * S)], F32)
        raw = staging[:, 0:2 * 3 * 1024].rearrange("p (s w n) -> p s w n", s=2, w=3)
        keys_b = staging[:, 0:KC * CB * HP * S].rearrange("p (m i j s) -> p m i j s", m=KC, i=CB, j=HP)
        gu_hi = sb("gu_hi", [P, 2, 2, KC, JW], F32R)
        gu_lo = sb("gu_lo", [P, 2, 2, KC, JW], F32R)
        idx_next = sb("idx_next", [P, TT], I32)
        idx_now = sb("idx_now", [P, TT], I32)
        dn_hi, dn_lo = (w[:].rearrange("p (s k) n -> p s k n", s=2) for w in (wq_hi, wq_lo))
        h_hi, h_lo = (w[:].rearrange("p (s k n) -> p s k n", s=2, k=JC) for w in (wkv_hi, wkv_lo))
        xg = x2
        x1g = x1
        rows = xn
        silu_g = qT[:, 2:4, 0:JC * CAP // 2]
        h_f = qT[:, 0:2, 0:JC * CAP // 2]
        wq_raw = raw[:, 0, 0:2, :].rearrange("p a b -> p (a b)").rearrange("p (o i) -> p o i", o=KC)
        wo_raw = raw[:, 1, 0:2, :].rearrange("p a b -> p (a b)").rearrange("p (o i) -> p o i", o=KC)
        wkv_raw = raw[:, 0, 2, :].rearrange("p (r l) -> p r l", l=L)

        banks = [st.enter_context(nc.psum_tensor(f"bank{i}", [P, BANK], F32)) for i in range(8)]
        score_b, turn_b, out_b, misc_b = banks[0:3], banks[3:5], banks[5:7], banks[7]
        logits_p = misc_b[0:E, 0:CT]
        ex_p = misc_b[:, CT:CT + CB * E]
        rank_p = misc_b[:, CT + CB * E:CT + 2 * CB * E]
        total_p = misc_b[:, CT + 2 * CB * E:CT + 2 * CB * E + E]
        gate_b, up_b, y_b, xT_b = banks[0:2], banks[2:4], banks[4:6], banks[6:8]

        wq_loaded, wo_loaded, wkv_loaded = sem("wq_loaded"), sem("wo_loaded"), sem("wkv_loaded")
        small_loaded = sem("small_loaded")
        consts = sem("consts")
        tanh_done = sem("tanh_done")
        w_turned, w_hi_done, w_lo_done = sem("w_turned"), sem("w_hi_done"), sem("w_lo_done")

        xt_loaded = Signal(sem("xt_loaded"), 16)
        ctx_loaded = Signal(sem("ctx_loaded"), 16)
        xr_loaded = [Signal(sem(f"xr_loaded{i}"), 16 * CB // 2) for i in range(2)]
        ln1_ready = Signal(sem("ln1_ready"), 1)
        xn_done = Signal(sem("xn_done"), CB, CB)
        xT_ready = Signal(sem("xT_ready"), CB)
        x_hi_done = Signal(sem("x_hi_done"), CB)
        x_lo_done = Signal(sem("x_lo_done"), CB)
        cT_ready = Signal(sem("cT_ready"), 1, 1)
        c_hi_done = Signal(sem("c_hi_done"), 1)
        c_lo_done = Signal(sem("c_lo_done"), 1)
        q_ready = Signal(sem("q_ready"), KC)
        q_done = Signal(sem("q_done"), KC)
        k_ready = Signal(sem("k_ready"), KC)
        k_done = Signal(sem("k_done"), KC)
        keys_zeroed = sem("keys_zeroed")
        v_ready = Signal(sem("v_ready"), CB)
        v_done = Signal(sem("v_done"), CB)
        s_ready = Signal(sem("s_ready"), NT)
        max_done = Signal(sem("max_done"), NT)
        exp_done = Signal(sem("exp_done"), NT, DEEP)
        inv_done = Signal(sem("inv_done"), NT)
        probs = Signal(sem("probs"), NT, DEEP)
        pT_ready = Signal(sem("pT_ready"), NT, DEEP)
        pT_copied = Signal(sem("pT_copied"), NT, NT)
        o_ready = Signal(sem("o_ready"), CB, 1)
        ao_hi_done = Signal(sem("ao_hi_done"), CB)
        ao_lo_done = Signal(sem("ao_lo_done"), CB)
        y_ready = Signal(sem("y_ready"), CB, 1)
        x1_done = Signal(sem("x1_done"), CB, 2)
        ln2_ready = Signal(sem("ln2_ready"), 1)
        x2_done = Signal(sem("x2_done"), CB)
        x2T_ready = Signal(sem("x2T_ready"), CB)
        x2T_copied = Signal(sem("x2T_copied"), CB)
        logits_ready = Signal(sem("logits_ready"), 1)
        ex_t_done = Signal(sem("ex_t_done"), 1)
        ex_ready = Signal(sem("ex_ready"), 1)
        hot_done = Signal(sem("hot_done"), 1)
        rank_ready = Signal(sem("rank_ready"), 1)
        rank_used = Signal(sem("rank_used"), 1, 1)
        slots_done = Signal(sem("slots_done"), 1)
        rows_stored = Signal(sem("rows_stored"), 32, 16)
        scale_stored = Signal(sem("scale_stored"), 16, 1)
        tok_scattered = Signal(sem("tok_scattered"), 16 * CB, 16 * 3)
        dve_chain = sem("dve_chain")

        rows_known = sem("rows_known")
        wait_passed, pe_wait_passed = sem("wait_passed"), sem("pe_wait_passed")
        units_scattered = sem("units_scattered")
        units_loaded = sem("units_loaded")
        raw_loaded = [[Signal(sem(f"raw_loaded{w}_{s}"), 16 * NJ // 2) for s in range(2)] for w in range(3)]
        w_hi = [Signal(sem(f"w_hi{w}"), NJ) for w in range(3)]
        w_lo = [Signal(sem(f"w_lo{w}"), NJ, 2) for w in range(3)]
        gu_ready = Signal(sem("gu_ready"), NJ, 2)
        dn_done = Signal(sem("dn_done"), NJ, 2)
        silu_done = Signal(sem("silu_done"), NJ, 2)
        h_done = Signal(sem("h_done"), NJ, 2)
        h_hi_done = Signal(sem("h_hi_done"), NJ, 1)
        h_lo_done = Signal(sem("h_lo_done"), NJ, 1)
        idx_next_loaded = Signal(sem("idx_next_loaded"), 16)
        idx_now_loaded = Signal(sem("idx_now_loaded"), 16)
        xg_loaded = Signal(sem("xg_loaded"), 16 * TT)
        x1g_loaded = Signal(sem("x1g_loaded"), 16 * TT)
        gT_ready = Signal(sem("gT_ready"), TT)
        g_hi_done = Signal(sem("g_hi_done"), TT)
        g_lo_done = Signal(sem("g_lo_done"), TT, TT)
        rows_done = Signal(sem("rows_done"), TT, TT)
        rows_sent = Signal(sem("rows_sent"), 16 * TT)
        unit_sent = Signal(sem("unit_sent"), 1, 1)

        CONSTS = 20

        block = st.enter_context(nc.Block())

        @block.sync
        def _(sp):
            for s in (rows_stored, scale_stored):
                sp.sem_inc(s.sem, s.credit)
            sp.dma_start(xt[0:S], x_chunk[0]).then_inc(xt_loaded.sem, 16)
            sp.dma_start(ctx_t[0:S], ctx_chunk[0]).then_inc(ctx_loaded.sem, 16)
            sp.dma_start(wq_raw, Wq.rearrange("(o p) i -> p o i", p=P)).then_inc(wq_loaded, 16)
            sp.dma_start(gates[:, 0:1], g_xattn.rearrange("(a b) -> a b", a=1).to_broadcast([P, 1])).then_inc(small_loaded, 16)
            sp.dma_start(gates[:, 1:2], g_ffn.rearrange("(a b) -> a b", a=1).to_broadcast([P, 1])).then_inc(small_loaded, 16)
            sp.dma_start(router[:], router_w.rearrange("(k p) e -> p k e", p=P)).then_inc(small_loaded, 16)
            sp.dma_start(wkv_raw, Wkv.rearrange("(r p) l -> p r l", p=P)).then_inc(wkv_loaded, 16)
            sp.dma_start(wo_raw, Wout.rearrange("(o p) i -> p o i", p=P)).then_inc(wo_loaded, 16)

            def load_chunk(c):
                sp.wait_ge(xn_done.sem, xn_done.after(c, 0))
                sp.dma_start(xt[0:S], x_chunk[bass.ds(c, 1)].rearrange("c s i d -> (c s) i d")).then_inc(xt_loaded.sem, 16)
                sp.wait_ge(cT_ready.sem, cT_ready.after(c, 0))
                sp.dma_start(ctx_t[0:S], ctx_chunk[bass.ds(c, 1)].rearrange("c s i d -> (c s) i d")).then_inc(ctx_loaded.sem, 16)

            def load_residual(c, i):
                sp.wait_ge(x1_done.sem, x1_done.after(c, i - 1))
                sp.dma_start(xr[0:S, i % 2, :], xf[bass.ds(c * CT + i * S, S), :]).then_inc(xr_loaded[i % 2].sem, 16)

            def store_x1(c):
                sp.wait_ge(x1_done.sem, x1_done.after(c, CB))
                sp.dma_start(x1_rows[bass.ds(c * CT, CT), 0:H].rearrange("(i s) d -> s i d", s=S), x1[0:S, :, 0:H]
                             ).then_inc(rows_stored.sem, 16)

            def store_x2(c):
                sp.wait_ge(x2_done.sem, x2_done.after(c, CB))
                sp.dma_start(x2_rows[bass.ds(c * CT, CT), :].rearrange("(i s) d -> s i d", s=S), x2[0:S]).then_inc(rows_stored.sem, 16)

            def store_scale(c):
                sp.wait_ge(slots_done.sem, slots_done.after(c, 1))
                sp.dma_start(x1_rows[bass.ds(c * CT, CT), H:XW].rearrange("(i s) d -> s i d", s=S), scale[0:S]
                             ).then_inc(scale_stored.sem, 16)

            def rows_of_chunk(c, load_next):
                for i in range(2, CB):
                    load_residual(c, i)
                if load_next:
                    load_chunk(c + 2)
                store_x1(c)
                for i in range(2):
                    load_residual(c + 1, i)
                store_x2(c)
                store_scale(c)

            load_chunk(1)
            for i in range(2):
                load_residual(0, i)
            with sp.Fori(0, NCH - 2) as c:
                rows_of_chunk(c, True)
            rows_of_chunk(NCH - 2, False)
            for i in range(2, CB):
                load_residual(NCH - 1, i)
            store_x1(NCH - 1)
            store_x2(NCH - 1)
            store_scale(NCH - 1)

            def load_step(e, u, j):
                s = j % 2
                src = [gate_w[bass.ds(e, 1), :, j * JW:(j + 1) * JW].rearrange("e (k p) n -> p (e k) n", p=P),
                       up_w[bass.ds(e, 1), :, j * JW:(j + 1) * JW].rearrange("e (k p) n -> p (e k) n", p=P),
                       down_w[bass.ds(e, 1), j * JW:(j + 1) * JW, :].rearrange("e (k p) n -> p (e k) n", p=P)]
                for w in range(3):
                    sp.wait_ge(w_lo[w].sem, w_lo[w].after(u, j - 1))
                    k = KC if w < 2 else JC
                    sp.dma_start(raw[:, s, w, :].rearrange("p (k n) -> p k n", k=k), src[w]).then_inc(raw_loaded[w][s].sem, 16)

            sp.wait_ge(s_ready.sem, s_ready.after(NCH, 0))
            for j in range(2):
                load_step(0, 0, j)
            sp.wait_ge(units_scattered, 16)
            sp.dma_start(units[:], unit_table.rearrange("(a u) w -> a (u w)", a=1)).then_inc(units_loaded, 16)
            for j in range(2, NJ):
                load_step(0, 0, j)
            sp.wait_ge(units_loaded, 16)
            sp.wait_ge(rows_known, 1)
            more = sp.value_load(more_units[0:1, 0:1], min_val=0, max_val=UNITS_MAX - E)
            with sp.Fori(1, more + E) as u:
                e = sp.value_load(units[0:1, bass.ds(u * 2, 1)], min_val=0, max_val=E - 1)
                for j in range(NJ):
                    load_step(e, u, j)

        @block.gpsimd
        def _(pool):
            nc.gpsimd.memset(ident[:], 0.0).then_inc(consts, 1)
            nc.gpsimd.memset(eye[:], 0.0).then_inc(consts, 1)
            nc.gpsimd.memset(mask[:], 0.0).then_inc(consts, 1)
            nc.gpsimd.memset(before[:], 1.0).then_inc(consts, 1)
            nc.gpsimd.memset(ones[:], 1.0).then_inc(consts, 1)
            nc.gpsimd.memset(earlier[:], 1.0).then_inc(consts, 1)
            nc.gpsimd.memset(empty[:], OUT_OF_BOUNDS).then_inc(consts, 1)
            pool.wait_ge(consts, 7)
            nc.gpsimd.affine_select(out=ident[:], in_=ident[:], compare_op=ALU.not_equal, fill=1.0, base=0,
                                    pattern=[[-1, P]], channel_multiplier=1).then_inc(consts, 1)
            nc.gpsimd.affine_select(out=eye[:], in_=eye[:], compare_op=ALU.not_equal, fill=1.0, base=0,
                                    pattern=[[-1, P]], channel_multiplier=1).then_inc(consts, 1)
            nc.gpsimd.affine_select(out=mask[:], in_=mask[:], compare_op=ALU.is_ge, fill=MASKED, base=0,
                                    pattern=[[-1, S]], channel_multiplier=1).then_inc(consts, 1)
            nc.gpsimd.affine_select(out=before[:], in_=before[:], compare_op=ALU.is_ge, fill=0.0, base=-1,
                                    pattern=[[1, S]], channel_multiplier=-1).then_inc(consts, 1)
            nc.gpsimd.affine_select(out=earlier[:], in_=earlier[:], compare_op=ALU.is_ge, fill=0.0, base=-1,
                                    pattern=[[-1, MORE]], channel_multiplier=1).then_inc(consts, 1)
            nc.gpsimd.iota(rev_e[:], [[-1, E]], base=E, channel_multiplier=0,
                           allow_small_or_imprecise_dtypes=True).then_inc(consts, 1)
            nc.gpsimd.iota(next_slot[:], [[SLOTS, E]], base=0, channel_multiplier=0,
                           allow_small_or_imprecise_dtypes=True).then_inc(consts, 1)
            nc.gpsimd.iota(thr[:], [[SLOTS, E], [CAP, BLOCKS - 1]], base=CAP, channel_multiplier=0,
                           allow_small_or_imprecise_dtypes=True).then_inc(consts, 1)
            nc.gpsimd.iota(tok_f[:], [[S, CB]], base=0, channel_multiplier=1,
                           allow_small_or_imprecise_dtypes=True).then_inc(consts, 1)
            nc.gpsimd.memset(x1[:], 0.0).then_inc(consts, 1)
            nc.gpsimd.memset(x2[:], 0.0).then_inc(consts, 1)
            nc.gpsimd.iota(first_rows[:, 0:1], [[0, 1]], base=0, channel_multiplier=1).then_inc(consts, 1)
            nc.gpsimd.iota(first_rows[:, 1:2], [[0, 1]], base=0, channel_multiplier=SLOTS).then_inc(consts, 1)
            pool.wait_ge(consts, CONSTS)
            nc.gpsimd.dma_start(token_table.rearrange("(p n) o -> p (n o)", p=P), empty[:]).then_inc(tok_scattered.sem, 16)
            nc.gpsimd.dma_start(unit_table[0:E, :], first_rows[:]).then_inc(tok_scattered.sem, 16)
            nc.gpsimd.dma_start(unit_table[E:UNITS_MAX, :], first_rows[0:UNITS_MAX - E, :]).then_inc(tok_scattered.sem, 16)
            for s in (xn_done, probs, unit_sent):
                pool.sem_inc(s.sem, s.credit)
            pool.wait_ge(tok_scattered.sem, tok_scattered.after(0, 0))

            def normalise(dst, src, ln, i):
                return nc.gpsimd.tensor_scalar(dst[0:S, i, :], src[0:S, i, 0:H], ln.rstd[0:S, i:i + 1],
                                               ln.shift[0:S, i:i + 1], ALU.mult, ALU.add)

            def normalise_tokens(c, i):
                if i == 0:
                    pool.wait_ge(ln1_ready.sem, ln1_ready.after(c, 1))
                    pool.sem_inc(wait_passed, 1)
                normalise(xn, xt, norm1, i).then_inc(xn_done.sem, 1)

            def scatter_tokens(c, i):
                if i == 0:
                    pool.wait_ge(slots_done.sem, slots_done.after(c, 1))
                    pool.sem_inc(wait_passed, 1)
                nc.gpsimd.indirect_dma_start(token_table, bass.IndirectOffsetOnAxis(ap=slot_i[0:S, i:i + 1], axis=0),
                                             tok_i[0:S, i:i + 1], None).then_inc(tok_scattered.sem, 16)

            def attend(c, first, last):
                for n in range(NT):
                    pool.wait_ge(inv_done.sem, inv_done.after(c, n + 1))
                    pool.wait_ge(pT_ready.sem, pT_ready.after(c, n + 1 - DEEP))
                    nc.gpsimd.tensor_tensor(pn[0:S, n % DEEP], pr[0:S, n % 2],
                                            inv[0:S, n % DEEP].unsqueeze(2).to_broadcast([S, HP, S]),
                                            ALU.mult).then_inc(probs.sem, 1)
                    if 8 <= n < 8 + CB and not last:
                        normalise_tokens(c + 1, n - 8)
                    if 12 <= n < 12 + CB and not first:
                        scatter_tokens(c - 1, n - 12)
                pool.wait_ge(ln2_ready.sem, ln2_ready.after(c, 1))
                pool.wait_ge(rows_stored.sem, rows_stored.after(c, 0))
                pool.sem_inc(wait_passed, 1)
                for i in range(CB):
                    normalise(x2, x1, norm2, i).then_inc(x2_done.sem, 1)

            for i in range(CB):
                normalise_tokens(0, i)
            pool.wait_ge(w_turned, 10)
            nc.gpsimd.memset(keys_b.rearrange("p m i j s -> p (m i j s)"), 0.0).then_inc(keys_zeroed, 1)
            attend(0, True, False)
            with pool.Fori(0, NCH - 2) as c:
                attend(c + 1, False, False)
            attend(NCH - 1, False, True)
            for i in range(CB):
                scatter_tokens(NCH - 1, i)

            pool.wait_ge(rows_known, 1)
            nc.gpsimd.indirect_dma_start(unit_table, bass.IndirectOffsetOnAxis(ap=u_slot[0:MORE, :], axis=0),
                                         unit_row[0:MORE, :], None, bounds_check=UNITS_MAX - 1,
                                         oob_is_err=False).then_inc(units_scattered, 16)
            pool.wait_ge(rows_stored.sem, rows_stored.after(NCH, 0))
            pool.wait_ge(scale_stored.sem, scale_stored.after(NCH, 0))
            pool.wait_ge(tok_scattered.sem, tok_scattered.after(NCH, 0))

            def gather_next(base, u):
                pool.wait_ge(g_lo_done.sem, g_lo_done.after(u, 0))
                nc.gpsimd.dma_start(idx_next[:], token_table[bass.ds(base, CAP), :].rearrange("(p t) o -> p (t o)", p=P)
                                    ).then_inc(idx_next_loaded.sem, 16)
                pool.wait_ge(idx_next_loaded.sem, idx_next_loaded.after(u, 16))
                pool.sem_inc(wait_passed, 1)
                for t in range(TT):
                    nc.gpsimd.indirect_dma_start(xg[:, t, :], None, x2_rows,
                                                 bass.IndirectOffsetOnAxis(ap=idx_next[:, t:t + 1], axis=0),
                                                 bounds_check=T - 1, oob_is_err=False).then_inc(xg_loaded.sem, 16)

            def gather_now(base, u):
                nc.gpsimd.dma_start(idx_now[:], token_table[bass.ds(base, CAP), :].rearrange("(p t) o -> p (t o)", p=P)
                                    ).then_inc(idx_now_loaded.sem, 16)
                pool.wait_ge(idx_now_loaded.sem, idx_now_loaded.after(u, 16))
                pool.sem_inc(wait_passed, 1)
                for t in range(TT):
                    nc.gpsimd.indirect_dma_start(x1g[:, t, :], None, x1_rows,
                                                 bass.IndirectOffsetOnAxis(ap=idx_now[:, t:t + 1], axis=0),
                                                 bounds_check=T - 1, oob_is_err=False).then_inc(x1g_loaded.sem, 16)

            def send_rows(u):
                for t in range(TT):
                    pool.wait_ge(rows_done.sem, rows_done.after(u, t + 1))
                    pool.sem_inc(wait_passed, 1)
                    nc.gpsimd.indirect_dma_start(of, bass.IndirectOffsetOnAxis(ap=idx_now[:, t:t + 1], axis=0),
                                                 rows[:, t, :], None, bounds_check=T - 1,
                                                 oob_is_err=False).then_inc(rows_sent.sem, 16)
                pool.wait_ge(rows_sent.sem, rows_sent.after(u, 16 * TT))
                pool.sem_inc(unit_sent.sem, 1)

            slot_max = E * SLOTS - CAP
            gather_next(0, 0)
            pool.wait_ge(units_loaded, 16)
            more = pool.value_load(more_units[0:1, 0:1], min_val=0, max_val=UNITS_MAX - E)
            with pool.Fori(0, more + (E - 1)) as u:
                base = pool.value_load(units[0:1, bass.ds(u * 2 + 3, 1)], min_val=0, max_val=slot_max)
                gather_next(base, u + 1)
                base = pool.value_load(units[0:1, bass.ds(u * 2 + 1, 1)], min_val=0, max_val=slot_max)
                gather_now(base, u)
                send_rows(u)
            base = pool.value_load(units[0:1, bass.ds(more * 2 + (2 * E - 1), 1)], min_val=0, max_val=slot_max)
            last = more + (E - 1)
            gather_now(base, last)
            send_rows(last)

        @block.scalar
        def _(act):
            def copy(dst, src):
                return nc.scalar.activation(dst, src, ACT.Copy)

            act.wait_ge(small_loaded, 48)
            nc.scalar.activation(tanh_x[:], gates[:, 0:1], ACT.Tanh).then_inc(tanh_done, 1)
            nc.scalar.activation(tanh_f[:], gates[:, 1:2], ACT.Tanh).then_inc(tanh_done, 1)
            for s in (exp_done, silu_done, h_hi_done):
                act.sem_inc(s.sem, s.credit)
            for n in range(10):
                act.wait_ge(w_turned, n + 1)
                dst = wq_hi[:, n, :] if n < KC else wkv_hi[:, (n - 4) * 512:(n - 3) * 512] if n < 6 else wo_hi[:, n - 6, :]
                copy(dst, banks[n % 8][:]).then_inc(w_hi_done, 1)

            def split_token(c, i):
                act.wait_ge(xT_ready.sem, xT_ready.after(c, i + 1))
                copy(x_hi[:, :, i * S:(i + 1) * S],
                     misc_b[:, 0:KC * S].rearrange("p (k s) -> p k s", k=KC)).then_inc(x_hi_done.sem, 1)

            def split_context(c):
                act.wait_ge(cT_ready.sem, cT_ready.after(c, 1))
                copy(c_hi[:], misc_b[:, 0:CT]).then_inc(c_hi_done.sem, 1)

            def keep_query(c, m):
                act.wait_ge(q_ready.sem, q_ready.after(c, m + 1))
                nc.scalar.activation(qT[:, m, :], score_b[(NT + KC + m) % DEEP][:, 0:CT], ACT.Copy, scale=SCALE).then_inc(q_done.sem, 1)

            def keep_keys(c, m):
                act.wait_ge(k_ready.sem, k_ready.after(c, m + 1))
                for j in range(HP):
                    r = slice(j * HD, (j + 1) * HD)
                    ins = copy(keys_b[r, m, :, j, :], score_b[(NT + m) % DEEP][r, 0:CT].rearrange("p (i s) -> p i s", i=CB))
                ins.then_inc(k_done.sem, 1)

            def keep_values(c, i):
                act.wait_ge(v_ready.sem, v_ready.after(c, i + 1))
                copy(v[0:S, i].rearrange("p h d -> p (h d)"), turn_b[i % 2][0:S, :]).then_inc(v_done.sem, 1)

            def split_output(c, i):
                act.wait_ge(o_ready.sem, o_ready.after(c, i + 1))
                act.wait_ge(y_ready.sem, y_ready.after(c, i))
                copy(ao_hi[:], out_b[i % 2][:, 0:KC * S].rearrange("p (k s) -> p k s", k=KC)).then_inc(ao_hi_done.sem, 1)

            def keep_normed(c, i):
                act.wait_ge(x2T_ready.sem, x2T_ready.after(c, i + 1))
                copy(x2T[:, :, i * S:(i + 1) * S],
                     misc_b[:, 0:KC * S].rearrange("p (k s) -> p k s", k=KC)).then_inc(x2T_copied.sem, 1)

            def exp_logits(c):
                act.wait_ge(logits_ready.sem, logits_ready.after(c, 1))
                nc.scalar.activation(ex_t[:], logits_p, ACT.Exp, scale=-1.0).then_inc(ex_t_done.sem, 1)

            def attend(c, first, last):
                for n in range(NT + 4):
                    if n < NT:
                        act.wait_ge(max_done.sem, max_done.after(c, n + 1))
                        act.wait_ge(probs.sem, probs.after(c, n - 2 + 1))
                        for h in range(HP):
                            ins = nc.scalar.activation(pr[0:S, n % 2, h, :], score_b[n % DEEP][0:S, h * S:(h + 1) * S], ACT.Exp,
                                                       bias=nmx[0:S, n % DEEP, h:h + 1],
                                                       accum_out=tot[0:S, n % DEEP, h:h + 1])
                        ins.then_inc(exp_done.sem, 1)
                    if n >= 7 and n % HP == 3:
                        split_output(c, n // HP - 1)
                    if 3 <= n < 3 + CB and not first:
                        keep_normed(c - 1, n - 3)
                    if n == 8 and not first:
                        exp_logits(c - 1)
                    if 12 <= n < 12 + CB and not last:
                        split_token(c + 1, n - 12)
                    if n == 12 + CB and not last:
                        split_context(c + 1)
                    if n == 1 + NT and not last:
                        for m in range(KC):
                            keep_keys(c + 1, m)
                if not last:
                    for m in range(KC):
                        keep_query(c + 1, m)
                    for i in range(CB):
                        keep_values(c + 1, i)

            for i in range(CB):
                split_token(0, i)
            split_context(0)
            act.wait_ge(keys_zeroed, 1)
            for m in range(KC):
                keep_keys(0, m)
            for m in range(KC):
                keep_query(0, m)
            for i in range(CB):
                keep_values(0, i)
            attend(0, True, False)
            with act.Fori(0, NCH - 2) as c:
                attend(c + 1, False, False)
            attend(NCH - 1, False, True)
            for i in range(CB):
                keep_normed(NCH - 1, i)
            exp_logits(NCH - 1)

            def split(u, j, w):
                s = j % 2
                act.wait_ge(raw_loaded[w][s].sem, raw_loaded[w][s].after(u, 16 * (j // 2 + 1)))
                if w < 2:
                    act.wait_ge(gu_ready.sem, gu_ready.after(u, j - 1))
                    dst = gu_hi[:, s, w]
                else:
                    act.wait_ge(dn_done.sem, dn_done.after(u, j - 1))
                    dst = dn_hi[:, s]
                copy(dst, raw[:, s, w, :].rearrange("p (k n) -> p k n", k=KC if w < 2 else JC)).then_inc(w_hi[w].sem, 1)

            def split_tokens(u):
                for t in range(TT):
                    act.wait_ge(gT_ready.sem, gT_ready.after(u, t + 1))
                    copy(x_hi[:, :, t * P:(t + 1) * P], xT_b[t][:].rearrange("p (k s) -> p k s", k=KC)
                         ).then_inc(g_hi_done.sem, 1)

            def step(u, j):
                act.wait_ge(gu_ready.sem, gu_ready.after(u, j + 1))
                act.wait_ge(h_done.sem, h_done.after(u, j))
                nc.scalar.activation(silu_g, gate_b[j % 2][:].rearrange("p (a n) -> p a n", a=2), ACT.Silu
                                     ).then_inc(silu_done.sem, 1)
                act.wait_ge(h_done.sem, h_done.after(u, j + 1))
                act.wait_ge(dn_done.sem, dn_done.after(u, j - 1))
                copy(h_hi[:, j % 2], h_f).then_inc(h_hi_done.sem, 1)
                split(u, j, 2)

            act.wait_ge(units_loaded, 16)
            more = act.value_load(more_units[0:1, 0:1], min_val=0, max_val=UNITS_MAX - E)
            for w in range(2):
                split(0, 0, w)
            split_tokens(0)
            for w in range(2):
                split(0, 1, w)
            step(0, 0)
            with act.Fori(0, more + (E - 1)) as u:
                for j in range(1, NJ):
                    for w in range(2):
                        split(*((u, j + 1) if j + 1 < NJ else (u + 1, 0)), w)
                    if j == NJ - 1:
                        act.wait_ge(gu_ready.sem, gu_ready.after(u, NJ))
                        split_tokens(u + 1)
                    step(u, j)
                for w in range(2):
                    split(u + 1, 1, w)
                step(u + 1, 0)
            last = more + (E - 1)
            for j in range(1, NJ):
                if j + 1 < NJ:
                    for w in range(2):
                        split(last, j + 1, w)
                step(last, j)

        @block.vector
        def _(dve):
            PER_CHUNK = 54
            chain = Chain(dve, dve_chain, PER_CHUNK)
            link = chain.link

            def lo_part(dst, src, hi):
                return nc.vector.tensor_tensor(dst, src, hi.bitcast(F32), ALU.subtract)

            def norm_step(ln, part):
                mean, var, nhv, tmp, rstd, shift = (t[0:S] for t in (ln.mean, ln.var, ln.nhv, ln.tmp, ln.rstd, ln.shift))
                even_mean, even_m2, odd_mean, odd_m2 = (ln.bn[0:S, :, k] for k in (1, 2, 4, 5))
                if part == 0:
                    nc.vector.tensor_tensor(mean, even_mean, odd_mean, ALU.add)
                    nc.vector.tensor_tensor(var, even_m2, odd_m2, ALU.add)
                    link(nc.vector.tensor_tensor(tmp, even_mean, odd_mean, ALU.subtract))
                elif part == 1:
                    link(nc.vector.scalar_tensor_tensor(out=tmp, in0=tmp, scalar=0.25, in1=tmp, op0=ALU.mult, op1=ALU.mult))
                elif part == 2:
                    link(nc.vector.scalar_tensor_tensor(out=var, in0=var, scalar=1.0 / H, in1=tmp, op0=ALU.mult, op1=ALU.add))
                elif part == 3:
                    link(nc.vector.tensor_scalar(var, var, EPS, None, ALU.add))
                elif part == 4:
                    nc.vector.tensor_scalar(nhv, var, -0.5, None, ALU.mult)
                    link(nc.vector.tensor_scalar(ln.half[0:S], var.bitcast(I32), 1, None, ALU.logical_shift_right))
                elif part == 5:
                    link(nc.vector.tensor_scalar(rstd.bitcast(I32), ln.half[0:S], -1.0, float(0x5F3759DF), ALU.mult, ALU.add))
                elif part < 15:
                    if part % 3 == 0:
                        link(nc.vector.tensor_tensor(tmp, rstd, rstd, ALU.mult))
                    elif part % 3 == 1:
                        link(nc.vector.tensor_tensor(tmp, tmp, nhv, ALU.mult))
                    else:
                        link(nc.vector.scalar_tensor_tensor(out=rstd, in0=tmp, scalar=1.5, in1=rstd, op0=ALU.add, op1=ALU.mult))
                else:
                    link(nc.vector.scalar_tensor_tensor(out=shift, in0=mean, scalar=-0.5, in1=rstd, op0=ALU.mult, op1=ALU.mult))

            NORM_STEPS = 16

            for s in (pT_copied, x1_done, rank_used, h_done, h_lo_done, g_lo_done, rows_done, *w_lo):
                dve.sem_inc(s.sem, s.credit)
            for n in range(10):
                dve.wait_ge(w_hi_done, n + 1)
                hi, lo = ((wq_hi[:, n, :], wq_lo[:, n, :]) if n < KC else
                          (wkv_hi[:, (n - 4) * 512:(n - 3) * 512], wkv_lo[:, (n - 4) * 512:(n - 3) * 512]) if n < 6 else
                          (wo_hi[:, n - 6, :], wo_lo[:, n - 6, :]))
                lo_part(lo, banks[n % 8][:], hi).then_inc(w_lo_done, 1)
            dve.wait_ge(consts, CONSTS)
            dve.wait_ge(tanh_done, 2)
            chain.begin(0, 0)
            link(nc.vector.tensor_tensor(picked[0:MORE], thr[0:MORE], ident[0:MORE, 0:MORE], ALU.mult))
            link(nc.vector.tensor_reduce(u_rank[0:MORE], picked[0:MORE], AX.X, ALU.add))
            link(nc.vector.tensor_copy(unit_row[0:MORE, 1:2], u_rank[0:MORE]))
            link(nc.vector.tensor_tensor(valid[0:MORE], ident[0:MORE, 0:MORE].rearrange("p (e k) -> p e k", e=E),
                                         rev_e[0:MORE].unsqueeze(2).to_broadcast([MORE, E, BLOCKS - 1]), ALU.mult))
            link(nc.vector.tensor_reduce(u_valid[0:MORE], valid[0:MORE].rearrange("p e k -> p (e k)"), AX.X, ALU.add))
            link(nc.vector.tensor_scalar(unit_row[0:MORE, 0:1], u_valid[0:MORE], -1.0, float(E), ALU.mult, ALU.add))

            def stats(c, i):
                if i == 0:
                    dve.wait_ge(xt_loaded.sem, xt_loaded.after(c, 16))
                    dve.wait_ge(xn_done.sem, xn_done.after(c, 0))
                link(nc.vector.bn_stats(norm1.bn[0:S, i, :], xt[0:S, i, :]))

            def split_token(c, i):
                dve.wait_ge(x_hi_done.sem, x_hi_done.after(c, i + 1))
                lo_part(x_lo[:, :, i * S:(i + 1) * S], misc_b[:, 0:KC * S].rearrange("p (k s) -> p k s", k=KC),
                        x_hi[:, :, i * S:(i + 1) * S]).then_inc(x_lo_done.sem, 1)

            def split_context(c):
                dve.wait_ge(c_hi_done.sem, c_hi_done.after(c, 1))
                lo_part(c_lo[:], misc_b[:, 0:CT], c_hi[:]).then_inc(c_lo_done.sem, 1)

            def residual(c, i):
                dve.wait_ge(y_ready.sem, y_ready.after(c, i + 1))
                dve.wait_ge(xr_loaded[i % 2].sem, xr_loaded[i % 2].after(c, 16 * (i // 2 + 1)))
                dve.wait_ge(rows_stored.sem, rows_stored.after(c, 0))
                nc.vector.scalar_tensor_tensor(out=x1[0:S, i, 0:H], in0=out_b[i % 2][0:S, :], scalar=tanh_x[0:S, 0:1],
                                               in1=xr[0:S, i % 2, :], op0=ALU.mult, op1=ALU.add).then_inc(x1_done.sem, 1)
                dve.wait_ge(x1_done.sem, x1_done.after(c, i + 1))
                link(nc.vector.bn_stats(norm2.bn[0:S, i, :], x1[0:S, i, 0:H]))

            def low_output(c, i):
                dve.wait_ge(ao_hi_done.sem, ao_hi_done.after(c, i + 1))
                lo_part(ao_lo[:], out_b[i % 2][:, 0:KC * S].rearrange("p (k s) -> p k s", k=KC), ao_hi[:]).then_inc(ao_lo_done.sem, 1)

            def choose(c):
                dve.wait_ge(ex_ready.sem, ex_ready.after(c, 1))
                link(nc.vector.tensor_scalar(ex[0:S], ex_p[0:S].rearrange("p (i e) -> p i e", e=E), 1.0, None, ALU.add))
                link(nc.vector.reciprocal(sig[0:S], ex[0:S]))
                link(nc.vector.tensor_reduce(prob[0:S], sig[0:S], AX.X, ALU.max))
                link(nc.vector.tensor_tensor(cand[0:S], sig[0:S], prob[0:S].unsqueeze(2).to_broadcast([S, CB, E]), ALU.is_equal))
                link(nc.vector.tensor_tensor(cand[0:S], cand[0:S], rev_e[0:S].unsqueeze(1).to_broadcast([S, CB, E]), ALU.mult))
                link(nc.vector.tensor_reduce(best[0:S], cand[0:S], AX.X, ALU.max))
                nc.vector.tensor_tensor(hot[0:S], cand[0:S], best[0:S].unsqueeze(2).to_broadcast([S, CB, E]), ALU.is_equal
                                        ).then_inc(hot_done.sem, 1)
                dve.wait_ge(scale_stored.sem, scale_stored.after(c, 0))
                link(nc.vector.tensor_scalar(scale[0:S], prob[0:S].unsqueeze(2).to_broadcast([S, CB, XW - H]), tanh_f[0:S, 0:1], None, ALU.mult))

            def place(c):
                dve.wait_ge(rank_ready.sem, rank_ready.after(c, 1))
                dve.wait_ge(tok_scattered.sem, tok_scattered.after(c, 0))
                link(nc.vector.tensor_tensor(pos[0:S], rank_p[0:S].rearrange("p (i e) -> p i e", e=E),
                                             next_slot[0:S].unsqueeze(1).to_broadcast([S, CB, E]), ALU.add))
                link(nc.vector.tensor_tensor(pos[0:S], pos[0:S], hot[0:S], ALU.mult))
                link(nc.vector.tensor_reduce(slot_f[0:S], pos[0:S], AX.X, ALU.add))
                link(nc.vector.tensor_copy(slot_i[0:S], slot_f[0:S]))
                link(nc.vector.tensor_copy(tok_i[0:S], tok_f[0:S]))
                link(nc.vector.tensor_scalar(tok_f[0:S], tok_f[0:S], float(CT), None, ALU.add))
                link(nc.vector.tensor_tensor(next_slot[0:S], next_slot[0:S], total_p[0:S], ALU.add))
                dve.sem_inc(slots_done.sem, 1)
                dve.sem_inc(rank_used.sem, 1)

            def attend(c, first, last):
                for n in range(NT + 7):
                    if n < NT:
                        b = n % DEEP
                        dve.wait_ge(s_ready.sem, s_ready.after(c, n + 1))
                        dve.wait_ge(exp_done.sem, exp_done.after(c, n + 1 - DEEP))
                        nc.vector.tensor_reduce(nmx[0:S, b], score_b[b][0:S, 0:HP * S].rearrange("p (h s) -> p h s", h=HP),
                                                AX.X, ALU.max, negate=True).then_inc(max_done.sem, 1)
                    if 1 <= n <= NT:
                        b = (n - 1) % DEEP
                        dve.wait_ge(exp_done.sem, exp_done.after(c, n))
                        dve.wait_ge(probs.sem, probs.after(c, n - DEEP))
                        nc.vector.reciprocal(inv[0:S, b], tot[0:S, b]).then_inc(inv_done.sem, 1)
                    if 2 <= n < NT + 2:
                        m = n - 2
                        dve.wait_ge(pT_ready.sem, pT_ready.after(c, m + 1))
                        dve.wait_ge(o_ready.sem, o_ready.after(c, (m - KEEP) // HP + 1 if m >= KEEP else 0))
                        nc.vector.tensor_copy(pT[0:S, m % KEEP], turn_b[m % 2][0:S, 0:HP * S].rearrange("p (h s) -> p h s", h=HP)
                                              ).then_inc(pT_copied.sem, 1)
                    if n >= 8 and n % HP == 0:
                        low_output(c, n // HP - 2)
                    if n >= 10 and n % HP == 2:
                        residual(c, n // HP - 2)
                    if n < CB and not last:
                        stats(c + 1, n)
                    elif n < CB + 4 and not last:
                        for part in range((n - CB) * 4, (n - CB) * 4 + 4):
                            norm_step(norm1, part)
                        if n == CB + 3:
                            dve.sem_inc(ln1_ready.sem, 1)
                    if n == 9 and not first:
                        choose(c - 1)
                    if n == 11 and not first:
                        place(c - 1)
                    if 12 <= n < 12 + CB and not last:
                        split_token(c + 1, n - 12)
                    if n == 12 + CB and not last:
                        split_context(c + 1)
                for part in range(NORM_STEPS):
                    norm_step(norm2, part)
                dve.sem_inc(ln2_ready.sem, 1)

            for i in range(CB):
                stats(0, i)
            for part in range(NORM_STEPS):
                norm_step(norm1, part)
            dve.sem_inc(ln1_ready.sem, 1)
            for i in range(CB):
                split_token(0, i)
            split_context(0)
            attend(0, True, False)
            done = chain.count - PER_CHUNK
            with dve.Fori(0, NCH - 2) as c:
                chain.begin(c + 1, done)
                attend(c + 1, False, False)
                assert chain.count == PER_CHUNK, chain.count
            chain.begin(NCH - 1, done)
            attend(NCH - 1, False, True)
            choose(NCH - 1)
            place(NCH - 1)

            link(nc.vector.tensor_tensor(valid[0:MORE], next_slot[0:MORE].unsqueeze(2).to_broadcast([MORE, E, BLOCKS - 1]),
                                         thr[0:MORE].rearrange("p (e k) -> p e k", e=E), ALU.is_gt))
            vflat = valid[0:MORE].rearrange("p e k -> p (e k)")
            link(nc.vector.tensor_reduce(u_count[0:MORE], vflat, AX.X, ALU.add))
            link(nc.vector.tensor_copy(more_units[0:MORE], u_count[0:MORE]))
            link(nc.vector.tensor_tensor(picked[0:MORE], vflat, earlier[0:MORE], ALU.mult))
            link(nc.vector.tensor_reduce(u_rank[0:MORE], picked[0:MORE], AX.X, ALU.add))
            link(nc.vector.tensor_tensor(picked[0:MORE], vflat, ident[0:MORE, 0:MORE], ALU.mult))
            link(nc.vector.tensor_reduce(u_valid[0:MORE], picked[0:MORE], AX.X, ALU.add))
            link(nc.vector.tensor_scalar(u_valid[0:MORE], u_valid[0:MORE], -float(OUT_OF_BOUNDS), float(E + OUT_OF_BOUNDS),
                                         ALU.mult, ALU.add))
            link(nc.vector.tensor_tensor(u_rank[0:MORE], u_rank[0:MORE], u_valid[0:MORE], ALU.add))
            nc.vector.tensor_copy(u_slot[0:MORE], u_rank[0:MORE]).then_inc(rows_known, 1)

            def split(u, j, w):
                s = j % 2
                dve.wait_ge(w_hi[w].sem, w_hi[w].after(u, j + 1))
                hi, lo = (gu_hi[:, s, w], gu_lo[:, s, w]) if w < 2 else (dn_hi[:, s], dn_lo[:, s])
                lo_part(lo, raw[:, s, w, :].rearrange("p (k n) -> p k n", k=KC if w < 2 else JC), hi).then_inc(w_lo[w].sem, 1)

            def split_tokens(u):
                for t in range(TT):
                    dve.wait_ge(g_hi_done.sem, g_hi_done.after(u, t + 1))
                    lo_part(x_lo[:, :, t * P:(t + 1) * P], xT_b[t][:].rearrange("p (k s) -> p k s", k=KC),
                            x_hi[:, :, t * P:(t + 1) * P]).then_inc(g_lo_done.sem, 1)

            def step(u, j):
                dve.wait_ge(silu_done.sem, silu_done.after(u, j + 1))
                dve.wait_ge(h_hi_done.sem, h_hi_done.after(u, j))
                dve.wait_ge(h_lo_done.sem, h_lo_done.after(u, j))
                nc.vector.tensor_tensor(h_f, silu_g, up_b[j % 2][:].rearrange("p (a n) -> p a n", a=2), ALU.mult
                                        ).then_inc(h_done.sem, 1)
                dve.wait_ge(h_hi_done.sem, h_hi_done.after(u, j + 1))
                lo_part(h_lo[:, j % 2], h_f, h_hi[:, j % 2]).then_inc(h_lo_done.sem, 1)
                split(u, j, 2)

            def finish(u):
                dve.wait_ge(dn_done.sem, dn_done.after(u, NJ))
                dve.wait_ge(x1g_loaded.sem, x1g_loaded.after(u, 16 * TT))
                dve.wait_ge(unit_sent.sem, unit_sent.after(u, 0))
                for t in range(TT):
                    nc.vector.scalar_tensor_tensor(out=rows[:, t, :], in0=y_b[t][:], scalar=x1g[:, t, H:H + 1],
                                                   in1=x1g[:, t, 0:H], op0=ALU.mult, op1=ALU.add).then_inc(rows_done.sem, 1)

            dve.wait_ge(units_loaded, 16)
            more = dve.value_load(more_units[0:1, 0:1], min_val=0, max_val=UNITS_MAX - E)
            for w in range(2):
                split(0, 0, w)
            split_tokens(0)
            for w in range(2):
                split(0, 1, w)
            step(0, 0)
            with dve.Fori(0, more + (E - 1)) as u:
                for j in range(1, NJ):
                    for w in range(2):
                        split(*((u, j + 1) if j + 1 < NJ else (u + 1, 0)), w)
                    if j == NJ - 1:
                        split_tokens(u + 1)
                    step(u, j)
                for w in range(2):
                    split(u + 1, 1, w)
                step(u + 1, 0)
                finish(u)
            last = more + (E - 1)
            for j in range(1, NJ):
                if j + 1 < NJ:
                    for w in range(2):
                        split(last, j + 1, w)
                step(last, j)
            finish(last)

        @block.tensor
        def _(pe):
            def three(dst, a, b, first, last):
                nc.tensor.matmul(dst, a[0], b[0], start=first, stop=False)
                nc.tensor.matmul(dst, a[0], b[1], start=False, stop=False)
                return nc.tensor.matmul(dst, a[1], b[0], start=False, stop=last)

            for s in (cT_ready, pT_ready, o_ready, y_ready, gu_ready, dn_done):
                pe.sem_inc(s.sem, s.credit)
            pe.wait_ge(consts, CONSTS)
            for n in range(10):
                pe.wait_ge(wq_loaded if n < 4 else wkv_loaded if n < 6 else wo_loaded, 16)
                if n >= 8:
                    pe.wait_ge(w_lo_done, n - 7)
                for o in range(4):
                    src = (wq_raw[:, o, n * P:(n + 1) * P] if n < 4 else wkv_raw[:, (n - 4) * 4 + o, :] if n < 6 else
                           wo_raw[:, o, (n - 6) * P:(n - 5) * P])
                    ins = nc.tensor.transpose(banks[n % 8][:, o * P:(o + 1) * P], src, ident[:])
                ins.then_inc(w_turned, 1)
            pe.wait_ge(w_lo_done, 10)
            pe.wait_ge(small_loaded, 48)

            def turn_chunk(c, i, first):
                pe.wait_ge(xn_done.sem, xn_done.after(c, i + 1))
                if i == 0 and not first:
                    pe.wait_ge(rank_used.sem, rank_used.after(c - 1, 0))
                if i:
                    pe.wait_ge(x_lo_done.sem, x_lo_done.after(c, i))
                for k in range(KC):
                    ins = nc.tensor.transpose(misc_b[:, k * S:(k + 1) * S], xn[0:S, i, k * P:(k + 1) * P], ident[0:S, 0:S])
                ins.then_inc(xT_ready.sem, 1)

            def turn_context(c):
                pe.wait_ge(ctx_loaded.sem, ctx_loaded.after(c, 16))
                pe.wait_ge(x_lo_done.sem, x_lo_done.after(c, CB))
                for i in range(CB):
                    ins = nc.tensor.transpose(misc_b[:, i * S:(i + 1) * S], ctx_t[0:S, i, :], ident[0:S, 0:S])
                ins.then_inc(cT_ready.sem, 1)

            def keys(c, m):
                if m == 0:
                    pe.wait_ge(c_lo_done.sem, c_lo_done.after(c, 1))
                if m < DEEP:
                    pe.wait_ge(exp_done.sem, exp_done.after(c - 1, NT + m - DEEP + 1))
                else:
                    pe.wait_ge(k_done.sem, k_done.after(c, m - DEEP + 1))
                three(score_b[(NT + m) % DEEP][:, 0:CT], (wkv_hi[:, m * P:(m + 1) * P], wkv_lo[:, m * P:(m + 1) * P]),
                      (c_hi[:], c_lo[:]), True, True).then_inc(k_ready.sem, 1)

            def queries(c, m):
                if m == 0:
                    pe.wait_ge(x_lo_done.sem, x_lo_done.after(c, CB))
                if m < DEEP:
                    pe.wait_ge(k_done.sem, k_done.after(c, KC + m - DEEP + 1))
                else:
                    pe.wait_ge(q_done.sem, q_done.after(c, m - DEEP + 1))
                for k in range(KC):
                    ins = three(score_b[(NT + KC + m) % DEEP][:, 0:CT],
                                (wq_hi[:, k, m * P:(m + 1) * P], wq_lo[:, k, m * P:(m + 1) * P]),
                                (x_hi[:, k, :], x_lo[:, k, :]), k == 0, k == KC - 1)
                ins.then_inc(q_ready.sem, 1)

            def values(c, i):
                if i < 2:
                    pe.wait_ge(pT_copied.sem, pT_copied.after(c, 0))
                else:
                    pe.wait_ge(v_done.sem, v_done.after(c, i - 1))
                r = slice(i * S, (i + 1) * S)
                three(turn_b[i % 2][0:S, :], (c_hi[:, r], c_lo[:, r]), (wkv_hi[:, H:2 * H], wkv_lo[:, H:2 * H]),
                      True, True).then_inc(v_ready.sem, 1)

            def scores(c, n):
                i, m, b = n // KC, n % KC, n % DEEP
                if n == 0:
                    pe.wait_ge(q_done.sem, q_done.after(c, KC))
                if n >= DEEP:
                    pe.wait_ge(exp_done.sem, exp_done.after(c, n - DEEP + 1))
                nc.tensor.matmul(score_b[b][0:S, 0:HP * S], eye[0:S, 0:S], mask[0:S].unsqueeze(1).to_broadcast([S, HP, S]),
                                 start=True, stop=False)
                nc.tensor.matmul(score_b[b][0:S, 0:HP * S], qT[:, m, i * S:(i + 1) * S],
                                 keys_b[:, m, i].rearrange("p j s -> p (j s)"), start=False, stop=True).then_inc(s_ready.sem, 1)

            def turn_probs(c, n):
                pe.wait_ge(probs.sem, probs.after(c, n + 1))
                if n < 2:
                    pe.wait_ge(v_done.sem, v_done.after(c, CB))
                else:
                    pe.wait_ge(pT_copied.sem, pT_copied.after(c, n - 1))
                for h in range(HP):
                    ins = nc.tensor.transpose(turn_b[n % 2][0:S, h * S:(h + 1) * S], pn[0:S, n % DEEP, h, :], ident[0:S, 0:S])
                ins.then_inc(pT_ready.sem, 1)

            def weigh(c, i):
                pe.wait_ge(pT_copied.sem, pT_copied.after(c, HP * (i + 1)))
                pe.wait_ge(x1_done.sem, x1_done.after(c, i - 1))
                for m in range(KC):
                    for j in range(HP):
                        ins = nc.tensor.matmul(out_b[i % 2][j * HD:(j + 1) * HD, m * S:(m + 1) * S], v[0:S, i, m * HP + j, :],
                                               pT[0:S, (i * KC + m) % KEEP, j, :], start=True, stop=True,
                                               tile_position=(0, j * HD))
                ins.then_inc(o_ready.sem, 1)

            def project(c, i):
                pe.wait_ge(ao_lo_done.sem, ao_lo_done.after(c, i + 1))
                for k in range(KC):
                    ins = three(out_b[i % 2][0:S, :], (ao_hi[:, k, :], ao_lo[:, k, :]), (wo_hi[:, k, :], wo_lo[:, k, :]),
                                k == 0, k == KC - 1)
                ins.then_inc(y_ready.sem, 1)

            def turn_normed(c, i, last):
                pe.wait_ge(x2_done.sem, x2_done.after(c, i + 1))
                if i:
                    pe.wait_ge(x2T_copied.sem, x2T_copied.after(c, i))
                elif last:
                    pe.wait_ge(rank_used.sem, rank_used.after(c, 0))
                else:
                    pe.wait_ge(c_lo_done.sem, c_lo_done.after(c + 1, 1))
                for k in range(KC):
                    ins = nc.tensor.transpose(misc_b[:, k * S:(k + 1) * S], x2[0:S, i, k * P:(k + 1) * P], ident[0:S, 0:S])
                ins.then_inc(x2T_ready.sem, 1)

            def route(c):
                pe.wait_ge(x2T_copied.sem, x2T_copied.after(c, CB))
                for k in range(KC):
                    ins = nc.tensor.matmul(logits_p, router[:, k, :], x2T[:, k, :], start=k == 0, stop=k == KC - 1)
                ins.then_inc(logits_ready.sem, 1)

            def turn_logits(c):
                pe.wait_ge(ex_t_done.sem, ex_t_done.after(c, 1))
                pe.sem_inc(pe_wait_passed, 1)
                for i in range(CB):
                    ins = nc.tensor.transpose(ex_p[0:S, i * E:(i + 1) * E], ex_t[:, i * S:(i + 1) * S], ident[0:E, 0:E])
                ins.then_inc(ex_ready.sem, 1)

            def rank(c):
                pe.wait_ge(hot_done.sem, hot_done.after(c, 1))
                nc.tensor.matmul(rank_p[0:S, :], before[0:S, :], hot[0:S].rearrange("p i e -> p (i e)"),
                                 start=True, stop=False, skip_group_check=True)
                for i in range(CB - 1):
                    later = CB - 1 - i
                    nc.tensor.matmul(rank_p[0:S, (i + 1) * E:CB * E], ones[0:S, :],
                                     hot[0:S, i:i + 1, :].to_broadcast([S, later, E]), start=False, stop=False,
                                     skip_group_check=True)
                for i in range(CB):
                    ins = nc.tensor.matmul(total_p[0:S, :], ones[0:S, :], hot[0:S, i, :], start=False,
                                           stop=i == CB - 1, skip_group_check=True)
                ins.then_inc(rank_ready.sem, 1)

            def attend(c, first, last):
                for n in range(DEEP):
                    scores(c, n)
                for n in range(NT + 4):
                    if n + DEEP < NT:
                        scores(c, n + DEEP)
                    if n < NT:
                        turn_probs(c, n)
                    if n >= 5 and n % HP == 1:
                        weigh(c, n // HP - 1)
                    if n >= 7 and n % HP == 3:
                        project(c, n // HP - 1)
                    if 1 <= n < 1 + CB and not first:
                        turn_normed(c - 1, n - 1, False)
                    if n == 5 and not first:
                        route(c - 1)
                    if n == 7 and not first:
                        turn_logits(c - 1)
                    if n == 8 and not first:
                        rank(c - 1)
                    if 10 <= n < 10 + CB and not last:
                        turn_chunk(c + 1, n - 10, False)
                    if n == 10 + CB and not last:
                        turn_context(c + 1)
                    if n == 11 + CB and not last:
                        for m in range(KC):
                            keys(c + 1, m)
                    if n >= NT and not last:
                        queries(c + 1, n - NT)
                if not last:
                    for i in range(CB):
                        values(c + 1, i)

            for i in range(CB):
                turn_chunk(0, i, True)
            turn_context(0)
            for m in range(KC):
                keys(0, m)
            for m in range(KC):
                queries(0, m)
            for i in range(CB):
                values(0, i)
            attend(0, True, False)
            with pe.Fori(0, NCH - 2) as c:
                attend(c + 1, False, False)
            attend(NCH - 1, False, True)
            for i in range(CB):
                turn_normed(NCH - 1, i, True)
            route(NCH - 1)
            turn_logits(NCH - 1)
            rank(NCH - 1)

            def turn_tokens(u):
                pe.wait_ge(xg_loaded.sem, xg_loaded.after(u, 16 * TT))
                pe.wait_ge(g_lo_done.sem, g_lo_done.after(u, 0))
                for t in range(TT):
                    for k in range(KC):
                        ins = nc.tensor.transpose(xT_b[t][:, k * P:(k + 1) * P], xg[:, t, k * P:(k + 1) * P], ident[:])
                    ins.then_inc(gT_ready.sem, 1)

            def gate_up(u, j):
                s = j % 2
                if j == 0:
                    pe.wait_ge(g_lo_done.sem, g_lo_done.after(u, TT))
                for w, bank in ((0, gate_b[s]), (1, up_b[s])):
                    pe.wait_ge(w_lo[w].sem, w_lo[w].after(u, j + 1))
                    if w == 0:
                        pe.wait_ge(silu_done.sem, silu_done.after(u, j - 1))
                    else:
                        pe.wait_ge(h_done.sem, h_done.after(u, j - 1))
                    for m in range(JC):
                        for k in range(KC):
                            r = slice(m * P, (m + 1) * P)
                            ins = three(bank[:, m * CAP:(m + 1) * CAP], (gu_hi[:, s, w, k, r], gu_lo[:, s, w, k, r]),
                                        (x_hi[:, k, 0:CAP], x_lo[:, k, 0:CAP]), k == 0, k == KC - 1)
                ins.then_inc(gu_ready.sem, 1)

            def down(u, j):
                s = j % 2
                pe.wait_ge(w_lo[2].sem, w_lo[2].after(u, j + 1))
                pe.wait_ge(h_lo_done.sem, h_lo_done.after(u, j + 1))
                if j == 0:
                    pe.wait_ge(rows_done.sem, rows_done.after(u, 0))
                for t in range(TT):
                    for k in range(JC):
                        r = slice(t * P, (t + 1) * P)
                        ins = three(y_b[t][:], (h_hi[:, s, k, r], h_lo[:, s, k, r]), (dn_hi[:, s, k, :], dn_lo[:, s, k, :]),
                                    j == 0 and k == 0, j == NJ - 1 and k == JC - 1)
                ins.then_inc(dn_done.sem, 1)

            pe.wait_ge(units_loaded, 16)
            more = pe.value_load(more_units[0:1, 0:1], min_val=0, max_val=UNITS_MAX - E)
            turn_tokens(0)
            gate_up(0, 0)
            with pe.Fori(0, more + (E - 1)) as u:
                gate_up(u, 1)
                down(u, 0)
                gate_up(u, 2)
                down(u, 1)
                turn_tokens(u + 1)
                gate_up(u, 3)
                down(u, 2)
                gate_up(u + 1, 0)
                down(u, 3)
            last = more + (E - 1)
            gate_up(last, 1)
            down(last, 0)
            gate_up(last, 2)
            down(last, 1)
            gate_up(last, 3)
            down(last, 2)
            down(last, 3)


_INS = ["x", "ctx_512", "g_xattn", "g_ffn", "L0_xattn_Wq", "L0_xattn_Wkv_expand", "L0_xattn_Wout", "L0_ffn_router_w",
        "L0_ffn_gate_w", "L0_ffn_up_w", "L0_ffn_down_w"]


def kernel(**inputs):
    import numpy as np
    import concourse.bacc as bacc
    from concourse.bass_utils import run_bass_kernel_spmd

    nc = bacc.Bacc("TRN2", target_bir_lowering=False, num_devices=1)
    arrays, args = {}, []
    for name in _INS:
        a = np.ascontiguousarray(inputs[name])
        arrays[f"in_{name}"] = a
        args.append(nc.dram_tensor(f"in_{name}", a.shape, mybir.dt.from_np(a.dtype), kind="ExternalInput").ap())
    out = nc.dram_tensor("out_x", inputs["x"].shape, F32, kind="ExternalOutput").ap()
    flamingo_block(nc, *args, out)
    r = run_bass_kernel_spmd(nc, [arrays], core_ids=[0])
    return r.results[0]["out_x"]
```

```python
from contextlib import ExitStack

import concourse.bass as bass
from concourse import mybir

F32 = mybir.dt.float32
F32R = mybir.dt.float32r
BF16 = mybir.dt.bfloat16
I32 = mybir.dt.int32
ALU = mybir.AluOpType
ACT = mybir.ActivationFunctionType
AX = mybir.AxisListType

P = 128
BANK = 512
EPS = 1e-5
MASKED = -3.0e38
OUT_OF_BOUNDS = 1 << 20


class Signal:

    def __init__(self, sem, per, credit=0):
        self.sem, self.per, self.credit = sem, per, credit

    def after(self, turn, count):
        return turn * self.per + (self.credit + count)


class Chain:

    def __init__(self, eng, sem, per):
        self.eng, self.sem, self.per = eng, sem, per
        self.turn, self.base, self.count = 0, 0, 0

    def begin(self, turn, base):
        self.turn, self.base, self.count = turn, base, 0

    def link(self, ins):
        ins.then_inc(self.sem, 1)
        self.count += 1
        self.eng.wait_ge(self.sem, self.turn * self.per + (self.base + self.count))


def flamingo_block(nc, x, ctx, g_xattn, g_ffn, Wq, Wkv, Wout, router_w, gate_w, up_w, down_w, out):
    B, S, H = x.shape
    L = ctx.shape[2]
    E, _, I = gate_w.shape
    HD = 32
    NH = H // HD
    T = B * S
    KC = H // P
    CB = 4
    NCH = B // CB
    CT = CB * S
    HP = P // HD
    NT = CB * KC
    SCALE = HD ** -0.5
    CAP = 256
    TT = CAP // P
    BLOCKS = -(-T // CAP)
    SLOTS = BLOCKS * CAP
    MORE = E * (BLOCKS - 1)
    UNITS_MAX = E + (T - E) // CAP
    NJ = 4
    JW = I // NJ
    JC = JW // P
    DEEP = 3
    KEEP = HP + 2
    XW = H + 8
    assert L == P and H == KC * P and CB * S <= BANK and JW * KC == JC * H == 1024

    xf = x.rearrange("b s d -> (b s) d")
    x_chunk = x.rearrange("(c i) s d -> c s i d", i=CB)
    ctx_chunk = ctx[:, 0:S, :].rearrange("(c i) s d -> c s i d", i=CB)
    of = out.rearrange("b s d -> (b s) d")

    x1_rows = nc.dram_tensor("x1_rows", [T, XW], F32, kind="Internal").ap()
    x2_rows = nc.dram_tensor("x2_rows", [T, H], F32, kind="Internal").ap()
    token_table = nc.dram_tensor("token_table", [E * SLOTS, 1], I32, kind="Internal").ap()
    unit_table = nc.dram_tensor("unit_table", [UNITS_MAX, 2], I32, kind="Internal").ap()

    st = ExitStack()
    with st:
        def sb(name, shape, dt):
            return st.enter_context(nc.sbuf_tensor(name, shape, dt))

        def sem(name):
            return st.enter_context(nc.semaphore(name))

        ident = sb("ident", [P, P], F32)
        eye = sb("eye", [P, P], BF16)
        mask = sb("mask", [P, S], BF16)
        before = sb("before", [P, S], BF16)
        ones = sb("ones", [P, S], BF16)
        rev_e = sb("rev_e", [P, E], F32)
        tanh_x = sb("tanh_x", [P, 1], F32)
        tanh_f = sb("tanh_f", [P, 1], F32)
        gates = sb("gates", [P, 2], F32)
        thr = sb("thr", [P, MORE], F32)
        earlier = sb("earlier", [P, MORE], F32)
        unit_row = sb("unit_row", [P, 2], I32)
        first_rows = sb("first_rows", [E, 2], I32)
        empty = sb("empty", [P, E * SLOTS // P], I32)

        wq_hi = sb("wq_hi", [P, KC, H], F32R)
        wq_lo = sb("wq_lo", [P, KC, H], F32R)
        wo_hi = sb("wo_hi", [P, KC, H], F32R)
        wo_lo = sb("wo_lo", [P, KC, H], F32R)
        wkv_hi = sb("wkv_hi", [P, 2 * H], F32R)
        wkv_lo = sb("wkv_lo", [P, 2 * H], F32R)
        router = sb("router", [P, KC, E], F32)

        xt = sb("xt", [P, CB, H], F32)
        xn = sb("xn", [P, CB, H], F32)
        x_hi = sb("x_hi", [P, KC, CT], F32R)
        x_lo = sb("x_lo", [P, KC, CT], F32R)
        ctx_t = sb("ctx_t", [P, CB, L], F32)
        c_hi = sb("c_hi", [P, CT], F32R)
        c_lo = sb("c_lo", [P, CT], F32R)
        qT = sb("qT", [P, KC, CT], F32)
        v = sb("v", [P, CB, NH, HD], F32)
        pr = sb("pr", [P, 2, HP, S], F32)
        pn = sb("pn", [P, DEEP, HP, S], F32)
        pT = sb("pT", [P, KEEP, HP, S], F32)
        nmx = sb("nmx", [P, DEEP, HP], F32)
        tot = sb("tot", [P, DEEP, HP], F32)
        inv = sb("inv", [P, DEEP, HP], F32)
        ao_hi = sb("ao_hi", [P, KC, S], F32R)
        ao_lo = sb("ao_lo", [P, KC, S], F32R)
        xr = sb("xr", [P, 2, H], F32)
        x1 = sb("x1", [P, CB, XW], F32)
        x2 = sb("x2", [P, CB, H], F32)
        x2T = sb("x2T", [P, KC, CT], F32)

        class NormBuffers:

            def __init__(self, name):
                self.bn = sb(f"{name}_bn", [P, CB, 6], F32)
                self.half = sb(f"{name}_half", [P, CB], I32)
                self.mean, self.var, self.nhv, self.tmp, self.rstd, self.shift = (
                    sb(f"{name}_{k}", [P, CB], F32) for k in ("mean", "var", "nhv", "tmp", "rstd", "shift"))

        norm1, norm2 = NormBuffers("norm1"), NormBuffers("norm2")

        ex_t = sb("ex_t", [E, CT], F32)
        ex = sb("ex", [P, CB, E], F32)
        sig = sb("sig", [P, CB, E], F32)
        cand = sb("cand", [P, CB, E], F32)
        prob = sb("prob", [P, CB], F32)
        scale = sb("scale", [P, CB, XW - H], F32)
        best = sb("best", [P, CB], F32)
        hot = sb("hot", [P, CB, E], BF16)
        pos = sb("pos", [P, CB, E], F32)
        slot_f = sb("slot_f", [P, CB], F32)
        slot_i = sb("slot_i", [P, CB], I32)
        next_slot = sb("next_slot", [P, E], F32)
        tok_f = sb("tok_f", [P, CB], F32)
        tok_i = sb("tok_i", [P, CB], I32)
        valid = sb("valid", [P, E, BLOCKS - 1], F32)
        picked = sb("picked", [P, MORE], F32)
        u_rank = sb("u_rank", [P, 1], F32)
        u_valid = sb("u_valid", [P, 1], F32)
        u_slot = sb("u_slot", [P, 1], I32)
        u_count = sb("u_count", [P, 1], F32)
        more_units = sb("more_units", [P, 1], I32)
        units = sb("units", [1, 2 * UNITS_MAX], I32)

        staging = sb("staging", [P, max(2 * 3 * 1024, KC * CB * HP * S)], F32)
        raw = staging[:, 0:2 * 3 * 1024].rearrange("p (s w n) -> p s w n", s=2, w=3)
        keys_b = staging[:, 0:KC * CB * HP * S].rearrange("p (m i j s) -> p m i j s", m=KC, i=CB, j=HP)
        gu_hi = sb("gu_hi", [P, 2, 2, KC, JW], F32R)
        gu_lo = sb("gu_lo", [P, 2, 2, KC, JW], F32R)
        idx_next = sb("idx_next", [P, TT], I32)
        idx_now = sb("idx_now", [P, TT], I32)
        dn_hi, dn_lo = (w[:].rearrange("p (s k) n -> p s k n", s=2) for w in (wq_hi, wq_lo))
        h_hi, h_lo = (w[:].rearrange("p (s k n) -> p s k n", s=2, k=JC) for w in (wkv_hi, wkv_lo))
        xg = x2
        x1g = x1
        rows = xn
        silu_g = qT[:, 2:4, 0:JC * CAP // 2]
        h_f = qT[:, 0:2, 0:JC * CAP // 2]
        wq_raw = raw[:, 0, 0:2, :].rearrange("p a b -> p (a b)").rearrange("p (o i) -> p o i", o=KC)
        wo_raw = x2[:]
        wkv_raw = raw[:, 0, 2, :].rearrange("p (r l) -> p r l", l=L)

        banks = [st.enter_context(nc.psum_tensor(f"bank{i}", [P, BANK], F32)) for i in range(8)]
        score_b, turn_b, out_b, misc_b = banks[0:3], banks[3:5], banks[5:7], banks[7]
        class Part:

            def __init__(self, number, first, stop, bank):
                self.number, self.first, self.stop, self.count = number, first, stop, stop - first
                self.batches, self.tokens = slice(first, stop), slice(first * S, stop * S)
                self.logits = bank[0:E, self.tokens]
                ex_p, rank_p, self.total = (bank[0:S, CT + k * CB * E:CT + k * CB * E + w]
                                            for k, w in ((0, CB * E), (1, CB * E), (2, E)))
                self.ex_b = [ex_p[:, i * E:(i + 1) * E] for i in range(CB)]
                self.ex = ex_p[:, first * E:stop * E].rearrange("p (i e) -> p i e", e=E)
                self.rank_from = [rank_p[:, i * E:stop * E] for i in range(stop)]
                self.rank = self.rank_from[first].rearrange("p (i e) -> p i e", e=E)

        whole = Part(0, 0, CB, misc_b)
        last_parts = Part(0, 0, CB - 1, misc_b), Part(1, CB - 1, CB, turn_b[1])
        weight_b = banks[0:6] + banks[6:8] + banks[4:6]
        first_token_b, first_context_b = banks[6:8] + banks[4:6], banks[3]
        token_b = misc_b, out_b[1], misc_b, out_b[1]
        last_row_b = banks[0:4]
        gate_b, up_b, y_b, xT_b = banks[0:2], banks[2:4], banks[4:6], banks[6:8]

        wq_loaded, wo_loaded, wkv_loaded = sem("wq_loaded"), sem("wo_loaded"), sem("wkv_loaded")
        small_loaded = sem("small_loaded")
        consts = sem("consts")
        tanh_done = sem("tanh_done")
        x1_cleared = sem("x1_cleared")
        w_turned, w_hi_done, w_lo_done = sem("w_turned"), sem("w_hi_done"), sem("w_lo_done")

        xt_loaded = Signal(sem("xt_loaded"), 16)
        ctx_loaded = Signal(sem("ctx_loaded"), 16)
        xr_loaded = [Signal(sem(f"xr_loaded{i}"), 16 * CB // 2) for i in range(2)]
        ln1_ready = Signal(sem("ln1_ready"), 1)
        xn_done = Signal(sem("xn_done"), CB, CB)
        xT_ready = Signal(sem("xT_ready"), CB)
        x_hi_done = Signal(sem("x_hi_done"), CB)
        x_lo_done = Signal(sem("x_lo_done"), CB)
        cT_ready = Signal(sem("cT_ready"), 1, 1)
        c_hi_done = Signal(sem("c_hi_done"), 1)
        c_lo_done = Signal(sem("c_lo_done"), 1)
        kq_ready = Signal(sem("kq_ready"), 2 * KC)
        kq_done = Signal(sem("kq_done"), 2 * KC)
        keys_zeroed = sem("keys_zeroed")
        v_ready = Signal(sem("v_ready"), CB)
        v_done = Signal(sem("v_done"), CB)
        s_ready = Signal(sem("s_ready"), NT)
        max_done = Signal(sem("max_done"), NT)
        exp_done = Signal(sem("exp_done"), NT, DEEP)
        inv_done = Signal(sem("inv_done"), NT)
        probs = Signal(sem("probs"), NT, DEEP)
        pT_ready = Signal(sem("pT_ready"), NT, DEEP)
        pT_copied = Signal(sem("pT_copied"), NT, NT)
        o_ready = Signal(sem("o_ready"), CB, 1)
        ao_hi_done = Signal(sem("ao_hi_done"), CB)
        ao_lo_done = Signal(sem("ao_lo_done"), CB)
        y_ready = Signal(sem("y_ready"), CB, 1)
        x1_done = Signal(sem("x1_done"), CB, 2)
        ln2_ready = Signal(sem("ln2_ready"), 1)
        x2_done = Signal(sem("x2_done"), CB)
        x2T_ready = Signal(sem("x2T_ready"), CB)
        x2T_copied = Signal(sem("x2T_copied"), CB)
        logits_ready = Signal(sem("logits_ready"), 1)
        ex_t_done = Signal(sem("ex_t_done"), 1)
        ex_ready = Signal(sem("ex_ready"), 1)
        hot_done = Signal(sem("hot_done"), 1)
        rank_ready = Signal(sem("rank_ready"), 1)
        rank_used = Signal(sem("rank_used"), 1, 2)
        slots_done = Signal(sem("slots_done"), 1)
        rows_stored = Signal(sem("rows_stored"), 32, 16)
        tok_scattered = Signal(sem("tok_scattered"), 16 * (CB + 1), 16 * 3)
        dve_chain = sem("dve_chain")

        rows_known = sem("rows_known")
        wait_passed, pe_wait_passed = sem("wait_passed"), sem("pe_wait_passed")
        units_scattered = sem("units_scattered")
        units_loaded = sem("units_loaded")
        raw_loaded = [[Signal(sem(f"raw_loaded{w}_{s}"), 16 * NJ // 2) for s in range(2)] for w in range(3)]
        w_hi = [Signal(sem(f"w_hi{w}"), NJ) for w in range(3)]
        w_lo = [Signal(sem(f"w_lo{w}"), NJ, 2) for w in range(3)]
        gu_ready = Signal(sem("gu_ready"), NJ, 2)
        dn_done = Signal(sem("dn_done"), NJ, 2)
        silu_done = Signal(sem("silu_done"), NJ, 2)
        h_done = Signal(sem("h_done"), NJ, 2)
        h_hi_done = Signal(sem("h_hi_done"), NJ, 1)
        h_lo_done = Signal(sem("h_lo_done"), NJ, 1)
        idx_next_loaded = Signal(sem("idx_next_loaded"), 16)
        idx_now_loaded = Signal(sem("idx_now_loaded"), 16)
        xg_loaded = Signal(sem("xg_loaded"), 16 * TT)
        x1g_loaded = Signal(sem("x1g_loaded"), 16 * TT)
        gT_ready = Signal(sem("gT_ready"), TT)
        g_hi_done = Signal(sem("g_hi_done"), TT)
        g_lo_done = Signal(sem("g_lo_done"), TT, TT)
        rows_done = Signal(sem("rows_done"), TT, TT)
        rows_sent = Signal(sem("rows_sent"), 16 * TT)
        unit_sent = Signal(sem("unit_sent"), 1, 1)

        CONSTS = 18

        block = st.enter_context(nc.Block())

        @block.sync
        def _(sp):
            sp.sem_inc(rows_stored.sem, rows_stored.credit)
            sp.dma_start(xt[0:S], x_chunk[0]).then_inc(xt_loaded.sem, 16)
            sp.dma_start(ctx_t[0:S], ctx_chunk[0]).then_inc(ctx_loaded.sem, 16)
            sp.dma_start(wq_raw, Wq.rearrange("(o p) i -> p o i", p=P)).then_inc(wq_loaded, 16)
            sp.dma_start(gates[:, 0:1], g_xattn.rearrange("(a b) -> a b", a=1).to_broadcast([P, 1])).then_inc(small_loaded, 16)
            sp.dma_start(gates[:, 1:2], g_ffn.rearrange("(a b) -> a b", a=1).to_broadcast([P, 1])).then_inc(small_loaded, 16)
            sp.dma_start(router[:], router_w.rearrange("(k p) e -> p k e", p=P)).then_inc(small_loaded, 16)
            sp.dma_start(wkv_raw, Wkv.rearrange("(r p) l -> p r l", p=P)).then_inc(wkv_loaded, 16)
            sp.dma_start(wo_raw, Wout.rearrange("(o p) i -> p o i", p=P)).then_inc(wo_loaded, 16)

            def load_chunk(c):
                sp.wait_ge(xn_done.sem, xn_done.after(c, 0))
                sp.dma_start(xt[0:S], x_chunk[bass.ds(c, 1)].rearrange("c s i d -> (c s) i d")).then_inc(xt_loaded.sem, 16)
                sp.wait_ge(cT_ready.sem, cT_ready.after(c, 0))
                sp.dma_start(ctx_t[0:S], ctx_chunk[bass.ds(c, 1)].rearrange("c s i d -> (c s) i d")).then_inc(ctx_loaded.sem, 16)

            def load_residual(c, i):
                sp.wait_ge(x1_done.sem, x1_done.after(c, i - 1))
                sp.dma_start(xr[0:S, i % 2, :], xf[bass.ds(c * CT + i * S, S), :]).then_inc(xr_loaded[i % 2].sem, 16)

            def store_x1(c):
                sp.wait_ge(x1_done.sem, x1_done.after(c, CB))
                sp.dma_start(x1_rows[bass.ds(c * CT, CT), 0:H].rearrange("(i s) d -> s i d", s=S), x1[0:S, :, 0:H]
                             ).then_inc(rows_stored.sem, 16)

            def store_x2(c):
                sp.wait_ge(x2_done.sem, x2_done.after(c, CB))
                sp.dma_start(x2_rows[bass.ds(c * CT, CT), :].rearrange("(i s) d -> s i d", s=S), x2[0:S]).then_inc(rows_stored.sem, 16)

            def rows_of_chunk(c, load_next):
                for i in range(2, CB):
                    load_residual(c, i)
                if load_next:
                    load_chunk(c + 2)
                store_x1(c)
                for i in range(2):
                    load_residual(c + 1, i)
                store_x2(c)

            load_chunk(1)
            for i in range(2):
                load_residual(0, i)
            with sp.Fori(0, NCH - 2) as c:
                rows_of_chunk(c, True)
            rows_of_chunk(NCH - 2, False)
            for i in range(2, CB):
                load_residual(NCH - 1, i)
            def load_step(e, u, j):
                s = j % 2
                src = [gate_w[bass.ds(e, 1), :, j * JW:(j + 1) * JW].rearrange("e (k p) n -> p (e k) n", p=P),
                       up_w[bass.ds(e, 1), :, j * JW:(j + 1) * JW].rearrange("e (k p) n -> p (e k) n", p=P),
                       down_w[bass.ds(e, 1), j * JW:(j + 1) * JW, :].rearrange("e (k p) n -> p (e k) n", p=P)]
                for w in range(3):
                    sp.wait_ge(w_lo[w].sem, w_lo[w].after(u, j - 1))
                    k = KC if w < 2 else JC
                    sp.dma_start(raw[:, s, w, :].rearrange("p (k n) -> p k n", k=k), src[w]).then_inc(raw_loaded[w][s].sem, 16)

            sp.wait_ge(s_ready.sem, s_ready.after(NCH, 0))
            for j in range(2):
                load_step(0, 0, j)
            store_x1(NCH - 1)
            store_x2(NCH - 1)
            for j in range(2, NJ):
                load_step(0, 0, j)
            sp.wait_ge(units_loaded, 16)
            sp.wait_ge(rows_known, 1)
            more = sp.value_load(more_units[0:1, 0:1], min_val=0, max_val=UNITS_MAX - E)
            with sp.Fori(1, more + E) as u:
                e = sp.value_load(units[0:1, bass.ds(u * 2, 1)], min_val=0, max_val=E - 1)
                for j in range(NJ):
                    load_step(e, u, j)

        @block.gpsimd
        def _(pool):
            for s in (xn_done, probs, unit_sent):
                pool.sem_inc(s.sem, s.credit)
            nc.gpsimd.memset(ident[:], 0.0).then_inc(consts, 1)
            nc.gpsimd.memset(eye[:], 0.0).then_inc(consts, 1)
            nc.gpsimd.memset(mask[:], 0.0).then_inc(consts, 1)
            nc.gpsimd.memset(before[:], 1.0).then_inc(consts, 1)
            nc.gpsimd.memset(ones[:], 1.0).then_inc(consts, 1)
            nc.gpsimd.memset(earlier[:], 1.0).then_inc(consts, 1)
            nc.gpsimd.memset(empty[:], OUT_OF_BOUNDS).then_inc(consts, 1)
            pool.wait_ge(consts, 7)
            nc.gpsimd.affine_select(out=ident[:], in_=ident[:], compare_op=ALU.not_equal, fill=1.0, base=0,
                                    pattern=[[-1, P]], channel_multiplier=1).then_inc(consts, 1)
            nc.gpsimd.affine_select(out=eye[:], in_=eye[:], compare_op=ALU.not_equal, fill=1.0, base=0,
                                    pattern=[[-1, P]], channel_multiplier=1).then_inc(consts, 1)
            nc.gpsimd.affine_select(out=mask[:], in_=mask[:], compare_op=ALU.is_ge, fill=MASKED, base=0,
                                    pattern=[[-1, S]], channel_multiplier=1).then_inc(consts, 1)
            nc.gpsimd.affine_select(out=before[:], in_=before[:], compare_op=ALU.is_ge, fill=0.0, base=-1,
                                    pattern=[[1, S]], channel_multiplier=-1).then_inc(consts, 1)
            nc.gpsimd.affine_select(out=earlier[:], in_=earlier[:], compare_op=ALU.is_ge, fill=0.0, base=-1,
                                    pattern=[[-1, MORE]], channel_multiplier=1).then_inc(consts, 1)
            nc.gpsimd.iota(rev_e[:], [[-1, E]], base=E, channel_multiplier=0,
                           allow_small_or_imprecise_dtypes=True).then_inc(consts, 1)
            nc.gpsimd.iota(next_slot[:], [[SLOTS, E]], base=0, channel_multiplier=0,
                           allow_small_or_imprecise_dtypes=True).then_inc(consts, 1)
            nc.gpsimd.iota(thr[:], [[SLOTS, E], [CAP, BLOCKS - 1]], base=CAP, channel_multiplier=0,
                           allow_small_or_imprecise_dtypes=True).then_inc(consts, 1)
            nc.gpsimd.iota(tok_f[:], [[S, CB]], base=0, channel_multiplier=1,
                           allow_small_or_imprecise_dtypes=True).then_inc(consts, 1)
            nc.gpsimd.iota(first_rows[:, 0:1], [[0, 1]], base=0, channel_multiplier=1).then_inc(consts, 1)
            nc.gpsimd.iota(first_rows[:, 1:2], [[0, 1]], base=0, channel_multiplier=SLOTS).then_inc(consts, 1)
            pool.wait_ge(consts, CONSTS)
            nc.gpsimd.memset(staging[:, 3 * 1024:], 0.0).then_inc(keys_zeroed, 1)
            nc.gpsimd.dma_start(token_table.rearrange("(p n) o -> p (n o)", p=P), empty[:]).then_inc(tok_scattered.sem, 16)
            nc.gpsimd.dma_start(unit_table[0:E, :], first_rows[:]).then_inc(tok_scattered.sem, 16)
            nc.gpsimd.dma_start(unit_table[E:UNITS_MAX, :], first_rows[0:UNITS_MAX - E, :]).then_inc(tok_scattered.sem, 16)
            def normalise(dst, src, ln, i):
                return nc.gpsimd.tensor_scalar(dst[0:S, i, :], src[0:S, i, 0:H], ln.rstd[0:S, i:i + 1],
                                               ln.shift[0:S, i:i + 1], ALU.mult, ALU.add)

            def normalise_tokens(c, i):
                if i == 0:
                    pool.wait_ge(ln1_ready.sem, ln1_ready.after(c, 1))
                    pool.sem_inc(wait_passed, 1)
                normalise(xn, xt, norm1, i).then_inc(xn_done.sem, 1)

            def normalise_rows(c, i):
                if i == 0:
                    pool.wait_ge(ln2_ready.sem, ln2_ready.after(c, 1))
                    pool.wait_ge(rows_stored.sem, rows_stored.after(c, 0))
                    pool.sem_inc(wait_passed, 1)
                normalise(x2, x1, norm2, i).then_inc(x2_done.sem, 1)

            def scatter_tokens(c, part):
                pool.wait_ge(slots_done.sem, slots_done.after(c, part.number + 1))
                pool.sem_inc(wait_passed, 1)
                for i in range(part.first, part.stop):
                    nc.gpsimd.indirect_dma_start(token_table, bass.IndirectOffsetOnAxis(ap=slot_i[0:S, i:i + 1], axis=0),
                                                 tok_i[0:S, i:i + 1], None).then_inc(tok_scattered.sem, 16)

            def store_scale(c):
                nc.gpsimd.dma_start(x1_rows[bass.ds(c * CT, CT), H:XW].rearrange("(i s) d -> s i d", s=S), scale[0:S]
                                    ).then_inc(tok_scattered.sem, 16)

            def attend(c, first, last):
                if not last:
                    for i in range(CB):
                        normalise_tokens(c + 1, i)
                for n in range(NT):
                    pool.wait_ge(inv_done.sem, inv_done.after(c, n + 1))
                    pool.wait_ge(pT_ready.sem, pT_ready.after(c, n + 1 - DEEP))
                    nc.gpsimd.tensor_tensor(pn[0:S, n % DEEP], pr[0:S, n % 2],
                                            inv[0:S, n % DEEP].unsqueeze(2).to_broadcast([S, HP, S]),
                                            ALU.mult).then_inc(probs.sem, 1)
                    if 4 <= n < 4 + CB and not first:
                        normalise_rows(c - 1, n - 4)
                if not first:
                    scatter_tokens(c - 1, whole)
                    store_scale(c - 1)

            for i in range(CB):
                normalise_tokens(0, i)
            pool.wait_ge(w_turned, 6)
            nc.gpsimd.memset(staging[:, 0:3 * 1024], 0.0).then_inc(keys_zeroed, 1)
            nc.gpsimd.memset(x1[:], 0.0).then_inc(x1_cleared, 1)
            pool.wait_ge(tok_scattered.sem, tok_scattered.after(0, 0))
            attend(0, True, False)
            with pool.Fori(0, NCH - 2) as c:
                attend(c + 1, False, False)
            attend(NCH - 1, False, True)
            for part in last_parts:
                scatter_tokens(NCH - 1, part)

            pool.wait_ge(rows_stored.sem, rows_stored.after(NCH, 0))
            pool.wait_ge(tok_scattered.sem, tok_scattered.after(NCH - 1, 16 * CB))

            def gather_next(base, u):
                pool.wait_ge(g_lo_done.sem, g_lo_done.after(u, 0))
                nc.gpsimd.dma_start(idx_next[:], token_table[bass.ds(base, CAP), :].rearrange("(p t) o -> p (t o)", p=P)
                                    ).then_inc(idx_next_loaded.sem, 16)
                pool.wait_ge(idx_next_loaded.sem, idx_next_loaded.after(u, 16))
                pool.sem_inc(wait_passed, 1)
                for t in range(TT):
                    nc.gpsimd.indirect_dma_start(xg[:, t, :], None, x2_rows,
                                                 bass.IndirectOffsetOnAxis(ap=idx_next[:, t:t + 1], axis=0),
                                                 bounds_check=T - 1, oob_is_err=False).then_inc(xg_loaded.sem, 16)

            def gather_now(base, u):
                nc.gpsimd.dma_start(idx_now[:], token_table[bass.ds(base, CAP), :].rearrange("(p t) o -> p (t o)", p=P)
                                    ).then_inc(idx_now_loaded.sem, 16)
                pool.wait_ge(idx_now_loaded.sem, idx_now_loaded.after(u, 16))
                pool.sem_inc(wait_passed, 1)
                for t in range(TT):
                    nc.gpsimd.indirect_dma_start(x1g[:, t, :], None, x1_rows,
                                                 bass.IndirectOffsetOnAxis(ap=idx_now[:, t:t + 1], axis=0),
                                                 bounds_check=T - 1, oob_is_err=False).then_inc(x1g_loaded.sem, 16)

            def send_rows(u):
                for t in range(TT):
                    pool.wait_ge(rows_done.sem, rows_done.after(u, t + 1))
                    pool.sem_inc(wait_passed, 1)
                    nc.gpsimd.indirect_dma_start(of, bass.IndirectOffsetOnAxis(ap=idx_now[:, t:t + 1], axis=0),
                                                 rows[:, t, :], None, bounds_check=T - 1,
                                                 oob_is_err=False).then_inc(rows_sent.sem, 16)

            def wait_sent(u):
                pool.wait_ge(rows_sent.sem, rows_sent.after(u, 16 * TT))
                pool.sem_inc(unit_sent.sem, 1)

            def first_slot(u):
                return pool.value_load(units[0:1, bass.ds(u * 2 + 1, 1)], min_val=0, max_val=slot_max)

            slot_max = E * SLOTS - CAP
            gather_next(0, 0)
            store_scale(NCH - 1)
            pool.wait_ge(rows_known, 1)
            nc.gpsimd.indirect_dma_start(unit_table, bass.IndirectOffsetOnAxis(ap=u_slot[0:MORE, :], axis=0),
                                         unit_row[0:MORE, :], None, bounds_check=UNITS_MAX - 1,
                                         oob_is_err=False).then_inc(units_scattered, 16)
            pool.wait_ge(units_scattered, 16)
            nc.gpsimd.dma_start(units[:], unit_table.rearrange("(a u) w -> a (u w)", a=1)).then_inc(units_loaded, 16)
            pool.wait_ge(tok_scattered.sem, tok_scattered.after(NCH, 0))
            pool.wait_ge(units_loaded, 16)
            more = pool.value_load(more_units[0:1, 0:1], min_val=0, max_val=UNITS_MAX - E)
            gather_next(first_slot(1), 1)
            gather_now(0, 0)
            with pool.Fori(0, more + (E - 2)) as u:
                send_rows(u)
                gather_next(first_slot(u + 2), u + 2)
                wait_sent(u)
                gather_now(first_slot(u + 1), u + 1)
            last = more + (E - 1)
            send_rows(last - 1)
            wait_sent(last - 1)
            gather_now(first_slot(last), last)
            send_rows(last)
            wait_sent(last)

        @block.scalar
        def _(act):
            def copy(dst, src):
                return nc.scalar.activation(dst, src, ACT.Copy)

            for s in (exp_done, silu_done, h_hi_done):
                act.sem_inc(s.sem, s.credit)
            def split_weights(n):
                act.wait_ge(w_turned, n + 1)
                dst = wq_hi[:, n, :] if n < KC else wkv_hi[:, (n - 4) * 512:(n - 3) * 512] if n < 6 else wo_hi[:, n - 6, :]
                copy(dst, weight_b[n][:]).then_inc(w_hi_done, 1)

            def split_token(c, i, bank):
                act.wait_ge(xT_ready.sem, xT_ready.after(c, i + 1))
                copy(x_hi[:, :, i * S:(i + 1) * S],
                     bank[:, 0:KC * S].rearrange("p (k s) -> p k s", k=KC)).then_inc(x_hi_done.sem, 1)

            def split_context(c, bank=misc_b):
                act.wait_ge(cT_ready.sem, cT_ready.after(c, 1))
                copy(c_hi[:], bank[:, 0:CT]).then_inc(c_hi_done.sem, 1)

            def keep(c, t):
                act.wait_ge(kq_ready.sem, kq_ready.after(c, t + 1))
                m, bank = t // 2, score_b[(NT + t) % DEEP]
                if t % 2 == 0:
                    for j in range(HP):
                        r = slice(j * HD, (j + 1) * HD)
                        ins = copy(keys_b[r, m, :, j, :], bank[r, 0:CT].rearrange("p (i s) -> p i s", i=CB))
                else:
                    ins = nc.scalar.activation(qT[:, m, :], bank[:, 0:CT], ACT.Copy, scale=SCALE)
                ins.then_inc(kq_done.sem, 1)

            def keep_values(c, i):
                act.wait_ge(v_ready.sem, v_ready.after(c, i + 1))
                copy(v[0:S, i].rearrange("p h d -> p (h d)"), turn_b[i % 2][0:S, :]).then_inc(v_done.sem, 1)

            def split_output(c, i):
                act.wait_ge(o_ready.sem, o_ready.after(c, i + 1))
                act.wait_ge(y_ready.sem, y_ready.after(c, i))
                copy(ao_hi[:], out_b[i % 2][:, 0:KC * S].rearrange("p (k s) -> p k s", k=KC)).then_inc(ao_hi_done.sem, 1)

            def keep_normed(c, i, bank=misc_b):
                act.wait_ge(x2T_ready.sem, x2T_ready.after(c, i + 1))
                copy(x2T[:, :, i * S:(i + 1) * S],
                     bank[:, 0:KC * S].rearrange("p (k s) -> p k s", k=KC)).then_inc(x2T_copied.sem, 1)

            def exp_logits(c, part):
                act.wait_ge(logits_ready.sem, logits_ready.after(c, part.number + 1))
                nc.scalar.activation(ex_t[:, part.tokens], part.logits, ACT.Exp, scale=-1.0).then_inc(ex_t_done.sem, 1)

            def attend(c, first, last):
                for n in range(NT + 1):
                    if n < NT:
                        act.wait_ge(max_done.sem, max_done.after(c, n + 1))
                        act.wait_ge(probs.sem, probs.after(c, n - 2 + 1))
                        for h in range(HP):
                            ins = nc.scalar.activation(pr[0:S, n % 2, h, :], score_b[n % DEEP][0:S, h * S:(h + 1) * S], ACT.Exp,
                                                       bias=nmx[0:S, n % DEEP, h:h + 1],
                                                       accum_out=tot[0:S, n % DEEP, h:h + 1])
                        ins.then_inc(exp_done.sem, 1)
                    if n < CB - 1:
                        keep_values(c, n + 1)
                    if n >= 8 and n % HP == 0:
                        split_output(c, n // HP - 2)
                    if 2 <= n < 2 + CB and not last:
                        split_token(c + 1, n - 2, token_b[n - 2])
                    if n == 2 + CB and not last:
                        split_context(c + 1)
                    if 8 <= n < 8 + CB and not first:
                        keep_normed(c - 1, n - 8)
                    if n == 14 and not first:
                        exp_logits(c - 1, whole)
                for t in range(2 * KC):
                    if t == KC:
                        split_output(c, CB - 1)
                    if not last:
                        keep(c + 1, t)
                if not last:
                    keep_values(c + 1, 0)

            def split(u, j, w):
                s = j % 2
                act.wait_ge(raw_loaded[w][s].sem, raw_loaded[w][s].after(u, 16 * (j // 2 + 1)))
                if w < 2:
                    act.wait_ge(gu_ready.sem, gu_ready.after(u, j - 1))
                    dst = gu_hi[:, s, w]
                else:
                    act.wait_ge(dn_done.sem, dn_done.after(u, j - 1))
                    dst = dn_hi[:, s]
                copy(dst, raw[:, s, w, :].rearrange("p (k n) -> p k n", k=KC if w < 2 else JC)).then_inc(w_hi[w].sem, 1)

            for n in range(6):
                split_weights(n)
            for i in range(CB):
                split_token(0, i, first_token_b[i])
            split_context(0, first_context_b)
            act.wait_ge(small_loaded, 48)
            nc.scalar.activation(tanh_x[:], gates[:, 0:1], ACT.Tanh).then_inc(tanh_done, 1)
            nc.scalar.activation(tanh_f[:], gates[:, 1:2], ACT.Tanh).then_inc(tanh_done, 1)
            act.wait_ge(keys_zeroed, 2)
            for t in range(2 * KC):
                keep(0, t)
                if t == 3:
                    for n in range(6, 10):
                        split_weights(n)
            keep_values(0, 0)
            attend(0, True, False)
            with act.Fori(0, NCH - 2) as c:
                attend(c + 1, False, False)
            attend(NCH - 1, False, True)
            for w in range(2):
                split(0, 0, w)
            for part in last_parts:
                for i in range(part.first, part.stop):
                    keep_normed(NCH - 1, i, last_row_b[i])
                exp_logits(NCH - 1, part)
            for w in range(2):
                split(0, 1, w)


            def split_tokens(u):
                for t in range(TT):
                    act.wait_ge(gT_ready.sem, gT_ready.after(u, t + 1))
                    copy(x_hi[:, :, t * P:(t + 1) * P], xT_b[t][:].rearrange("p (k s) -> p k s", k=KC)
                         ).then_inc(g_hi_done.sem, 1)

            def step(u, j):
                act.wait_ge(gu_ready.sem, gu_ready.after(u, j + 1))
                act.wait_ge(h_done.sem, h_done.after(u, j))
                nc.scalar.activation(silu_g, gate_b[j % 2][:].rearrange("p (a n) -> p a n", a=2), ACT.Silu
                                     ).then_inc(silu_done.sem, 1)
                act.wait_ge(h_done.sem, h_done.after(u, j + 1))
                act.wait_ge(dn_done.sem, dn_done.after(u, j - 1))
                copy(h_hi[:, j % 2], h_f).then_inc(h_hi_done.sem, 1)
                split(u, j, 2)

            split_tokens(0)
            step(0, 0)
            act.wait_ge(units_loaded, 16)
            more = act.value_load(more_units[0:1, 0:1], min_val=0, max_val=UNITS_MAX - E)
            with act.Fori(0, more + (E - 1)) as u:
                for j in range(1, NJ):
                    for w in range(2):
                        split(*((u, j + 1) if j + 1 < NJ else (u + 1, 0)), w)
                    if j == NJ - 1:
                        act.wait_ge(gu_ready.sem, gu_ready.after(u, NJ))
                        split_tokens(u + 1)
                    step(u, j)
                for w in range(2):
                    split(u + 1, 1, w)
                step(u + 1, 0)
            last = more + (E - 1)
            for j in range(1, NJ):
                if j + 1 < NJ:
                    for w in range(2):
                        split(last, j + 1, w)
                step(last, j)

        @block.vector
        def _(dve):
            PER_CHUNK = 54
            chain = Chain(dve, dve_chain, PER_CHUNK)
            link = chain.link

            def lo_part(dst, src, hi):
                return nc.vector.tensor_tensor(dst, src, hi.bitcast(F32), ALU.subtract)

            def norm_step(ln, part, b=slice(0, CB)):
                mean, var, nhv, tmp, rstd, shift = (t[0:S, b] for t in (ln.mean, ln.var, ln.nhv, ln.tmp, ln.rstd, ln.shift))
                even_mean, even_m2, odd_mean, odd_m2 = (ln.bn[0:S, b, k] for k in (1, 2, 4, 5))
                if part == 0:
                    nc.vector.tensor_tensor(mean, even_mean, odd_mean, ALU.add)
                    nc.vector.tensor_tensor(var, even_m2, odd_m2, ALU.add)
                    link(nc.vector.tensor_tensor(tmp, even_mean, odd_mean, ALU.subtract))
                elif part == 1:
                    link(nc.vector.scalar_tensor_tensor(out=tmp, in0=tmp, scalar=0.25, in1=tmp, op0=ALU.mult, op1=ALU.mult))
                elif part == 2:
                    link(nc.vector.scalar_tensor_tensor(out=var, in0=var, scalar=1.0 / H, in1=tmp, op0=ALU.mult, op1=ALU.add))
                elif part == 3:
                    link(nc.vector.tensor_scalar(var, var, EPS, None, ALU.add))
                elif part == 4:
                    nc.vector.tensor_scalar(nhv, var, -0.5, None, ALU.mult)
                    link(nc.vector.tensor_scalar(ln.half[0:S, b], var.bitcast(I32), 1, None, ALU.logical_shift_right))
                elif part == 5:
                    link(nc.vector.tensor_scalar(rstd.bitcast(I32), ln.half[0:S, b], -1.0, float(0x5F3759DF), ALU.mult, ALU.add))
                elif part < 15:
                    if part % 3 == 0:
                        link(nc.vector.tensor_tensor(tmp, rstd, rstd, ALU.mult))
                    elif part % 3 == 1:
                        link(nc.vector.tensor_tensor(tmp, tmp, nhv, ALU.mult))
                    else:
                        link(nc.vector.scalar_tensor_tensor(out=rstd, in0=tmp, scalar=1.5, in1=rstd, op0=ALU.add, op1=ALU.mult))
                else:
                    link(nc.vector.scalar_tensor_tensor(out=shift, in0=mean, scalar=-0.5, in1=rstd, op0=ALU.mult, op1=ALU.mult))

            NORM_STEPS = 16

            for s in (pT_copied, x1_done, rank_used, h_done, h_lo_done, g_lo_done, rows_done, *w_lo):
                dve.sem_inc(s.sem, s.credit)
            def split_weights(n):
                dve.wait_ge(w_hi_done, n + 1)
                hi, lo = ((wq_hi[:, n, :], wq_lo[:, n, :]) if n < KC else
                          (wkv_hi[:, (n - 4) * 512:(n - 3) * 512], wkv_lo[:, (n - 4) * 512:(n - 3) * 512]) if n < 6 else
                          (wo_hi[:, n - 6, :], wo_lo[:, n - 6, :]))
                lo_part(lo, weight_b[n][:], hi).then_inc(w_lo_done, 1)

            def stats(c, i):
                if i == 0:
                    dve.wait_ge(xt_loaded.sem, xt_loaded.after(c, 16))
                    dve.wait_ge(xn_done.sem, xn_done.after(c, 0))
                link(nc.vector.bn_stats(norm1.bn[0:S, i, :], xt[0:S, i, :]))

            def split_token(c, i, bank):
                dve.wait_ge(x_hi_done.sem, x_hi_done.after(c, i + 1))
                lo_part(x_lo[:, :, i * S:(i + 1) * S], bank[:, 0:KC * S].rearrange("p (k s) -> p k s", k=KC),
                        x_hi[:, :, i * S:(i + 1) * S]).then_inc(x_lo_done.sem, 1)

            def split_context(c, bank=misc_b):
                dve.wait_ge(c_hi_done.sem, c_hi_done.after(c, 1))
                lo_part(c_lo[:], bank[:, 0:CT], c_hi[:]).then_inc(c_lo_done.sem, 1)

            def residual(c, i):
                dve.wait_ge(y_ready.sem, y_ready.after(c, i + 1))
                dve.wait_ge(xr_loaded[i % 2].sem, xr_loaded[i % 2].after(c, 16 * (i // 2 + 1)))
                dve.wait_ge(rows_stored.sem, rows_stored.after(c, 0))
                nc.vector.scalar_tensor_tensor(out=x1[0:S, i, 0:H], in0=out_b[i % 2][0:S, :], scalar=tanh_x[0:S, 0:1],
                                               in1=xr[0:S, i % 2, :], op0=ALU.mult, op1=ALU.add).then_inc(x1_done.sem, 1)
                dve.wait_ge(x1_done.sem, x1_done.after(c, i + 1))
                link(nc.vector.bn_stats(norm2.bn[0:S, i, :], x1[0:S, i, 0:H]))

            def low_output(c, i):
                dve.wait_ge(ao_hi_done.sem, ao_hi_done.after(c, i + 1))
                lo_part(ao_lo[:], out_b[i % 2][:, 0:KC * S].rearrange("p (k s) -> p k s", k=KC), ao_hi[:]).then_inc(ao_lo_done.sem, 1)

            def choose(c, part):
                b, n = part.batches, part.count
                dve.wait_ge(ex_ready.sem, ex_ready.after(c, part.number + 1))
                link(nc.vector.tensor_scalar(ex[0:S, b], part.ex, 1.0, None, ALU.add))
                link(nc.vector.reciprocal(sig[0:S, b], ex[0:S, b]))
                link(nc.vector.tensor_reduce(prob[0:S, b], sig[0:S, b], AX.X, ALU.max))
                link(nc.vector.tensor_tensor(cand[0:S, b], sig[0:S, b], prob[0:S, b].unsqueeze(2).to_broadcast([S, n, E]), ALU.is_equal))
                link(nc.vector.tensor_tensor(cand[0:S, b], cand[0:S, b], rev_e[0:S].unsqueeze(1).to_broadcast([S, n, E]), ALU.mult))
                link(nc.vector.tensor_reduce(best[0:S, b], cand[0:S, b], AX.X, ALU.max))
                nc.vector.tensor_tensor(hot[0:S, b], cand[0:S, b], best[0:S, b].unsqueeze(2).to_broadcast([S, n, E]), ALU.is_equal
                                        ).then_inc(hot_done.sem, 1)
                dve.wait_ge(tok_scattered.sem, tok_scattered.after(c, 0))
                link(nc.vector.tensor_scalar(scale[0:S, b], prob[0:S, b].unsqueeze(2).to_broadcast([S, n, XW - H]),
                                             tanh_f[0:S, 0:1], None, ALU.mult))

            def place(c, part):
                b, n = part.batches, part.count
                dve.wait_ge(rank_ready.sem, rank_ready.after(c, part.number + 1))
                link(nc.vector.tensor_tensor(pos[0:S, b], part.rank, next_slot[0:S].unsqueeze(1).to_broadcast([S, n, E]), ALU.add))
                link(nc.vector.tensor_tensor(pos[0:S, b], pos[0:S, b], hot[0:S, b], ALU.mult))
                link(nc.vector.tensor_reduce(slot_f[0:S, b], pos[0:S, b], AX.X, ALU.add))
                link(nc.vector.tensor_copy(slot_i[0:S, b], slot_f[0:S, b]))
                link(nc.vector.tensor_copy(tok_i[0:S, b], tok_f[0:S, b]))
                link(nc.vector.tensor_scalar(tok_f[0:S, b], tok_f[0:S, b], float(CT), None, ALU.add))
                link(nc.vector.tensor_tensor(next_slot[0:S], next_slot[0:S], part.total, ALU.add))
                dve.sem_inc(slots_done.sem, 1)
                dve.sem_inc(rank_used.sem, 1)

            def attend(c, first, last):
                if not last:
                    for i in range(CB):
                        stats(c + 1, i)
                    for part in range(NORM_STEPS):
                        norm_step(norm1, part)
                    dve.sem_inc(ln1_ready.sem, 1)
                if first:
                    for n in range(6, 10):
                        split_weights(n)
                if not first:
                    residual(c - 1, CB - 1)
                for n in range(NT + 4):
                    if n < NT:
                        b = n % DEEP
                        dve.wait_ge(s_ready.sem, s_ready.after(c, n + 1))
                        dve.wait_ge(exp_done.sem, exp_done.after(c, n + 1 - DEEP))
                        nc.vector.tensor_reduce(nmx[0:S, b], score_b[b][0:S, 0:HP * S].rearrange("p (h s) -> p h s", h=HP),
                                                AX.X, ALU.max, negate=True).then_inc(max_done.sem, 1)
                    if 2 <= n < NT + 2:
                        m = n - 2
                        dve.wait_ge(exp_done.sem, exp_done.after(c, m + 1))
                        dve.wait_ge(probs.sem, probs.after(c, m + 1 - DEEP))
                        nc.vector.reciprocal(inv[0:S, m % DEEP], tot[0:S, m % DEEP]).then_inc(inv_done.sem, 1)
                    if 3 <= n < NT + 3:
                        m = n - 3
                        dve.wait_ge(pT_ready.sem, pT_ready.after(c, m + 1))
                        dve.wait_ge(o_ready.sem, o_ready.after(c, (m - KEEP) // HP + 1 if m >= KEEP else 0))
                        nc.vector.tensor_copy(pT[0:S, m % KEEP], turn_b[m % 2][0:S, 0:HP * S].rearrange("p (h s) -> p h s", h=HP)
                                              ).then_inc(pT_copied.sem, 1)
                    if n in (9, 13, 17):
                        low_output(c, n // HP - 2)
                    if n in (12, 16, 19):
                        residual(c, (n - 11) // HP)
                    if n < 4 and not first:
                        for part in range(n * 4, n * 4 + 4):
                            norm_step(norm2, part)
                        if n == 3:
                            dve.sem_inc(ln2_ready.sem, 1)
                    if 4 <= n < 4 + CB and not last:
                        split_token(c + 1, n - 4, token_b[n - 4])
                    if n == 4 + CB and not last:
                        split_context(c + 1)
                    if n == 17 and not first:
                        choose(c - 1, whole)
                low_output(c, CB - 1)
                if not first:
                    place(c - 1, whole)

            def split(u, j, w):
                s = j % 2
                dve.wait_ge(w_hi[w].sem, w_hi[w].after(u, j + 1))
                hi, lo = (gu_hi[:, s, w], gu_lo[:, s, w]) if w < 2 else (dn_hi[:, s], dn_lo[:, s])
                lo_part(lo, raw[:, s, w, :].rearrange("p (k n) -> p k n", k=KC if w < 2 else JC), hi).then_inc(w_lo[w].sem, 1)

            chain.begin(0, 0)
            for i in range(CB):
                stats(0, i)
            for part in range(NORM_STEPS):
                norm_step(norm1, part)
            dve.sem_inc(ln1_ready.sem, 1)
            for n in range(6):
                split_weights(n)
            for i in range(CB):
                split_token(0, i, first_token_b[i])
            split_context(0, first_context_b)
            dve.wait_ge(consts, CONSTS)
            dve.wait_ge(tanh_done, 2)
            dve.wait_ge(x1_cleared, 1)
            attend(0, True, False)
            done = chain.count - PER_CHUNK
            with dve.Fori(0, NCH - 2) as c:
                chain.begin(c + 1, done)
                attend(c + 1, False, False)
                assert chain.count == PER_CHUNK, chain.count
            chain.begin(NCH - 1, done)
            attend(NCH - 1, False, True)
            dve.wait_ge(rows_stored.sem, rows_stored.after(NCH - 1, 0))
            for part in last_parts:
                if part.number:
                    residual(NCH - 1, CB - 1)
                for k in range(NORM_STEPS):
                    norm_step(norm2, k, part.batches)
                for i in range(part.first, part.stop):
                    nc.vector.tensor_scalar(x2[0:S, i, :], x1[0:S, i, 0:H], norm2.rstd[0:S, i:i + 1], norm2.shift[0:S, i:i + 1],
                                            ALU.mult, ALU.add).then_inc(x2_done.sem, 1)
            for part in last_parts:
                choose(NCH - 1, part)
                place(NCH - 1, part)

            link(nc.vector.tensor_tensor(picked[0:MORE], thr[0:MORE], ident[0:MORE, 0:MORE], ALU.mult))
            link(nc.vector.tensor_reduce(u_rank[0:MORE], picked[0:MORE], AX.X, ALU.add))
            link(nc.vector.tensor_copy(unit_row[0:MORE, 1:2], u_rank[0:MORE]))
            link(nc.vector.tensor_tensor(valid[0:MORE], ident[0:MORE, 0:MORE].rearrange("p (e k) -> p e k", e=E),
                                         rev_e[0:MORE].unsqueeze(2).to_broadcast([MORE, E, BLOCKS - 1]), ALU.mult))
            link(nc.vector.tensor_reduce(u_valid[0:MORE], valid[0:MORE].rearrange("p e k -> p (e k)"), AX.X, ALU.add))
            link(nc.vector.tensor_scalar(unit_row[0:MORE, 0:1], u_valid[0:MORE], -1.0, float(E), ALU.mult, ALU.add))
            link(nc.vector.tensor_tensor(valid[0:MORE], next_slot[0:MORE].unsqueeze(2).to_broadcast([MORE, E, BLOCKS - 1]),
                                         thr[0:MORE].rearrange("p (e k) -> p e k", e=E), ALU.is_gt))
            vflat = valid[0:MORE].rearrange("p e k -> p (e k)")
            link(nc.vector.tensor_reduce(u_count[0:MORE], vflat, AX.X, ALU.add))
            link(nc.vector.tensor_copy(more_units[0:MORE], u_count[0:MORE]))
            link(nc.vector.tensor_tensor(picked[0:MORE], vflat, earlier[0:MORE], ALU.mult))
            link(nc.vector.tensor_reduce(u_rank[0:MORE], picked[0:MORE], AX.X, ALU.add))
            link(nc.vector.tensor_tensor(picked[0:MORE], vflat, ident[0:MORE, 0:MORE], ALU.mult))
            link(nc.vector.tensor_reduce(u_valid[0:MORE], picked[0:MORE], AX.X, ALU.add))
            link(nc.vector.tensor_scalar(u_valid[0:MORE], u_valid[0:MORE], -float(OUT_OF_BOUNDS), float(E + OUT_OF_BOUNDS),
                                         ALU.mult, ALU.add))
            link(nc.vector.tensor_tensor(u_rank[0:MORE], u_rank[0:MORE], u_valid[0:MORE], ALU.add))
            nc.vector.tensor_copy(u_slot[0:MORE], u_rank[0:MORE]).then_inc(rows_known, 1)

            def split_tokens(u):
                for t in range(TT):
                    dve.wait_ge(g_hi_done.sem, g_hi_done.after(u, t + 1))
                    lo_part(x_lo[:, :, t * P:(t + 1) * P], xT_b[t][:].rearrange("p (k s) -> p k s", k=KC),
                            x_hi[:, :, t * P:(t + 1) * P]).then_inc(g_lo_done.sem, 1)

            def step(u, j):
                dve.wait_ge(silu_done.sem, silu_done.after(u, j + 1))
                dve.wait_ge(h_hi_done.sem, h_hi_done.after(u, j))
                dve.wait_ge(h_lo_done.sem, h_lo_done.after(u, j))
                nc.vector.tensor_tensor(h_f, silu_g, up_b[j % 2][:].rearrange("p (a n) -> p a n", a=2), ALU.mult
                                        ).then_inc(h_done.sem, 1)
                dve.wait_ge(h_hi_done.sem, h_hi_done.after(u, j + 1))
                lo_part(h_lo[:, j % 2], h_f, h_hi[:, j % 2]).then_inc(h_lo_done.sem, 1)
                split(u, j, 2)

            def finish(u):
                dve.wait_ge(dn_done.sem, dn_done.after(u, NJ))
                dve.wait_ge(x1g_loaded.sem, x1g_loaded.after(u, 16 * TT))
                dve.wait_ge(unit_sent.sem, unit_sent.after(u, 0))
                for t in range(TT):
                    nc.vector.scalar_tensor_tensor(out=rows[:, t, :], in0=y_b[t][:], scalar=x1g[:, t, H:H + 1],
                                                   in1=x1g[:, t, 0:H], op0=ALU.mult, op1=ALU.add).then_inc(rows_done.sem, 1)

            for j in range(2):
                for w in range(2):
                    split(0, j, w)
            split_tokens(0)
            step(0, 0)
            dve.wait_ge(units_loaded, 16)
            more = dve.value_load(more_units[0:1, 0:1], min_val=0, max_val=UNITS_MAX - E)
            with dve.Fori(0, more + (E - 1)) as u:
                for j in range(1, NJ):
                    for w in range(2):
                        split(*((u, j + 1) if j + 1 < NJ else (u + 1, 0)), w)
                    if j == NJ - 1:
                        split_tokens(u + 1)
                    step(u, j)
                for w in range(2):
                    split(u + 1, 1, w)
                step(u + 1, 0)
                finish(u)
            last = more + (E - 1)
            for j in range(1, NJ):
                if j + 1 < NJ:
                    for w in range(2):
                        split(last, j + 1, w)
                step(last, j)
            finish(last)

        @block.tensor
        def _(pe):
            def three(dst, a, b, first, last):
                nc.tensor.matmul(dst, a[0], b[0], start=first, stop=False)
                nc.tensor.matmul(dst, a[0], b[1], start=False, stop=False)
                return nc.tensor.matmul(dst, a[1], b[0], start=False, stop=last)

            for s in (cT_ready, pT_ready, o_ready, y_ready, gu_ready, dn_done):
                pe.sem_inc(s.sem, s.credit)
            pe.wait_ge(consts, CONSTS)

            def turn_weights(n):
                pe.wait_ge(wq_loaded if n < 4 else wkv_loaded if n < 6 else wo_loaded, 16)
                if n >= 6:
                    pe.wait_ge(x_lo_done.sem, x_lo_done.after(0, n - 5))
                for o in range(4):
                    src = (wq_raw[:, o, n * P:(n + 1) * P] if n < 4 else wkv_raw[:, (n - 4) * 4 + o, :] if n < 6 else
                           wo_raw[:, o, (n - 6) * P:(n - 5) * P])
                    ins = nc.tensor.transpose(weight_b[n][:, o * P:(o + 1) * P], src, ident[:])
                ins.then_inc(w_turned, 1)

            def turn_chunk(c, i, bank, first):
                pe.wait_ge(xn_done.sem, xn_done.after(c, i + 1))
                if first:
                    if i >= 2:
                        pe.wait_ge(w_lo_done, 3 + i)
                elif i == 0:
                    pe.wait_ge(rank_used.sem, rank_used.after(c - 2, 0))
                elif i == 1:
                    pe.wait_ge(x1_done.sem, x1_done.after(c - 1, 0))
                else:
                    pe.wait_ge(x_lo_done.sem, x_lo_done.after(c, i - 1))
                for k in range(KC):
                    ins = nc.tensor.transpose(bank[:, k * S:(k + 1) * S], xn[0:S, i, k * P:(k + 1) * P], ident[0:S, 0:S])
                ins.then_inc(xT_ready.sem, 1)

            def turn_context(c, bank=misc_b):
                pe.wait_ge(ctx_loaded.sem, ctx_loaded.after(c, 16))
                if bank is misc_b:
                    pe.wait_ge(x_lo_done.sem, x_lo_done.after(c, CB))
                else:
                    pe.wait_ge(w_lo_done, KC)
                for i in range(CB):
                    ins = nc.tensor.transpose(bank[:, i * S:(i + 1) * S], ctx_t[0:S, i, :], ident[0:S, 0:S])
                ins.then_inc(cT_ready.sem, 1)

            def keys_or_queries(c, t):
                m, bank = t // 2, score_b[(NT + t) % DEEP][:, 0:CT]
                if t < DEEP:
                    pe.wait_ge(exp_done.sem, exp_done.after(c - 1, NT + t - DEEP + 1))
                else:
                    pe.wait_ge(kq_done.sem, kq_done.after(c, t - DEEP + 1))
                r = slice(m * P, (m + 1) * P)
                if t % 2 == 0:
                    pe.wait_ge(c_lo_done.sem, c_lo_done.after(c, 1))
                    ins = three(bank, (wkv_hi[:, r], wkv_lo[:, r]), (c_hi[:], c_lo[:]), True, True)
                else:
                    pe.wait_ge(x_lo_done.sem, x_lo_done.after(c, CB))
                    for k in range(KC):
                        ins = three(bank, (wq_hi[:, k, r], wq_lo[:, k, r]), (x_hi[:, k, :], x_lo[:, k, :]), k == 0, k == KC - 1)
                ins.then_inc(kq_ready.sem, 1)

            def values(c, i):
                if i < 2:
                    pe.wait_ge(pT_copied.sem, pT_copied.after(c, 0))
                else:
                    pe.wait_ge(v_done.sem, v_done.after(c, i - 1))
                r = slice(i * S, (i + 1) * S)
                three(turn_b[i % 2][0:S, :], (c_hi[:, r], c_lo[:, r]), (wkv_hi[:, H:2 * H], wkv_lo[:, H:2 * H]),
                      True, True).then_inc(v_ready.sem, 1)

            def scores(c, n):
                i, m, b = n // KC, n % KC, n % DEEP
                if n == 0:
                    pe.wait_ge(kq_done.sem, kq_done.after(c, 2 * KC))
                if n >= DEEP:
                    pe.wait_ge(exp_done.sem, exp_done.after(c, n - DEEP + 1))
                nc.tensor.matmul(score_b[b][0:S, 0:HP * S], eye[0:S, 0:S], mask[0:S].unsqueeze(1).to_broadcast([S, HP, S]),
                                 start=True, stop=False)
                nc.tensor.matmul(score_b[b][0:S, 0:HP * S], qT[:, m, i * S:(i + 1) * S],
                                 keys_b[:, m, i].rearrange("p j s -> p (j s)"), start=False, stop=True).then_inc(s_ready.sem, 1)

            def turn_probs(c, n):
                pe.wait_ge(probs.sem, probs.after(c, n + 1))
                if n < 2:
                    pe.wait_ge(v_done.sem, v_done.after(c, CB - 1 + n))
                else:
                    pe.wait_ge(pT_copied.sem, pT_copied.after(c, n - 1))
                for h in range(HP):
                    ins = nc.tensor.transpose(turn_b[n % 2][0:S, h * S:(h + 1) * S], pn[0:S, n % DEEP, h, :], ident[0:S, 0:S])
                ins.then_inc(pT_ready.sem, 1)

            def weigh(c, i):
                pe.wait_ge(pT_copied.sem, pT_copied.after(c, HP * (i + 1)))
                pe.wait_ge(x1_done.sem, x1_done.after(c, i - 1))
                for m in range(KC):
                    for j in range(HP):
                        ins = nc.tensor.matmul(out_b[i % 2][j * HD:(j + 1) * HD, m * S:(m + 1) * S], v[0:S, i, m * HP + j, :],
                                               pT[0:S, (i * KC + m) % KEEP, j, :], start=True, stop=True,
                                               tile_position=(0, j * HD))
                ins.then_inc(o_ready.sem, 1)

            def project(c, i):
                pe.wait_ge(ao_lo_done.sem, ao_lo_done.after(c, i + 1))
                for k in range(KC):
                    ins = three(out_b[i % 2][0:S, :], (ao_hi[:, k, :], ao_lo[:, k, :]), (wo_hi[:, k, :], wo_lo[:, k, :]),
                                k == 0, k == KC - 1)
                ins.then_inc(y_ready.sem, 1)

            def turn_normed(c, i, last, bank=misc_b):
                pe.wait_ge(x2_done.sem, x2_done.after(c, i + 1))
                if bank is misc_b:
                    if i:
                        pe.wait_ge(x2T_copied.sem, x2T_copied.after(c, i))
                    elif last:
                        pe.wait_ge(rank_used.sem, rank_used.after(c, 0))
                    else:
                        pe.wait_ge(c_lo_done.sem, c_lo_done.after(c + 2, 1))
                for k in range(KC):
                    ins = nc.tensor.transpose(bank[:, k * S:(k + 1) * S], x2[0:S, i, k * P:(k + 1) * P], ident[0:S, 0:S])
                ins.then_inc(x2T_ready.sem, 1)

            def route(c, part, first, stop):
                pe.wait_ge(x2T_copied.sem, x2T_copied.after(c, stop))
                for k in range(KC):
                    ins = nc.tensor.matmul(part.logits[:, (first - part.first) * S:(stop - part.first) * S], router[:, k, :],
                                           x2T[:, k, first * S:stop * S], start=k == 0, stop=k == KC - 1)
                if stop == part.stop:
                    ins.then_inc(logits_ready.sem, 1)

            def turn_logits(c, part):
                pe.wait_ge(ex_t_done.sem, ex_t_done.after(c, part.number + 1))
                pe.sem_inc(pe_wait_passed, 1)
                for i in range(part.first, part.stop):
                    ins = nc.tensor.transpose(part.ex_b[i], ex_t[:, i * S:(i + 1) * S], ident[0:E, 0:E])
                ins.then_inc(ex_ready.sem, 1)

            def rank(c, part):
                pe.wait_ge(hot_done.sem, hot_done.after(c, part.number + 1))
                nc.tensor.matmul(part.rank_from[part.first], before[0:S, :], hot[0:S, part.batches].rearrange("p i e -> p (i e)"),
                                 start=True, stop=False, skip_group_check=True)
                for i in range(part.first, part.stop - 1):
                    nc.tensor.matmul(part.rank_from[i + 1], ones[0:S, :],
                                     hot[0:S, i:i + 1, :].to_broadcast([S, part.stop - 1 - i, E]), start=False, stop=False,
                                     skip_group_check=True)
                for i in range(part.first, part.stop):
                    ins = nc.tensor.matmul(part.total, ones[0:S, :], hot[0:S, i, :], start=False,
                                           stop=i == part.stop - 1, skip_group_check=True)
                ins.then_inc(rank_ready.sem, 1)

            def attend(c, first, last):
                for n in range(DEEP):
                    scores(c, n)
                    if n:
                        values(c, n)
                for n in range(NT + 4):
                    if n + DEEP < NT:
                        scores(c, n + DEEP)
                    if n == 0:
                        values(c, CB - 1)
                    if 1 <= n < 1 + CB and not last:
                        turn_chunk(c + 1, n - 1, token_b[n - 1], False)
                    if n == 1 + CB and not last:
                        turn_context(c + 1)
                    if 7 <= n < 7 + CB and not first:
                        turn_normed(c - 1, n - 7, last)
                    if n < NT:
                        turn_probs(c, n)
                    if n >= 5 and n % HP == 1:
                        weigh(c, n // HP - 1)
                    if n in (8, 12, 16, 18):
                        project(c, n // HP - 2 if n < NT + 2 else CB - 1)
                    if n == 11 and not first:
                        route(c - 1, whole, 0, CB)
                    if n == 13 and not first:
                        turn_logits(c - 1, whole)
                    if n == 17 and not first:
                        rank(c - 1, whole)
                    if n >= 13 and not last:
                        for t in range(n - 13, n - 12) if n < NT + 3 else range(6, 2 * KC):
                            keys_or_queries(c + 1, t)
                if not last:
                    values(c + 1, 0)

            for n in range(6):
                turn_weights(n)
            for i in range(CB):
                turn_chunk(0, i, first_token_b[i], True)
            turn_context(0, first_context_b)
            pe.wait_ge(small_loaded, 48)
            for t in range(2 * KC):
                keys_or_queries(0, t)
                if t == 3:
                    for n in range(6, 10):
                        turn_weights(n)
            pe.wait_ge(w_lo_done, 10)
            values(0, 0)
            attend(0, True, False)
            with pe.Fori(0, NCH - 2) as c:
                attend(c + 1, False, False)
            attend(NCH - 1, False, True)
            pe.wait_ge(rank_used.sem, rank_used.after(NCH - 1, 0))
            for part in last_parts:
                for i in range(part.first, part.stop):
                    turn_normed(NCH - 1, i, True, last_row_b[i])
                    if i > part.first:
                        route(NCH - 1, part, i - 1, i)
                route(NCH - 1, part, part.stop - 1, part.stop)
                if part.number:
                    rank(NCH - 1, last_parts[0])
                turn_logits(NCH - 1, part)
            rank(NCH - 1, last_parts[1])

            def turn_tokens(u):
                pe.wait_ge(xg_loaded.sem, xg_loaded.after(u, 16 * TT))
                pe.wait_ge(g_lo_done.sem, g_lo_done.after(u, 0))
                for t in range(TT):
                    for k in range(KC):
                        ins = nc.tensor.transpose(xT_b[t][:, k * P:(k + 1) * P], xg[:, t, k * P:(k + 1) * P], ident[:])
                    ins.then_inc(gT_ready.sem, 1)

            def gate_up(u, j):
                s = j % 2
                if j == 0:
                    pe.wait_ge(g_lo_done.sem, g_lo_done.after(u, TT))
                for w, bank in ((0, gate_b[s]), (1, up_b[s])):
                    pe.wait_ge(w_lo[w].sem, w_lo[w].after(u, j + 1))
                    if w == 0:
                        pe.wait_ge(silu_done.sem, silu_done.after(u, j - 1))
                    else:
                        pe.wait_ge(h_done.sem, h_done.after(u, j - 1))
                    for m in range(JC):
                        for k in range(KC):
                            r = slice(m * P, (m + 1) * P)
                            ins = three(bank[:, m * CAP:(m + 1) * CAP], (gu_hi[:, s, w, k, r], gu_lo[:, s, w, k, r]),
                                        (x_hi[:, k, 0:CAP], x_lo[:, k, 0:CAP]), k == 0, k == KC - 1)
                ins.then_inc(gu_ready.sem, 1)

            def down(u, j):
                s = j % 2
                pe.wait_ge(w_lo[2].sem, w_lo[2].after(u, j + 1))
                pe.wait_ge(h_lo_done.sem, h_lo_done.after(u, j + 1))
                if j == 0:
                    pe.wait_ge(rows_done.sem, rows_done.after(u, 0))
                for t in range(TT):
                    for k in range(JC):
                        r = slice(t * P, (t + 1) * P)
                        ins = three(y_b[t][:], (h_hi[:, s, k, r], h_lo[:, s, k, r]), (dn_hi[:, s, k, :], dn_lo[:, s, k, :]),
                                    j == 0 and k == 0, j == NJ - 1 and k == JC - 1)
                ins.then_inc(dn_done.sem, 1)

            turn_tokens(0)
            gate_up(0, 0)
            pe.wait_ge(units_loaded, 16)
            more = pe.value_load(more_units[0:1, 0:1], min_val=0, max_val=UNITS_MAX - E)
            with pe.Fori(0, more + (E - 1)) as u:
                gate_up(u, 1)
                down(u, 0)
                gate_up(u, 2)
                down(u, 1)
                turn_tokens(u + 1)
                gate_up(u, 3)
                down(u, 2)
                gate_up(u + 1, 0)
                down(u, 3)
            last = more + (E - 1)
            gate_up(last, 1)
            down(last, 0)
            gate_up(last, 2)
            down(last, 1)
            gate_up(last, 3)
            down(last, 2)
            down(last, 3)


_INS = ["x", "ctx_512", "g_xattn", "g_ffn", "L0_xattn_Wq", "L0_xattn_Wkv_expand", "L0_xattn_Wout", "L0_ffn_router_w",
        "L0_ffn_gate_w", "L0_ffn_up_w", "L0_ffn_down_w"]


def kernel(**inputs):
    import numpy as np
    import concourse.bacc as bacc
    from concourse.bass_utils import run_bass_kernel_spmd

    nc = bacc.Bacc("TRN2", target_bir_lowering=False, num_devices=1)
    arrays, args = {}, []
    for name in _INS:
        a = np.ascontiguousarray(inputs[name])
        arrays[f"in_{name}"] = a
        args.append(nc.dram_tensor(f"in_{name}", a.shape, mybir.dt.from_np(a.dtype), kind="ExternalInput").ap())
    out = nc.dram_tensor("out_x", inputs["x"].shape, F32, kind="ExternalOutput").ap()
    flamingo_block(nc, *args, out)
    r = run_bass_kernel_spmd(nc, [arrays], core_ids=[0])
    return r.results[0]["out_x"]
```
